# Optimizing a Trainium2 kernel written in Bass

```python
import numpy as np
import jax
import jax.numpy as jnp

def _softmax(x, axis=-1):
    return jax.nn.softmax(x, axis=axis)

def _gelu(x):
    return jax.nn.gelu(x, approximate=True)

def _silu(x):
    return jax.nn.silu(x)

def _sigmoid(x):
    return jax.nn.sigmoid(x)

def _layernorm(x, axis=-1, eps=1e-05):
    m = jnp.mean(x, axis=axis, keepdims=True)
    v = jnp.var(x, axis=axis, keepdims=True)
    return (x - m) / jnp.sqrt(v + eps)

def _scatter_add(tgt, idx, src, axis=0):
    return tgt.at[idx].add(src)

def _segment_sum(src, seg, n):
    return jax.ops.segment_sum(src, seg, n)
kernel_name = 'mk_seq_preln_d2_jaxref_r8_0fda52'

def setup_inputs(seed: int=0):
    np.random.seed(seed)
    _w = jnp.asarray

    def _L0_attn_setup():
        import jax, jax.numpy as jnp
        import numpy as np
        EPS = 1e-06
        N_HEADS, N_KV_HEADS = (16, 4)
        HYBRID_RATIO = 0.5
        ROPE_BASE = 10000.0

        def rms(x, w):
            return x * jax.lax.rsqrt(jnp.mean(x * x, axis=-1, keepdims=True) + EPS) * w

        def rotate_half(x):
            x1, x2 = jnp.split(x, 2, axis=-1)
            return jnp.concatenate((-x2, x1), axis=-1)
        key = jax.random.key(seed)
        ks = jax.random.split(key, 20)
        B, L, D = (2, 128, 128)
        N = 128
        R = 64
        hd = D // N_HEADS
        F = 4 * D
        rn = lambda k, s, sc=0.02: jax.random.normal(k, s, jnp.float32) * sc
        return {'x': jax.random.normal(ks[0], (B, L, D), jnp.float32), 'norm_attn_w': jnp.ones((D,), jnp.float32), 'Wq': rn(ks[1], (D, D)), 'Wk': rn(ks[2], (D, N_KV_HEADS * hd)), 'Wv': rn(ks[3], (D, N_KV_HEADS * hd)), 'Wo': rn(ks[4], (D, D)), 'qn_w': jnp.ones((hd,), jnp.float32), 'kn_w': jnp.ones((hd,), jnp.float32), 'ssm_norm_w': jnp.ones((D,), jnp.float32), 'Wx': rn(ks[5], (D, R + 2 * N)), 'Wdt': rn(ks[6], (R, D)), 'bdt': jnp.zeros((D,), jnp.float32), 'A_log': rn(ks[7], (D, N), 0.1), 'Dp': jnp.ones((D,), jnp.float32), 'Wsel': rn(ks[8], (D, D)), 'bsel': jnp.zeros((D,), jnp.float32), 'sel_gate': jnp.ones((D,), jnp.float32), 'Wimp': rn(ks[9], (D, N)), 'bimp': jnp.zeros((N,), jnp.float32), 'Wg': rn(ks[10], (D, D)), 'bg': jnp.zeros((D,), jnp.float32), 'Wout': rn(ks[11], (D, D)), 'norm_ffn_w': jnp.ones((D,), jnp.float32), 'W1': rn(ks[12], (D, 2 * F)), 'W2': rn(ks[13], (F, D))}
    _L0_attn_in = _L0_attn_setup()

    def _L0_ffn_setup():
        import jax, jax.numpy as jnp
        import numpy as np
        SL, BS, HS, FF, E, TOPK = (256, 2, 128, 512, 8, 2)
        key = jax.random.key(seed)
        ks = jax.random.split(key, 6)
        T = SL * BS
        x = jax.random.normal(ks[0], (SL, BS, HS), jnp.float32)
        scores = jax.random.uniform(ks[1], (T, E), jnp.float32)
        expert_weights = jax.random.uniform(ks[2], (T, TOPK), jnp.float32)
        expert_indices = jax.random.randint(ks[3], (T, TOPK), 0, E, jnp.int32)
        w1 = jax.random.normal(ks[4], (E, HS, FF), jnp.float32) * (1.0 / np.sqrt(HS))
        w2 = jax.random.normal(ks[5], (E, FF, HS), jnp.float32) * (1.0 / np.sqrt(FF))
        bias = jnp.zeros((HS,), jnp.float32)
        return dict(x=x, scores=scores, expert_weights=expert_weights, expert_indices=expert_indices, w1=w1, w2=w2, bias=bias)
    _L0_ffn_in = _L0_ffn_setup()

    def _L1_attn_setup():
        import math
        import jax, jax.numpy as jnp
        import numpy as np
        N_HEAD = 16

        def _reference_tuple_inner(x, W_dq, W_uq, W_dkv, W_uk, W_uv, W_o):
            B, T, C = x.shape
            nh = N_HEAD
            hs = C // nh
            kvl = W_dkv.shape[0]
            k_eff = (W_dq.T @ W_uq.T @ W_uk).reshape(nh, hs, kvl)
            v_eff = (W_uv.T @ W_o.T).reshape(kvl, nh, hs).transpose(1, 0, 2)
            c_kv = x @ W_dkv.T
            q = (x @ W_dq.T @ W_uq.T).reshape(B, T, nh, hs).transpose(0, 2, 1, 3)
            q_lat = jnp.einsum('bhtd,hdl->bhtl', q, k_eff)
            attn = jnp.einsum('bhtl,bsl->bhts', q_lat, c_kv) / math.sqrt(hs)
            causal_mask = jnp.triu(jnp.ones((T, T), bool), k=1)
            attn = jnp.where(causal_mask[None, None], -jnp.inf, attn)
            attn = jax.nn.softmax(attn, axis=-1)
            ctx = jnp.einsum('bhts,bsl->bhtl', attn, c_kv)
            y = jnp.einsum('bhtl,hld->bhtd', ctx, v_eff).transpose(0, 2, 1, 3).reshape(B, T, C)
            return (y, c_kv)
        key = jax.random.key(seed)
        ks = jax.random.split(key, 7)
        B, T, C = (4, 256, 128)
        QL, KVL = (32, 32)
        s = 0.02
        return {'x': jax.random.normal(ks[0], (B, T, C), jnp.float32), 'W_dq': jax.random.normal(ks[1], (QL, C), jnp.float32) * s, 'W_uq': jax.random.normal(ks[2], (C, QL), jnp.float32) * s, 'W_dkv': jax.random.normal(ks[3], (KVL, C), jnp.float32) * s, 'W_uk': jax.random.normal(ks[4], (C, KVL), jnp.float32) * s, 'W_uv': jax.random.normal(ks[5], (C, KVL), jnp.float32) * s, 'W_o': jax.random.normal(ks[6], (C, C), jnp.float32) * s}
    _L1_attn_in = _L1_attn_setup()

    def _L1_ffn_setup():
        import jax, jax.numpy as jnp
        import numpy as np
        D = 128
        E = 8
        K = 2
        NUM_ITER = 2
        DT = 0.1
        H = 64
        CTX = 2 * D

        def _gelu(t):
            return jax.nn.gelu(t, approximate=False)

        def _inl(ctrl, x, v, mu):
            alpha_raw, beta_raw, gate_raw = jnp.split(ctrl, 3, axis=-1)
            alpha = jax.nn.sigmoid(alpha_raw)
            beta = jax.nn.softplus(beta_raw)
            gate = jax.nn.sigmoid(gate_raw)
            error = x - mu
            v_next = alpha * v - beta * error
            x_next = x + DT * gate * v_next
            return (x_next, v_next)
        key = jax.random.key(seed)
        ks = jax.random.split(key, 20)
        s = 0.02
        inp = {'x': jax.random.normal(ks[0], (4, 512, D), jnp.float32), 'w_r1': jax.random.normal(ks[1], (D, D // 4), jnp.float32) * s, 'b_r1': jnp.zeros((D // 4,), jnp.float32), 'w_r2': jax.random.normal(ks[2], (D // 4, E), jnp.float32) * s, 'b_r2': jnp.zeros((E,), jnp.float32), 'w_h1': jax.random.normal(ks[3], (D, D // 4), jnp.float32) * s, 'b_h1': jnp.zeros((D // 4,), jnp.float32), 'w_h2': jax.random.normal(ks[4], (D // 4, 1), jnp.float32) * s, 'b_h2': jnp.zeros((1,), jnp.float32), 'expert_w1': jax.random.normal(ks[5], (E, CTX, H), jnp.float32) * s, 'expert_b1': jnp.zeros((E, H), jnp.float32), 'expert_w2': jax.random.normal(ks[6], (E, H, 3 * D), jnp.float32) * s, 'expert_b2': jnp.zeros((E, 3 * D), jnp.float32), 'w_s1': jax.random.normal(ks[7], (CTX, H), jnp.float32) * s, 'b_s1': jnp.zeros((H,), jnp.float32), 'w_s2': jax.random.normal(ks[8], (H, 3 * D), jnp.float32) * s, 'b_s2': jnp.zeros((3 * D,), jnp.float32), 'shared_weight': jnp.asarray(0.5, jnp.float32), 'w_f1': jax.random.normal(ks[9], (D, 2 * D), jnp.float32) * s, 'b_f1': jnp.zeros((2 * D,), jnp.float32), 'w_f2': jax.random.normal(ks[10], (2 * D, D), jnp.float32) * s, 'b_f2': jnp.zeros((D,), jnp.float32), 'integration_weight': jnp.full((D,), 0.5, jnp.float32), 'mu': jnp.zeros((D,), jnp.float32)}
        return inp
    _L1_ffn_in = _L1_ffn_setup()
    _d = {'L0_attn_x': _L0_attn_in['x'], 'L0_attn_norm_attn_w': _L0_attn_in['norm_attn_w'], 'L0_attn_Wq': _L0_attn_in['Wq'], 'L0_attn_Wk': _L0_attn_in['Wk'], 'L0_attn_Wv': _L0_attn_in['Wv'], 'L0_attn_Wo': _L0_attn_in['Wo'], 'L0_attn_qn_w': _L0_attn_in['qn_w'], 'L0_attn_kn_w': _L0_attn_in['kn_w'], 'L0_attn_ssm_norm_w': _L0_attn_in['ssm_norm_w'], 'L0_attn_Wx': _L0_attn_in['Wx'], 'L0_attn_Wdt': _L0_attn_in['Wdt'], 'L0_attn_bdt': _L0_attn_in['bdt'], 'L0_attn_A_log': _L0_attn_in['A_log'], 'L0_attn_Dp': _L0_attn_in['Dp'], 'L0_attn_Wsel': _L0_attn_in['Wsel'], 'L0_attn_bsel': _L0_attn_in['bsel'], 'L0_attn_sel_gate': _L0_attn_in['sel_gate'], 'L0_attn_Wimp': _L0_attn_in['Wimp'], 'L0_attn_bimp': _L0_attn_in['bimp'], 'L0_attn_Wg': _L0_attn_in['Wg'], 'L0_attn_bg': _L0_attn_in['bg'], 'L0_attn_Wout': _L0_attn_in['Wout'], 'L0_attn_norm_ffn_w': _L0_attn_in['norm_ffn_w'], 'L0_attn_W1': _L0_attn_in['W1'], 'L0_attn_W2': _L0_attn_in['W2'], 'L0_ffn_scores': _L0_ffn_in['scores'], 'L0_ffn_expert_weights': _L0_ffn_in['expert_weights'], 'L0_ffn_expert_indices': _L0_ffn_in['expert_indices'], 'L0_ffn_w1': _L0_ffn_in['w1'], 'L0_ffn_w2': _L0_ffn_in['w2'], 'L0_ffn_bias': _L0_ffn_in['bias'], 'L1_attn_W_dq': _L1_attn_in['W_dq'], 'L1_attn_W_uq': _L1_attn_in['W_uq'], 'L1_attn_W_dkv': _L1_attn_in['W_dkv'], 'L1_attn_W_uk': _L1_attn_in['W_uk'], 'L1_attn_W_uv': _L1_attn_in['W_uv'], 'L1_attn_W_o': _L1_attn_in['W_o'], 'L1_ffn_w_r1': _L1_ffn_in['w_r1'], 'L1_ffn_b_r1': _L1_ffn_in['b_r1'], 'L1_ffn_w_r2': _L1_ffn_in['w_r2'], 'L1_ffn_b_r2': _L1_ffn_in['b_r2'], 'L1_ffn_w_h1': _L1_ffn_in['w_h1'], 'L1_ffn_b_h1': _L1_ffn_in['b_h1'], 'L1_ffn_w_h2': _L1_ffn_in['w_h2'], 'L1_ffn_b_h2': _L1_ffn_in['b_h2'], 'L1_ffn_expert_w1': _L1_ffn_in['expert_w1'], 'L1_ffn_expert_b1': _L1_ffn_in['expert_b1'], 'L1_ffn_expert_w2': _L1_ffn_in['expert_w2'], 'L1_ffn_expert_b2': _L1_ffn_in['expert_b2'], 'L1_ffn_w_s1': _L1_ffn_in['w_s1'], 'L1_ffn_b_s1': _L1_ffn_in['b_s1'], 'L1_ffn_w_s2': _L1_ffn_in['w_s2'], 'L1_ffn_b_s2': _L1_ffn_in['b_s2'], 'L1_ffn_shared_weight': _L1_ffn_in['shared_weight'], 'L1_ffn_w_f1': _L1_ffn_in['w_f1'], 'L1_ffn_b_f1': _L1_ffn_in['b_f1'], 'L1_ffn_w_f2': _L1_ffn_in['w_f2'], 'L1_ffn_b_f2': _L1_ffn_in['b_f2'], 'L1_ffn_integration_weight': _L1_ffn_in['integration_weight'], 'L1_ffn_mu': _L1_ffn_in['mu']}
    _x0 = _d['L0_attn_x']
    _d['L0_attn_x'] = jax.random.normal(jax.random.fold_in(jax.random.key(seed), 1), (2, 1024, 128), dtype=_x0.dtype)
    del _x0
    return _d

def reference(L0_attn_x, L0_attn_norm_attn_w, L0_attn_Wq, L0_attn_Wk, L0_attn_Wv, L0_attn_Wo, L0_attn_qn_w, L0_attn_kn_w, L0_attn_ssm_norm_w, L0_attn_Wx, L0_attn_Wdt, L0_attn_bdt, L0_attn_A_log, L0_attn_Dp, L0_attn_Wsel, L0_attn_bsel, L0_attn_sel_gate, L0_attn_Wimp, L0_attn_bimp, L0_attn_Wg, L0_attn_bg, L0_attn_Wout, L0_attn_norm_ffn_w, L0_attn_W1, L0_attn_W2, L0_ffn_scores, L0_ffn_expert_weights, L0_ffn_expert_indices, L0_ffn_w1, L0_ffn_w2, L0_ffn_bias, L1_attn_W_dq, L1_attn_W_uq, L1_attn_W_dkv, L1_attn_W_uk, L1_attn_W_uv, L1_attn_W_o, L1_ffn_w_r1, L1_ffn_b_r1, L1_ffn_w_r2, L1_ffn_b_r2, L1_ffn_w_h1, L1_ffn_b_h1, L1_ffn_w_h2, L1_ffn_b_h2, L1_ffn_expert_w1, L1_ffn_expert_b1, L1_ffn_expert_w2, L1_ffn_expert_b2, L1_ffn_w_s1, L1_ffn_b_s1, L1_ffn_w_s2, L1_ffn_b_s2, L1_ffn_shared_weight, L1_ffn_w_f1, L1_ffn_b_f1, L1_ffn_w_f2, L1_ffn_b_f2, L1_ffn_integration_weight, L1_ffn_mu):

    def _L0_attn_ref(x, norm_attn_w, Wq, Wk, Wv, Wo, qn_w, kn_w, ssm_norm_w, Wx, Wdt, bdt, A_log, Dp, Wsel, bsel, sel_gate, Wimp, bimp, Wg, bg, Wout, norm_ffn_w, W1, W2):
        import jax, jax.numpy as jnp
        import numpy as np
        EPS = 1e-06
        N_HEADS, N_KV_HEADS = (16, 4)
        HYBRID_RATIO = 0.5
        ROPE_BASE = 10000.0

        def rms(x, w):
            return x * jax.lax.rsqrt(jnp.mean(x * x, axis=-1, keepdims=True) + EPS) * w

        def rotate_half(x):
            x1, x2 = jnp.split(x, 2, axis=-1)
            return jnp.concatenate((-x2, x1), axis=-1)
        B, L, D = x.shape
        H, KVH = (N_HEADS, N_KV_HEADS)
        hd = D // H
        R = Wdt.shape[0]
        N = A_log.shape[1]
        xa = rms(x, norm_attn_w)
        q = (xa @ Wq).reshape(B, L, H, hd).transpose(0, 2, 1, 3)
        k = (xa @ Wk).reshape(B, L, KVH, hd).transpose(0, 2, 1, 3)
        v = (xa @ Wv).reshape(B, L, KVH, hd).transpose(0, 2, 1, 3)
        q = rms(q, qn_w)
        k = rms(k, kn_w)
        inv_freq = 1.0 / ROPE_BASE ** (jnp.arange(0, hd, 2, dtype=jnp.float32) / hd)
        freqs = jnp.arange(L, dtype=jnp.float32)[:, None] * inv_freq[None, :]
        emb = jnp.concatenate((freqs, freqs), axis=-1)
        cos, sin = (jnp.cos(emb), jnp.sin(emb))
        q = q * cos + rotate_half(q) * sin
        k = k * cos + rotate_half(k) * sin
        n_rep = H // KVH
        k = jnp.repeat(k, n_rep, axis=1)
        v = jnp.repeat(v, n_rep, axis=1)
        scores = jnp.einsum('bhqd,bhkd->bhqk', q, k) / jnp.sqrt(jnp.float32(hd))
        attn = jax.nn.softmax(scores, axis=-1)
        attn = jnp.einsum('bhqk,bhkd->bhqd', attn, v)
        attn_out = attn.transpose(0, 2, 1, 3).reshape(B, L, D) @ Wo
        xn = rms(x, ssm_norm_w)
        xp = xn @ Wx
        dr, Bs, Cs = (xp[..., :R], xp[..., R:R + N], xp[..., R + N:])
        sel = jax.nn.sigmoid((xn @ Wsel + bsel) * sel_gate)
        xn = xn * sel
        imp = jax.nn.sigmoid(xn @ Wimp + bimp)
        delta = jax.nn.softplus(dr @ Wdt + bdt)
        A = -jnp.exp(A_log)
        gate = jax.nn.sigmoid(xn @ Wg + bg)
        xn = xn * gate
        Bs = Bs * imp
        Cs = Cs * imp

        def step(h, inputs):
            dt, bt, ct, xt = inputs
            dA = jnp.exp(dt[:, :, None] * A)
            h = dA * h + dt[:, :, None] * bt[:, None, :] * xt[:, :, None]
            y = jnp.sum(h * ct[:, None, :], axis=-1)
            return (h, y)
        h0 = jnp.zeros((B, D, N), x.dtype)
        seq = (delta.transpose(1, 0, 2), Bs.transpose(1, 0, 2), Cs.transpose(1, 0, 2), xn.transpose(1, 0, 2))
        _, ys = jax.lax.scan(step, h0, seq)
        y = ys.transpose(1, 0, 2)
        ssm_out = (y + x * Dp) @ Wout
        x1 = x + HYBRID_RATIO * attn_out + (1.0 - HYBRID_RATIO) * ssm_out
        xf = rms(x1, norm_ffn_w)
        u = xf @ W1
        a, g = jnp.split(u, 2, axis=-1)
        ff = jax.nn.silu(a) * g @ W2
        return x1 + ff

    def _L0_ffn_ref(x, scores, expert_weights, expert_indices, w1, w2, bias):
        import jax, jax.numpy as jnp
        import numpy as np
        SL, BS, HS, FF, E, TOPK = (256, 2, 128, 512, 8, 2)
        sl, bs, hs = x.shape
        n_exp = w1.shape[0]
        top_k = expert_indices.shape[-1]
        xf = x.reshape(-1, hs)
        flat_idx = expert_indices.reshape(-1)
        flat_w = expert_weights.reshape(-1)
        order = jnp.argsort(flat_idx)
        tok = order // top_k
        tokens_per_expert = jnp.bincount(flat_idx, length=n_exp).astype(jnp.int32)
        xs = xf[tok]
        h = jax.nn.gelu(jax.lax.ragged_dot(xs, w1, tokens_per_expert), approximate=False)
        ys = jax.lax.ragged_dot(h, w2, tokens_per_expert)
        ys = ys * flat_w[order][:, None]
        out = jnp.zeros_like(xf).at[tok].add(ys)
        return out.reshape(sl, bs, hs) + bias

    def _L1_attn_ref(x, W_dq, W_uq, W_dkv, W_uk, W_uv, W_o):
        import math
        import jax, jax.numpy as jnp
        import numpy as np
        N_HEAD = 16

        def _reference_tuple_inner(x, W_dq, W_uq, W_dkv, W_uk, W_uv, W_o):
            B, T, C = x.shape
            nh = N_HEAD
            hs = C // nh
            kvl = W_dkv.shape[0]
            k_eff = (W_dq.T @ W_uq.T @ W_uk).reshape(nh, hs, kvl)
            v_eff = (W_uv.T @ W_o.T).reshape(kvl, nh, hs).transpose(1, 0, 2)
            c_kv = x @ W_dkv.T
            q = (x @ W_dq.T @ W_uq.T).reshape(B, T, nh, hs).transpose(0, 2, 1, 3)
            q_lat = jnp.einsum('bhtd,hdl->bhtl', q, k_eff)
            attn = jnp.einsum('bhtl,bsl->bhts', q_lat, c_kv) / math.sqrt(hs)
            causal_mask = jnp.triu(jnp.ones((T, T), bool), k=1)
            attn = jnp.where(causal_mask[None, None], -jnp.inf, attn)
            attn = jax.nn.softmax(attn, axis=-1)
            ctx = jnp.einsum('bhts,bsl->bhtl', attn, c_kv)
            y = jnp.einsum('bhtl,hld->bhtd', ctx, v_eff).transpose(0, 2, 1, 3).reshape(B, T, C)
            return (y, c_kv)
        return _reference_tuple_inner(x, W_dq, W_uq, W_dkv, W_uk, W_uv, W_o)[0]

    def _L1_ffn_ref(x, w_r1, b_r1, w_r2, b_r2, w_h1, b_h1, w_h2, b_h2, expert_w1, expert_b1, expert_w2, expert_b2, w_s1, b_s1, w_s2, b_s2, shared_weight, w_f1, b_f1, w_f2, b_f2, integration_weight, mu):
        import jax, jax.numpy as jnp
        import numpy as np
        D = 128
        E = 8
        K = 2
        NUM_ITER = 2
        DT = 0.1
        H = 64
        CTX = 2 * D

        def _gelu(t):
            return jax.nn.gelu(t, approximate=False)

        def _inl(ctrl, x, v, mu):
            alpha_raw, beta_raw, gate_raw = jnp.split(ctrl, 3, axis=-1)
            alpha = jax.nn.sigmoid(alpha_raw)
            beta = jax.nn.softplus(beta_raw)
            gate = jax.nn.sigmoid(gate_raw)
            error = x - mu
            v_next = alpha * v - beta * error
            x_next = x + DT * gate * v_next
            return (x_next, v_next)
        B, N, Dm = x.shape
        xf = x.reshape(B * N, Dm)
        logits = _gelu(xf @ w_r1 + b_r1) @ w_r2 + b_r2
        probs = jax.nn.softmax(logits, axis=-1)
        top_p, top_i = jax.lax.top_k(probs, K)
        top_p = top_p / jnp.sum(top_p, axis=-1, keepdims=True)
        flat_idx = top_i.reshape(-1)
        flat_w = top_p.reshape(-1, 1)
        v = jnp.zeros_like(xf)
        integrated = xf
        for _ in range(NUM_ITER):
            ctx = jnp.concatenate([integrated, v], axis=-1)
            shared_ctrl = _gelu(ctx @ w_s1 + b_s1) @ w_s2 + b_s2
            x_shared, v_shared = _inl(shared_ctrl, integrated, v, mu)
            sw = jax.nn.sigmoid(shared_weight)
            ctx_e = jnp.repeat(ctx, K, axis=0)
            x_e = jnp.repeat(integrated, K, axis=0)
            v_e = jnp.repeat(v, K, axis=0)
            w1 = expert_w1[flat_idx]
            b1 = expert_b1[flat_idx]
            w2 = expert_w2[flat_idx]
            b2 = expert_b2[flat_idx]
            hidden = _gelu(jnp.einsum('tc,tch->th', ctx_e, w1) + b1)
            ctrl = jnp.einsum('th,tho->to', hidden, w2) + b2
            x_r, v_r = _inl(ctrl, x_e, v_e, mu)
            x_r = (x_r * flat_w).reshape(B * N, K, Dm).sum(axis=1)
            v_r = (v_r * flat_w).reshape(B * N, K, Dm).sum(axis=1)
            x_next = sw * x_shared + (1.0 - sw) * x_r
            v_next = sw * v_shared + (1.0 - sw) * v_r
            halt = jax.nn.sigmoid(_gelu(x_next @ w_h1 + b_h1) @ w_h2 + b_h2)
            refined = _gelu(x_next @ w_f1 + b_f1) @ w_f2 + b_f2
            integrated = integrated + halt * refined * integration_weight
            v = v_next
        return integrated.reshape(B, N, Dm)
    x = L0_attn_x
    x = x + _L0_attn_ref(_layernorm(x, axis=-1), L0_attn_norm_attn_w, L0_attn_Wq, L0_attn_Wk, L0_attn_Wv, L0_attn_Wo, L0_attn_qn_w, L0_attn_kn_w, L0_attn_ssm_norm_w, L0_attn_Wx, L0_attn_Wdt, L0_attn_bdt, L0_attn_A_log, L0_attn_Dp, L0_attn_Wsel, L0_attn_bsel, L0_attn_sel_gate, L0_attn_Wimp, L0_attn_bimp, L0_attn_Wg, L0_attn_bg, L0_attn_Wout, L0_attn_norm_ffn_w, L0_attn_W1, L0_attn_W2)
    x = x + _L0_ffn_ref(_layernorm(x, axis=-1), L0_ffn_scores, L0_ffn_expert_weights, L0_ffn_expert_indices, L0_ffn_w1, L0_ffn_w2, L0_ffn_bias)
    x = x + _L1_attn_ref(_layernorm(x, axis=-1), L1_attn_W_dq, L1_attn_W_uq, L1_attn_W_dkv, L1_attn_W_uk, L1_attn_W_uv, L1_attn_W_o)
    x = x + _L1_ffn_ref(_layernorm(x, axis=-1), L1_ffn_w_r1, L1_ffn_b_r1, L1_ffn_w_r2, L1_ffn_b_r2, L1_ffn_w_h1, L1_ffn_b_h1, L1_ffn_w_h2, L1_ffn_b_h2, L1_ffn_expert_w1, L1_ffn_expert_b1, L1_ffn_expert_w2, L1_ffn_expert_b2, L1_ffn_w_s1, L1_ffn_b_s1, L1_ffn_w_s2, L1_ffn_b_s2, L1_ffn_shared_weight, L1_ffn_w_f1, L1_ffn_b_f1, L1_ffn_w_f2, L1_ffn_b_f2, L1_ffn_integration_weight, L1_ffn_mu)
    return x

_drawn_inputs = setup_inputs


def setup_inputs(seed=0):
    import zlib

    import numpy as np

    out = dict(_drawn_inputs(seed))
    spreads = {'L0_attn_norm_attn_w': (1.0, 0.6),
     'L0_attn_qn_w': (1.0, 0.6),
     'L0_attn_kn_w': (1.0, 0.6),
     'L0_attn_ssm_norm_w': (1.0, 0.6),
     'L0_attn_bdt': (0.0, 0.8),
     'L0_attn_Dp': (1.0, 0.6),
     'L0_attn_bsel': (0.0, 0.8),
     'L0_attn_sel_gate': (1.0, 0.6),
     'L0_attn_bimp': (0.0, 0.8),
     'L0_attn_bg': (0.0, 0.8),
     'L0_attn_norm_ffn_w': (1.0, 0.6),
     'L0_ffn_bias': (0.0, 0.8),
     'L1_ffn_b_r1': (0.0, 2.0),
     'L1_ffn_b_r2': (0.0, 2.0),
     'L1_ffn_b_h1': (0.0, 0.8),
     'L1_ffn_expert_b1': (0.0, 2.0),
     'L1_ffn_expert_b2': (0.0, 2.0),
     'L1_ffn_b_s1': (0.0, 2.0),
     'L1_ffn_b_s2': (0.0, 2.0),
     'L1_ffn_b_f1': (0.0, 0.8),
     'L1_ffn_b_f2': (0.0, 2.0),
     'L1_ffn_integration_weight': (0.5, 0.6),
     'L1_ffn_mu': (0.0, 2.0)}
    factors = {'L0_attn_Wq': 8.0,
     'L0_attn_Wk': 8.0,
     'L0_attn_Wv': 8.0,
     'L0_attn_Wo': 8.0,
     'L0_attn_Wx': 8.0,
     'L0_attn_Wdt': 8.0,
     'L0_attn_A_log': 8.0,
     'L0_attn_Wsel': 8.0,
     'L0_attn_Wimp': 8.0,
     'L0_attn_Wg': 8.0,
     'L0_attn_W1': 8.0,
     'L0_attn_W2': 8.0,
     'L1_attn_W_dq': 8.0,
     'L1_attn_W_uq': 8.0,
     'L1_attn_W_dkv': 8.0,
     'L1_attn_W_uk': 8.0,
     'L1_attn_W_uv': 8.0,
     'L1_attn_W_o': 8.0,
     'L1_ffn_w_r1': 64.0,
     'L1_ffn_w_r2': 55.001,
     'L1_ffn_w_h1': 8.0,
     'L1_ffn_w_h2': 8.0,
     'L1_ffn_expert_w1': 63.225,
     'L1_ffn_expert_w2': 54.452,
     'L1_ffn_w_s1': 28.723,
     'L1_ffn_w_s2': 21.643,
     'L1_ffn_w_f1': 8.0,
     'L1_ffn_w_f2': 8.0,
     'L0_ffn_expert_weights': 6.005,
     'L0_ffn_w1': 3.266,
     'L0_ffn_w2': 2.956}
    for name, (base, spread) in spreads.items():
        noise = np.random.default_rng([zlib.crc32(name.encode()), seed]).standard_normal(out[name].shape)
        drawn = base * np.exp(spread * noise) if base else spread * noise
        out[name] = jnp.asarray(drawn.astype(out[name].dtype))
    for name, factor in factors.items():
        out[name] = (out[name] * factor).astype(out[name].dtype)
    return out
```

```python
import numpy as np
import concourse.bass as bass
from concourse import mybir
from contextlib import ExitStack, contextmanager

F32 = mybir.dt.float32
BF16 = mybir.dt.bfloat16
I32 = mybir.dt.int32
ALU = mybir.AluOpType
ACT = mybir.ActivationFunctionType
AX = mybir.AxisListType

D = 128
BATCH, SEQ = 2, 1024
T = BATCH * SEQ
BLK = 512
NBLK = T // BLK
TILE = 128
NT = T // TILE
HEADS, KV, HD = 16, 4, 8
GROUPS = 4
N_STATE = 128
R_DT = 64
FF0 = 512
EXPERTS = 8
MOE_T = 512
EH = 64
BIG = 1.0e30

COLS = ["norm_attn_w", "ssm_norm_w", "bdt", "Dp", "bsel", "sel_gate", "bimp", "bg", "norm_ffn_w", "qn", "kn",
        "moe_bias", "b_r1", "b_h1", "b_f1_0", "b_f1_1", "b_f2", "iw", "mu", "b_h2", "shared_weight", "b_s1",
        "b_s2_0", "b_s2_1", "b_s2_2"] + [f"eb1_{p}" for p in range(4)] + [f"eb2_{e}_{c}" for e in range(8) for c in range(3)]
CI = {n: i for i, n in enumerate(COLS)}

MATS = {"ident": 128, "center": 128, "rot": 128, "mean8": 16, "mean128": 1, "eye96": 32, "iota8": 8,
        "mask_kq": 128, "mask_qk": 128,
        "Wq": 128, "Wk": 32, "Wv": 32, "Wo": 128, "Wx": R_DT + 2 * N_STATE, "Wdt": 128, "Wsel": 128, "Wimp": 128,
        "Wg": 128, "Wout": 128, "W1": 1024, "W2": 512, "A_log": 128,
        "W_dqT": 32, "W_dkvT": 32, "W_dq": 128, "W_uqT": 128, "W_uk": 32, "W_uv": 32, "W_oT": 128,
        "w_r1": 32, "w_r2": 8, "b_r2": 8, "w_h1": 32, "w_h2": 1, "w_s1": 128, "w_s2": 384, "w_f1": 256, "w_f2": 256,
        "ew1": 1024}
MOFF, _o = {}, 0
for _n, _w in MATS.items():
    MOFF[_n] = _o
    _o += _w
MTOT = _o


class Core:

    def __init__(self, nc, ctx):
        self.nc, self.ctx = nc, ctx
        self.sem_ctx, self.sems = ctx, []
        pairs = [ctx.enter_context(nc.psum_tensor(f"banks{2 * i}_{2 * i + 1}", [128, 2, BLK], F32)) for i in range(4)]
        self.pair = [p[:, :, :] for p in pairs]
        self.bank = [pairs[i // 2][:, i % 2, :] for i in range(8)]
        self.warm = self.sb("warm", [1, 1])
        self.mats = self.sb("mats", [128, MTOT])
        self.cols = self.sb("cols", [128, len(COLS)])
        self.x = self.sb("x", [128, T])
        self.hn = self.sb("hn", [128, T])

    def sb(self, name, shape, dt=F32, ctx=None):
        return (ctx or self.ctx).enter_context(self.nc.sbuf_tensor(name, shape, dt))

    def sem(self, name):
        s = self.sem_ctx.enter_context(self.nc.semaphore(name))
        self.sems.append(s)
        return s

    @contextmanager
    def scope(self):
        outer = self.sem_ctx, self.sems
        with ExitStack() as ctx:
            self.sem_ctx, self.sems = ctx, []
            yield
            sems = self.sems
            with self.nc.Block() as block:
                @block.gpsimd
                def _(pool):
                    for s in sems:
                        pool.sem_clear(s)
        self.sem_ctx, self.sems = outer

    def m(self, name, rows=128, lo=0, n=None):
        o = MOFF[name] + lo
        return self.mats[0:rows, o:o + (MATS[name] - lo if n is None else n)]

    def c(self, name, rows=128):
        i = CI[name]
        return self.cols[0:rows, i:i + 1]


def linker(eng, sem):
    n = [0]

    def link(ins):
        n[0] += 1
        ins.then_inc(sem, 1)
        eng.wait_ge(sem, n[0])
    return link


def blocks(n):
    return range(n // BLK)


def sl(i, w=BLK):
    return slice(i * w, (i + 1) * w)


def normalise(k, tag, src, ncols, outs, groups=1, eps=1e-5, centre=None):
    nc = k.nc
    nb, nt = ncols // BLK, ncols // TILE
    width = nt * groups
    with ExitStack() as ctx:
        sq = k.sb(f"{tag}_sq", [128, ncols], ctx=ctx)
        ve = k.sb(f"{tag}_ve", [128, width], ctx=ctx)
        sd = k.sb(f"{tag}_sd", [128, width], ctx=ctx)
        r = k.sb(f"{tag}_r", [128, width], ctx=ctx)
        t = k.sb(f"{tag}_t", [128, width], ctx=ctx)
        rx = r if groups == 1 else k.sb(f"{tag}_rx", [128, width, HD], ctx=ctx)
        centred = k.sem(f"{tag}_centred")
        src_ready = k.sem(f"{tag}_src_ready")
        squared = k.sem(f"{tag}_squared")
        stat_done = k.sem(f"{tag}_stat_done")
        var_ready = k.sem(f"{tag}_var_ready")
        sd_ready = k.sem(f"{tag}_sd_ready")
        r_ready = k.sem(f"{tag}_r_ready")
        spread = k.sem(f"{tag}_spread")
        scaled = k.sem(f"{tag}_scaled")
        own = k.sem(f"{tag}_own")
        stat = k.bank[6][:, 0:width]
        mean = k.m("mean128") if groups == 1 else k.m("mean8")
        per = BLK // TILE
        with nc.Block() as block:
            @block.tensor
            def _(pe):
                if centre is not None:
                    for b in range(nb):
                        nc.tensor.matmul(k.bank[b][:, :], k.m("center"), centre[:, sl(b)], start=True, stop=True)\
                            .then_inc(centred, 1)
                for b in range(nb):
                    pe.wait_ge(squared, b + 1)
                    for j in range(b * per, (b + 1) * per):
                        last = nc.tensor.matmul(stat[:, j * groups:(j + 1) * groups], sq[:, sl(j, TILE)], mean,
                                                start=True, stop=True)
                last.then_inc(stat_done, 1)
                pe.wait_ge(r_ready, 1)
                for b in range(nb):
                    if b >= 2:
                        pe.wait_ge(scaled, (b - 1) * len(outs))
                    elif centre is not None:
                        pe.wait_ge(src_ready, nb)
                    for j in range(per):
                        jt = b * per + j
                        if groups == 1:
                            lhs = r[:, jt:jt + 1].to_broadcast([128, 128])
                        else:
                            lhs = rx[:, jt * groups:(jt + 1) * groups, :].rearrange("p g d -> p (g d)")
                        last = nc.tensor.matmul(k.bank[4 + b % 2][:, sl(j, TILE)], lhs, k.m("ident"),
                                                start=True, stop=True)
                    last.then_inc(spread, 1)

            @block.scalar
            def _(act):
                for b in range(nb):
                    if centre is not None:
                        act.wait_ge(src_ready, b + 1)
                    nc.scalar.activation(sq[:, sl(b)], src[:, sl(b)], ACT.Square).then_inc(squared, 1)
                act.wait_ge(var_ready, 1)
                nc.scalar.activation(sd[:, :], ve[:, :], ACT.Sqrt).then_inc(sd_ready, 1)

            @block.vector
            def _(dve):
                link = linker(dve, own)
                if centre is not None:
                    for b in range(nb):
                        dve.wait_ge(centred, b + 1)
                        nc.vector.tensor_copy(src[:, sl(b)], k.bank[b][:, :]).then_inc(src_ready, 1)
                dve.wait_ge(stat_done, 1)
                nc.vector.tensor_scalar_add(ve[:, :], stat, eps).then_inc(var_ready, 1)
                dve.wait_ge(sd_ready, 1)
                link(nc.vector.reciprocal(r[:, :], sd[:, :]))
                link(nc.vector.tensor_tensor(t[:, :], r[:, :], r[:, :], ALU.mult))
                link(nc.vector.tensor_tensor(t[:, :], t[:, :], ve[:, :], ALU.mult))
                link(nc.vector.tensor_scalar(t[:, :], t[:, :], -0.5, 1.5, ALU.mult, ALU.add))
                if groups == 1:
                    nc.vector.tensor_tensor(r[:, :], r[:, :], t[:, :], ALU.mult).then_inc(r_ready, 1)
                else:
                    wide = [128, width, HD]
                    nc.vector.tensor_tensor(rx[:, :, :], r[:, :].unsqueeze(2).to_broadcast(wide),
                                            t[:, :].unsqueeze(2).to_broadcast(wide), ALU.mult).then_inc(r_ready, 1)
                if centre is not None:
                    dve.wait_ge(src_ready, nb)
                for b in range(nb):
                    dve.wait_ge(spread, b + 1)
                    for out, w in outs:
                        nc.vector.scalar_tensor_tensor(out[:, sl(b)], src[:, sl(b)], 1.0 if w is None else w,
                                                       k.bank[4 + b % 2][:, :], ALU.mult, ALU.mult)\
                            .then_inc(scaled, 1)


def split3(k, tag, src, parts, tmp, ncols, dst_dma):
    nc = k.nc
    hi = k.sem(f"{tag}_hi")
    r1 = k.sem(f"{tag}_r1")
    mid = k.sem(f"{tag}_mid")
    lo = k.sem(f"{tag}_lo")
    sent = k.sem(f"{tag}_sent")
    nb = ncols // BLK
    with nc.Block() as block:
        @block.scalar
        def _(act):
            for b in range(nb):
                nc.scalar.copy(parts[0][:, sl(b)], src[:, sl(b)]).then_inc(hi, 1)
            for b in range(nb):
                act.wait_ge(r1, b + 1)
                nc.scalar.copy(parts[1][:, sl(b)], tmp[:, sl(b)]).then_inc(mid, 1)

        @block.vector
        def _(dve):
            for b in range(nb):
                dve.wait_ge(hi, b + 1)
                nc.vector.tensor_tensor(tmp[:, sl(b)], src[:, sl(b)], parts[0][:, sl(b)], ALU.subtract).then_inc(r1, 1)
            for b in range(nb):
                dve.wait_ge(mid, b + 1)
                nc.vector.tensor_tensor(parts[2][:, sl(b)], tmp[:, sl(b)], parts[1][:, sl(b)], ALU.subtract).then_inc(lo, 1)

        @block.sync
        def _(sp):
            n = 0
            for p, (s, v) in enumerate(((hi, nb), (mid, nb), (lo, nb))):
                sp.wait_ge(s, v)
                n += dst_dma(sp, p, sent)
            sp.wait_ge(sent, 16 * n)


def replicate_terms(k, tag, lin, full, order):
    nc = k.nc
    done = k.sem(f"{tag}_done")
    with nc.Block() as block:
        @block.sync
        def _(sp):
            for j, p in enumerate(order):
                sp.dma_start(full[8 * j:8 * j + 8], lin[p].rearrange("(h d) t -> d h t", d=8)).then_inc(done, 16)
            sp.wait_ge(done, 16 * len(order))


def attention(k, tag, q_full, k_full, k_heads, v_aug, causal, attn_t):
    nc = k.nc
    scale = float(HD) ** -0.5
    shared = k_heads == GROUPS
    nk = 1 if shared else 4
    ROWS = 9 * HD
    MROW = 96
    KROWS = MROW + 3
    QT = SEQ // TILE
    with ExitStack() as ctx:
        qa = [k.sb(f"{tag}_qa{i}", [KROWS, 4, SEQ], BF16, ctx) for i in range(2)]
        ka = [k.sb(f"{tag}_ka{i}", [KROWS, nk, SEQ], BF16, ctx) for i in range(2)]
        probs = [k.sb(f"{tag}_probs{i}", [128, 2, BLK], F32, ctx) for i in range(3)]
        mx = k.sb(f"{tag}_mx", [128, QT * 4, 2], F32, ctx)
        mneg = k.sb(f"{tag}_mneg", [128, QT, 4], F32, ctx)
        mres = k.sb(f"{tag}_mres", [128, QT, 4], F32, ctx)
        mparts = k.sb(f"{tag}_mparts", [128, QT, 3, 4], BF16, ctx)
        mrow = k.sb(f"{tag}_mrow", [64, BLK], BF16, ctx)
        osb = k.sb(f"{tag}_osb", [128, BLK], F32, ctx)
        rden = k.sb(f"{tag}_rden", [128, 4, 4], F32, ctx)
        attn_tok = k.sb(f"{tag}_tok", [128, NT, HEADS * HD], F32, ctx)
        ident_b = k.sb(f"{tag}_identb", [128, 128], BF16, ctx)
        mask_kq = k.sb(f"{tag}_maskkq", [128, 128], BF16, ctx)
        mask_qk = k.sb(f"{tag}_maskqk", [128, 128], BF16, ctx)
        scores_max = [k.bank[0], k.bank[1]]
        scores_exp = [k.bank[2], k.bank[3], k.bank[4], k.bank[5]]
        out_acc = k.bank[6]
        turned = k.bank[7]

        max_units = []
        for qt in range(QT):
            for j in range(4):
                for half in range(2):
                    n = BLK if not causal else min(BLK, (qt + 1) * TILE - half * BLK)
                    if n > 0:
                        max_units.append((qt, j, half, n))
        exp_units = []
        for qb in range(2):
            for kt in range(QT if not causal else 4 * (qb + 1)):
                c0 = max(0, kt * TILE - qb * BLK) if causal else 0
                for hp in range(2):
                    exp_units.append((qb, kt, hp, c0))
        NM, NE = len(max_units), len(exp_units)
        half_end = [max(s for s, u in enumerate(exp_units) if u[0] == qb) for qb in range(2)]
        per_slot = 3

        loaded = k.sem(f"{tag}_loaded")
        const_ready = k.sem(f"{tag}_const")
        max_scored = k.sem(f"{tag}_max_scored")
        max_taken = k.sem(f"{tag}_max_taken")
        mparts_ready = k.sem(f"{tag}_mparts_ready")
        mturned = k.sem(f"{tag}_mturned")
        mrow_ready = k.sem(f"{tag}_mrow_ready")
        mrow_sent = k.sem(f"{tag}_mrow_sent")
        exp_scored = k.sem(f"{tag}_exp_scored")
        probs_ready = k.sem(f"{tag}_probs_ready")
        pv_done = k.sem(f"{tag}_pv_done")
        osb_ready = k.sem(f"{tag}_osb_ready")
        oturned = k.sem(f"{tag}_oturned")
        normed = k.sem(f"{tag}_normed")
        own_dve = k.sem(f"{tag}_own_dve")
        own_pool = k.sem(f"{tag}_own_pool")
        final_turned = k.sem(f"{tag}_final_turned")
        final_copied = k.sem(f"{tag}_final_copied")

        vst = [k.sb(f"{tag}_vst{i}", [128, QT, nk, 32], F32, ctx) for i in range(2)]
        vstaged = k.sem(f"{tag}_vstaged")

        with nc.Block() as block:
            @block.sync
            def _(sp):
                def load(i, g, b):
                    toks = slice(b * SEQ, (b + 1) * SEQ)
                    sp.dma_start(qa[b][0:ROWS, :, :], q_full[:, bass.ds(4 * g, 4), toks]).then_inc(loaded, 16)
                    ks = bass.ds(g, 1) if shared else bass.ds(4 * g, 4)
                    sp.dma_start(ka[b][0:ROWS, :, :], k_full[:, ks, toks]).then_inc(loaded, 16)

                def rows(i, b):
                    sp.wait_ge(mrow_ready, 2 * i + 2)
                    for p in range(3):
                        for half in range(2):
                            sp.dma_start(qa[b][MROW + p:MROW + p + 1, :, sl(half)],
                                         mrow[32 * half + 4 * p:32 * half + 4 * p + 4, :]).then_inc(mrow_sent, 16)

                def body(g, b, last):
                    i = 2 * g + b
                    if not last:
                        sp.wait_ge(pv_done, NE * i)
                        load(i + 1, g if b == 0 else g + 1, 1 - b)
                        rows(i + 1, 1 - b)

                sp.wait_ge(const_ready, 2)
                load(0, 0, 0)
                rows(0, 0)
                body(0, 0, False)
                body(0, 1, False)
                with sp.Fori(1, GROUPS - 1) as g:
                    body(g, 0, False)
                    body(g, 1, False)
                body(GROUPS - 1, 0, False)
                body(GROUPS - 1, 1, True)

            @block.gpsimd
            def _(pool):
                link = linker(pool, own_pool)
                for b in range(2):
                    link(nc.gpsimd.memset(qa[b][64:KROWS, :, :], 0.0))
                    link(nc.gpsimd.memset(ka[b][64:96, :, :], 0.0))
                    link(nc.gpsimd.memset(ka[b][MROW:KROWS, :, :], 1.0))
                    pool.sem_inc(const_ready, 1)
                nc.gpsimd.tensor_copy(ident_b[:, :], k.m("ident")).then_inc(const_ready, 1)
                nc.gpsimd.tensor_copy(mask_kq[:, :], k.m("mask_kq")).then_inc(const_ready, 1)
                nc.gpsimd.tensor_copy(mask_qk[:, :], k.m("mask_qk")).then_inc(const_ready, 1)

            @block.tensor
            def _(pe):
                def kj(j):
                    return 0 if shared else j

                def max_unit(i, b, n):
                    qt, j, half, w = max_units[n]
                    if n == 0:
                        pe.wait_ge(loaded, 32 * (i + 1))
                    pe.wait_ge(max_taken, NM * i + max(n - 1, 0))
                    diag = causal and half * BLK + w == (qt + 1) * TILE
                    out = scores_max[n % 2]
                    ins = nc.tensor.matmul(out[:, 0:w], qa[b][0:ROWS, j, sl(qt, TILE)],
                                           ka[b][0:ROWS, kj(j), half * BLK:half * BLK + w], start=True, stop=not diag)
                    if diag:
                        ins = nc.tensor.matmul(out[:, w - TILE:w], ident_b[:, :], mask_qk[:, :], start=False, stop=True)
                    ins.then_inc(max_scored, 1)

                def turn_max(i):
                    pe.wait_ge(mparts_ready, i + 1)
                    pe.wait_ge(normed, 2 * i)
                    for qt in range(QT):
                        p0 = 32 * (qt // 4)
                        last = nc.tensor.matmul(turned[p0:p0 + 12, sl(qt % 4, TILE)],
                                                mparts[:, qt, :, :].rearrange("p a j -> p (a j)"), ident_b[:, :],
                                                start=True, stop=True)
                    last.then_inc(mturned, 1)

                def exp_unit(i, b, s):
                    qb, kt, hp, c0 = exp_units[s]
                    if s == 0:
                        pe.wait_ge(mrow_sent, 96 * (i + 1))
                    pe.wait_ge(probs_ready, NE * i + max(s - 1, 0))
                    for jj in range(2):
                        j = 2 * hp + jj
                        out = scores_exp[2 * (s % 2) + jj]
                        diag = causal and kt // 4 == qb
                        ins = nc.tensor.matmul(out[:, c0:BLK], ka[b][:, kj(j), sl(kt, TILE)],
                                               qa[b][:, j, qb * BLK + c0:(qb + 1) * BLK], start=True, stop=not diag)
                        if diag:
                            ins = nc.tensor.matmul(out[:, c0:c0 + TILE], ident_b[:, :], mask_kq[:, :],
                                                   start=False, stop=True)
                    ins.then_inc(exp_scored, 1)

                def pv_unit(i, b, g, s, vstage):
                    qb, kt, hp, c0 = exp_units[s]
                    pe.wait_ge(probs_ready, NE * i + s + 1)
                    if s == 0 or s == half_end[0] + 1:
                        pe.wait_ge(osb_ready, 2 * i + qb)
                    for jj in range(2):
                        j = 2 * hp + jj
                        last = nc.tensor.matmul(out_acc[32 * j:32 * j + 32, c0:BLK], vstage[:, kt, kj(j), :],
                                                probs[s % 3][:, jj, c0:BLK], start=kt == 0,
                                                stop=s + 1 >= half_end[qb])
                    last.then_inc(pv_done, 1)

                def turn_out(i, qb):
                    pe.wait_ge(osb_ready, 2 * i + qb + 1)
                    pe.wait_ge(normed, 2 * i + qb)
                    pe.wait_ge(mrow_ready, 2 * i + 2)
                    for t in range(4):
                        last = nc.tensor.matmul(turned[:, sl(t, TILE)], osb[:, sl(t, TILE)], k.m("ident"),
                                                start=True, stop=True)
                    last.then_inc(oturned, 1)

                def body(g, b, last):
                    i = 2 * g + b
                    pe.wait_ge(vstaged, i + 1)
                    done = 0
                    for s in range(NE):
                        exp_unit(i, b, s)
                        if s >= 1:
                            pv_unit(i, b, g, s - 1, vst[b])
                        if s == half_end[0] + 3:
                            turn_out(i, 0)
                        if not last:
                            while done < NM and done < per_slot * (s + 1):
                                max_unit(i + 1, 1 - b, done)
                                done += 1
                    pv_unit(i, b, g, NE - 1, vst[b])
                    while not last and done < NM:
                        max_unit(i + 1, 1 - b, done)
                        done += 1
                    turn_out(i, 1)
                    if not last:
                        turn_max(i + 1)

                pe.wait_ge(const_ready, 5)
                for n in range(NM):
                    max_unit(0, 0, n)
                turn_max(0)
                body(0, 0, False)
                body(0, 1, False)
                with pe.Fori(1, GROUPS - 1) as g:
                    body(g, 0, False)
                    body(g, 1, False)
                body(GROUPS - 1, 0, False)
                body(GROUPS - 1, 1, True)
                pe.wait_ge(normed, 16)
                for n in range(NBLK):
                    if n >= 2:
                        pe.wait_ge(final_copied, n - 1)
                    for t in range(4):
                        last = nc.tensor.matmul(scores_max[n % 2][:, sl(t, TILE)], attn_tok[:, 4 * n + t, :],
                                                k.m("ident"), start=True, stop=True)
                    last.then_inc(final_turned, 1)

            @block.scalar
            def _(act):
                def rows(i):
                    act.wait_ge(mturned, i + 1)
                    act.wait_ge(mrow_sent, 96 * i)
                    for half in range(2):
                        nc.scalar.copy(mrow[32 * half:32 * half + 12, :], turned[32 * half:32 * half + 12, :])\
                            .then_inc(mrow_ready, 1)

                def out_copy(i, qb):
                    act.wait_ge(pv_done, NE * i + half_end[qb] + 1)
                    act.wait_ge(oturned, 2 * i + qb)
                    nc.scalar.copy(osb[:, :], out_acc[:, :]).then_inc(osb_ready, 1)

                def body(g, b, last):
                    i = 2 * g + b
                    for s in range(NE):
                        qb, kt, hp, c0 = exp_units[s]
                        act.wait_ge(exp_scored, NE * i + s + 1)
                        act.wait_ge(pv_done, NE * i + max(s - 2, 0))
                        src = k.pair[1 + s % 2][:, :, c0:BLK]
                        nc.scalar.activation(probs[s % 3][:, :, c0:BLK], src, ACT.Exp, scale=scale)\
                            .then_inc(probs_ready, 1)
                        if s == half_end[0] + 2:
                            out_copy(i, 0)
                        if s == 2 and not last:
                            stage_next(g, b)
                    out_copy(i, 1)
                    if not last:
                        rows(i + 1)

                def stage_next(g, b):
                    i = 2 * g + b
                    act.wait_ge(pv_done, NE * i)
                    g1 = g if b == 0 else g + 1
                    vs = bass.ds(g1, 1) if shared else bass.ds(4 * g1, 4)
                    nb_ = 1 - b
                    nc.scalar.copy(vst[nb_][:, :, :, :], v_aug[:, nb_ * QT:(nb_ + 1) * QT, vs, :]).then_inc(vstaged, 1)

                nc.scalar.activation(k.warm[:, :], k.m("ident")[0:1, 0:1], ACT.Exp)
                vs = slice(0, 1) if shared else slice(0, 4)
                nc.scalar.copy(vst[0][:, :, :, :], v_aug[:, 0:QT, vs, :]).then_inc(vstaged, 1)
                rows(0)
                body(0, 0, False)
                body(0, 1, False)
                with act.Fori(1, GROUPS - 1) as g:
                    body(g, 0, False)
                    body(g, 1, False)
                body(GROUPS - 1, 0, False)
                body(GROUPS - 1, 1, True)
                for n in range(NBLK):
                    act.wait_ge(final_turned, n + 1)
                    nc.scalar.copy(attn_t[:, sl(n)], scores_max[n % 2][:, :]).then_inc(final_copied, 1)

            @block.vector
            def _(dve):
                def link(ins, value):
                    ins.then_inc(own_dve, 1)
                    dve.wait_ge(own_dve, value)

                def take_max(i, n):
                    qt, j, half, w = max_units[n]
                    dve.wait_ge(max_scored, NM * i + n + 1)
                    nc.vector.reduce_max(mx[:, 4 * qt + j, half:half + 1], scores_max[n % 2][:, 0:w], AX.X)\
                        .then_inc(max_taken, 1)

                def combine(i):
                    base = 7 * i + 1
                    mn = mneg[:, :, :].rearrange("p a b -> p (a b)")
                    dve.wait_ge(max_taken, NM * (i + 1))
                    dve.wait_ge(mturned, i)
                    link(nc.vector.tensor_reduce(mn, mx[:, :, :], AX.X, ALU.max), base + 1)
                    link(nc.vector.tensor_scalar_mul(mn, mn, -1.0), base + 2)
                    link(nc.vector.tensor_copy(mparts[:, :, 0, :], mneg[:, :, :]), base + 3)
                    link(nc.vector.tensor_tensor(mres[:, :, :], mneg[:, :, :], mparts[:, :, 0, :], ALU.subtract),
                         base + 4)
                    link(nc.vector.tensor_copy(mparts[:, :, 1, :], mres[:, :, :]), base + 5)
                    nc.vector.tensor_tensor(mparts[:, :, 2, :], mres[:, :, :], mparts[:, :, 1, :], ALU.subtract)\
                        .then_inc(mparts_ready, 1)
                    dve.wait_ge(mparts_ready, i + 1)

                def out_norm(i, g, b, qb):
                    dve.wait_ge(oturned, 2 * i + qb + 1)
                    dve.wait_ge(normed, 2 * i + qb)
                    tv = turned[:, :].rearrange("p (t j c) -> p t j c", t=4, j=4)
                    link(nc.vector.reciprocal(rden[:, :, :], tv[:, :, :, 8]), 7 * i + 1 + 5 + qb + 1)
                    t0 = b * QT + 4 * qb
                    dst = attn_tok[:, t0:t0 + 4, bass.ds(32 * g, 32)].rearrange("p t (j c) -> p t j c", j=4)
                    nc.vector.tensor_tensor(dst, tv[:, :, :, 0:8],
                                            rden[:, :, :].unsqueeze(3).to_broadcast([128, 4, 4, 8]), ALU.mult)\
                        .then_inc(normed, 1)

                def body(g, b, last):
                    i = 2 * g + b
                    first = 0 if last else min(NM, per_slot * (half_end[0] + 3))
                    for n in range(first):
                        take_max(i + 1, n)
                    out_norm(i, g, b, 0)
                    for n in range(first, 0 if last else NM):
                        take_max(i + 1, n)
                    out_norm(i, g, b, 1)
                    if not last:
                        combine(i + 1)

                link(nc.vector.memset(mx[:, :, :], -BIG), 1)
                for n in range(NM):
                    take_max(0, n)
                combine(0)
                body(0, 0, False)
                body(0, 1, False)
                with dve.Fori(1, GROUPS - 1) as g:
                    body(g, 0, False)
                    body(g, 1, False)
                body(GROUPS - 1, 0, False)
                body(GROUPS - 1, 1, True)


def products(k, tag, steps):
    nc = k.nc
    made = k.sem(f"{tag}_made")
    taken = {e: k.sem(f"{tag}_taken_{e}") for e in ("act", "dve")}

    def before(n, engine):
        return sum(1 for s in steps[:n] if s[0] == engine)

    def takers(eng, name):
        for n, (engine, _, take) in enumerate(steps):
            if engine == name:
                eng.wait_ge(made, n + 1)
                take(k.bank[n % 8]).then_inc(taken[name], 1)

    with nc.Block() as block:
        @block.tensor
        def _(pe):
            for n, (_, mms, _) in enumerate(steps):
                if n >= 8:
                    engine = steps[n - 8][0]
                    pe.wait_ge(taken[engine], before(n - 7, engine))
                for rows, cols, lhs, rhs, first, last in mms:
                    ins = nc.tensor.matmul(k.bank[n % 8][rows, cols], lhs, rhs, start=first, stop=last)
                ins.then_inc(made, 1)

        @block.scalar
        def _(act):
            takers(act, "act")

        @block.vector
        def _(dve):
            takers(dve, "dve")


def one(lhs, rhs, rows=slice(0, 128), cols=slice(0, BLK)):
    return [(rows, cols, lhs, rhs, True, True)]


def project_qkv(k, xa, qf, kf, v_aug):
    nc = k.nc
    cleared = k.sem("v_cleared")
    with nc.Block() as block:
        @block.gpsimd
        def _(pool):
            nc.gpsimd.memset(v_aug[:, :, :, :], 0.0).then_inc(cleared, 1)
            pool.wait_ge(cleared, 1)
            nc.gpsimd.memset(v_aug[:, :, :, HD:HD + 1], 1.0).then_inc(cleared, 1)
    steps = []
    for b in blocks(T):
        steps.append(("act", one(k.m("Wq"), xa[:, sl(b)]), lambda p, b=b: nc.scalar.copy(qf[:, sl(b)], p)))
    steps.append(("dve", [(slice(32 * b, 32 * b + 32), slice(0, BLK), k.m("Wk"), xa[:, sl(b)], True, True)
                          for b in blocks(T)], lambda p: nc.vector.tensor_copy(kf[:, :], p)))
    steps.append(("dve", [(slice(0, 128), sl(t, 32), xa[:, sl(t, TILE)], k.m("Wv"), True, True) for t in range(NT)],
                  lambda p: nc.vector.tensor_copy(v_aug[:, :, :, 0:HD],
                                                  p.rearrange("p (t g d) -> p t g d", t=NT, g=KV))))
    products(k, "qkv", steps)


def rope(k, tag, src, table, ncols, period, t1):
    nc = k.nc
    rotated = k.sem(f"{tag}_rotated")
    cos_done = k.sem(f"{tag}_cos_done")
    sin_done = k.sem(f"{tag}_sin_done")
    nb = ncols // BLK
    with nc.Block() as block:
        @block.tensor
        def _(pe):
            for b in range(nb):
                nc.tensor.matmul(k.bank[b][:, :], k.m("rot"), src[:, sl(b)], start=True, stop=True).then_inc(rotated, 1)

        @block.gpsimd
        def _(pool):
            for b in range(nb):
                nc.gpsimd.tensor_tensor(t1[:, sl(b)], src[:, sl(b)], table[:, 0, sl(b % (period // BLK))], ALU.mult)\
                    .then_inc(cos_done, 1)

        @block.vector
        def _(dve):
            for b in range(nb):
                dve.wait_ge(rotated, b + 1)
                dve.wait_ge(cos_done, b + 1)
                nc.vector.tensor_tensor(src[:, sl(b)], table[:, 1, sl(b % (period // BLK))], k.bank[b][:, :], ALU.mult)\
                    .then_inc(sin_done, 1)
            for b in range(nb):
                dve.wait_ge(sin_done, b + 1)
                nc.vector.tensor_tensor(src[:, sl(b)], src[:, sl(b)], t1[:, sl(b)], ALU.add)


def send_linear(k, lin, parts):
    def send(eng, p, sem):
        eng.dma_start(lin[p], parts[p][:, :]).then_inc(sem, 16)
        return 1
    return send


Q_ORDER = [0, 0, 0, 1, 1, 1, 2, 2, 2]
K_ORDER = [0, 1, 2] * 3


def hybrid_attention(k, d, rope_q, rope_k, attn_t):
    nc = k.nc
    with ExitStack() as ctx:
        v_aug = k.sb("v_aug", [128, NT, KV, 32], ctx=ctx)
        with ExitStack() as pre:
            xa = k.sb("xa", [128, T], ctx=pre)
            qf = k.sb("qf", [128, T], ctx=pre)
            kf = k.sb("kf", [128, BLK], ctx=pre)
            tmp = k.sb("rtmp", [128, T], ctx=pre)
            tq = k.sb("rope_q", [128, 2, SEQ], ctx=pre)
            tk = k.sb("rope_k", [128, 2, BLK], ctx=pre)
            parts = [k.sb(f"qparts{i}", [128, T], BF16, pre) for i in range(3)]
            tables = k.sem("rope_tables")
            with nc.Block() as block:
                @block.sync
                def _(sp):
                    sp.dma_start(tq[:, :, :], rope_q).then_inc(tables, 16)
                    sp.dma_start(tk[:, :, :], rope_k).then_inc(tables, 16)
                    sp.wait_ge(tables, 32)
            normalise(k, "rms_a", k.hn, T, [(xa, k.c("norm_attn_w"))], eps=1e-6)
            project_qkv(k, xa, qf, kf, v_aug)
            normalise(k, "rms_q", qf, T, [(qf, k.c("qn"))], groups=16, eps=1e-6)
            normalise(k, "rms_k", kf, BLK, [(kf, k.c("kn"))], groups=16, eps=1e-6)
            rope(k, "rope_q", qf, tq, T, SEQ, tmp)
            rope(k, "rope_k", kf, tk, BLK, BLK, tmp)
            split3(k, "split_q", qf, parts, tmp, T, send_linear(k, d["q_lin"], parts))

            def send_k(eng, p, sem):
                for b in blocks(T):
                    eng.dma_start(d["k_lin"][p, 0:32, sl(b)], parts[p][32 * b:32 * b + 32, 0:BLK]).then_inc(sem, 16)
                return NBLK
            split3(k, "split_k", kf, parts, tmp, BLK, send_k)
            replicate_terms(k, "rep_q", d["q_lin"], d["q_full"], Q_ORDER)
            replicate_terms(k, "rep_k", d["k_lin"][:, 0:32], d["k_full"][:, 0:KV], K_ORDER)
        attention(k, "attn0", d["q_full"], d["k_full"], KV, v_aug, False, attn_t)


def softplus(k, tag, z, out, tmp):
    nc = k.nc
    own = k.sem(f"{tag}_own")
    logs = k.sem(f"{tag}_logs")
    with nc.Block() as block:
        @block.scalar
        def _(act):
            link = linker(act, own)
            link(nc.scalar.activation(tmp, z, ACT.Abs))
            link(nc.scalar.activation(tmp, tmp, ACT.Exp, scale=-1.0))
            nc.scalar.activation(tmp, tmp, ACT.Ln, bias=1.0).then_inc(logs, 1)

        @block.vector
        def _(dve):
            dve.wait_ge(logs, 1)
            nc.vector.scalar_tensor_tensor(out, z, 0.0, tmp, ALU.max, ALU.add)


def state_space(k, ssm_in):
    nc = k.nc
    with ExitStack() as ctx:
        bt = k.sb("bt", [128, T], ctx=ctx)
        ct = k.sb("ct", [128, T], ctx=ctx)
        a_neg = k.sb("a_neg", [128, 128], ctx=ctx)
        dparts = k.sb("dparts", [96, 4, T], BF16, ctx)
        xparts = k.sb("xparts", [96, 4, T], BF16, ctx)
        sel = k.sb("sel", [96, 32, 128], BF16, ctx)
        onehot = k.sb("onehot", [128, 32, 32], F32, ctx)
        with ExitStack() as pre:
            xn = k.sb("xn", [128, T], ctx=pre)
            gate = k.sb("gate", [128, T], ctx=pre)
            delta = k.sb("delta", [128, T], ctx=pre)
            dr = k.sb("dr", [R_DT, T], ctx=pre)
            tmp = k.sb("stmp", [128, T], ctx=pre)
            bsg = k.sb("bsg", [128, 1], ctx=pre)
            parts = [k.sb(f"sparts{i}", [128, T], BF16, pre) for i in range(3)]
            prep = k.sem("ssm_prep")
            one_sem = k.sem("ssm_onehot")
            with nc.Block() as block:
                @block.scalar
                def _(act):
                    nc.scalar.activation(a_neg[:, :], k.m("A_log"), ACT.Exp).then_inc(prep, 1)

                @block.vector
                def _(dve):
                    nc.vector.tensor_tensor(bsg[:, :], k.c("bsel"), k.c("sel_gate"), ALU.mult)
                    nc.vector.tensor_copy(sel[:, :, :], k.m("eye96", 96).unsqueeze(2).to_broadcast([96, 32, 128]))
                    dve.wait_ge(prep, 1)
                    nc.vector.tensor_scalar_mul(a_neg[:, :], a_neg[:, :], -1.0)

                @block.gpsimd
                def _(pool):
                    nc.gpsimd.memset(onehot[:, :, :], 0.0).then_inc(one_sem, 1)
                    pool.wait_ge(one_sem, 1)
                    nc.gpsimd.affine_select(out=onehot[:, :, :], in_=onehot[:, :, :], compare_op=ALU.not_equal,
                                            fill=1.0, base=0, pattern=[[1, 32], [-1, 32]], channel_multiplier=0)
            normalise(k, "rms_s", k.hn, T, [(xn, k.c("ssm_norm_w"))], eps=1e-6)
            steps = []
            for b in blocks(T):
                x = xn[:, sl(b)]
                steps += [
                    ("act", one(k.m("Wx", lo=0, n=R_DT), x, rows=slice(0, R_DT)),
                     lambda p, b=b: nc.scalar.copy(dr[:, sl(b)], p[0:R_DT, :])),
                    ("dve", one(k.m("Wx", lo=R_DT, n=N_STATE), x),
                     lambda p, b=b: nc.vector.tensor_copy(bt[:, sl(b)], p)),
                    ("act", one(k.m("Wsel"), x),
                     lambda p, b=b: nc.scalar.activation(gate[:, sl(b)], p, ACT.Sigmoid, bias=bsg[:, :],
                                                         scale=k.c("sel_gate"))),
                    ("dve", one(k.m("Wx", lo=R_DT + N_STATE, n=N_STATE), x),
                     lambda p, b=b: nc.vector.tensor_copy(ct[:, sl(b)], p))]
            products(k, "ssm_p1", steps)
            with nc.Block() as block:
                @block.vector
                def _(dve):
                    nc.vector.tensor_tensor(xn[:, :], xn[:, :], gate[:, :], ALU.mult)
            steps = []
            for b in blocks(T):
                x = xn[:, sl(b)]
                steps += [
                    ("dve", one(k.m("Wdt", R_DT), dr[:, sl(b)]),
                     lambda p, b=b: nc.vector.tensor_scalar_add(delta[:, sl(b)], p, k.c("bdt"))),
                    ("act", one(k.m("Wimp"), x),
                     lambda p, b=b: nc.scalar.activation(tmp[:, sl(b)], p, ACT.Sigmoid, bias=k.c("bimp"))),
                    ("act", one(k.m("Wg"), x),
                     lambda p, b=b: nc.scalar.activation(gate[:, sl(b)], p, ACT.Sigmoid, bias=k.c("bg")))]
            products(k, "ssm_p2", steps)
            with nc.Block() as block:
                @block.vector
                def _(dve):
                    nc.vector.tensor_tensor(bt[:, :], bt[:, :], tmp[:, :], ALU.mult)
                    nc.vector.tensor_tensor(xn[:, :], xn[:, :], gate[:, :], ALU.mult)

                @block.gpsimd
                def _(pool):
                    nc.gpsimd.tensor_tensor(ct[:, :], ct[:, :], tmp[:, :], ALU.mult)
            softplus(k, "delta", delta[:, :], delta[:, :], tmp[:, :])
            with nc.Block() as block:
                @block.vector
                def _(dve):
                    nc.vector.tensor_tensor(xn[:, :], xn[:, :], delta[:, :], ALU.mult)

            def spread_to(dst):
                def send(eng, p, sem):
                    for g in range(4):
                        eng.dma_start(dst[32 * p:32 * p + 32, g, :], parts[p][32 * g:32 * g + 32, :]).then_inc(sem, 16)
                    return 4
                return send
            split3(k, "split_dt", delta, parts, tmp, T, spread_to(dparts))
            split3(k, "split_dtx", xn, parts, tmp, T, spread_to(xparts))
        scan_states(k, bt, ct, a_neg, dparts, xparts, sel, onehot, ssm_in)


def scan_states(k, bt, ct, a_neg, dparts, xparts, sel, onehot, ssm_in):
    nc = k.nc
    with ExitStack() as ctx:
        da = [k.sb(f"da{i}", [128, SEQ], ctx=ctx) for i in range(2)]
        inp = [k.sb(f"inp{i}", [128, SEQ], ctx=ctx) for i in range(2)]
        st = [k.sb(f"st{i}", [128, SEQ], ctx=ctx) for i in range(2)]
        hc = [k.sb(f"hc{i}", [128, SEQ], ctx=ctx) for i in range(2)]
        col = [k.sb(f"onecol{i}", [128, 32], ctx=ctx) for i in range(2)]
        zero = k.sb("zero_b", [128, BLK], BF16, ctx)
        a_now = k.sb("a_now", [128, 4, 2], ctx=ctx)
        a_copied = k.sem("scan_a_copied")
        zeroed = k.sem("scan_zeroed")
        dt_spread = k.sem("scan_dt_spread")
        dtx_spread = k.sem("scan_dtx_spread")
        decay_ready = k.sem("scan_decay_ready")
        input_ready = k.sem("scan_input_ready")
        state_ready = k.sem("scan_state_ready")
        hc_ready = k.sem("scan_hc_ready")
        summed = k.sem("scan_summed")
        col_ready = k.sem("scan_col_ready")
        closed = k.sem("scan_closed")
        AHEAD = 3
        UNITS = 16
        STEPS = 16
        y_bank = [[k.bank[0], k.bank[1]], [k.bank[2], k.bank[3]]]
        dt_bank = [k.bank[4], k.bank[5]]
        dtx_bank = [k.bank[6], k.bank[7]]

        def where(n):
            return n // 8, (n // 2) % 4, n % 2

        with nc.Block() as block:
            @block.tensor
            def _(pe):
                def spread(jj, n):
                    jp, g, b = where(n)
                    u = UNITS * jj + n
                    w = sel[:, bass.ds(2 * jj + jp, 1), :].rearrange("p a m -> p (a m)")
                    for h in range(2):
                        cols = slice(b * SEQ + h * BLK, b * SEQ + (h + 1) * BLK)
                        pe.wait_ge(decay_ready, first_zero(2 * u + h - 1, u))
                        nc.tensor.matmul(dt_bank[h][:, :], w, dparts[:, g, cols], start=True, stop=True)\
                            .then_inc(dt_spread, 1)
                        pe.wait_ge(input_ready, first_zero(2 * u + h - 1, u))
                        nc.tensor.matmul(dtx_bank[h][:, :], w, xparts[:, g, cols], start=True, stop=True)\
                            .then_inc(dtx_spread, 1)

                def first_zero(value, u):
                    return max(value, 0) if isinstance(u, int) else value

                def reduce(jj, n):
                    jp, g, b = where(n)
                    u = UNITS * jj + n
                    if n % 8 == 0:
                        pe.wait_ge(col_ready, 2 * jj + jp + 1)
                    pe.wait_ge(hc_ready, u + 1)
                    for h in range(2):
                        last = nc.tensor.matmul(y_bank[b][h][32 * g:32 * g + 32, :], col[jp][:, :],
                                                hc[b][:, sl(h)], start=False, stop=False, skip_group_check=True)
                    last.then_inc(summed, 1)

                pe.wait_ge(zeroed, 1)
                for b in range(2):
                    for h in range(2):
                        nc.tensor.matmul(y_bank[b][h][:, :], zero[:, 0:128], zero[:, :], start=True, stop=False,
                                         skip_group_check=True)
                for n in range(AHEAD):
                    spread(0, n)

                def step(jj, last):
                    for n in range(UNITS):
                        if n + AHEAD < UNITS:
                            spread(jj, n + AHEAD)
                        elif not last:
                            spread(jj + 1, n + AHEAD - UNITS)
                        reduce(jj, n)

                step(0, False)
                with pe.Fori(1, STEPS - 1) as jj:
                    step(jj, False)
                step(STEPS - 1, True)
                for b in range(2):
                    for h in range(2):
                        last = nc.tensor.matmul(y_bank[b][h][:, :], zero[:, 0:128], zero[:, :], start=False, stop=True,
                                                skip_group_check=True)
                last.then_inc(closed, 1)

            @block.scalar
            def _(act):
                nc.scalar.activation(k.warm[:, :], k.m("ident")[0:1, 0:1], ACT.Exp)

                def columns(jj):
                    act.wait_ge(decay_ready, 2 * UNITS * jj)
                    src = a_neg[:, :].rearrange("p (g j) -> p g j", g=4)[:, :, bass.ds(2 * jj, 2)]
                    nc.scalar.copy(a_now[:, :, :], src).then_inc(a_copied, 1)
                    act.wait_ge(a_copied, jj + 1)

                def decay(jj, n):
                    jp, g, b = where(n)
                    u = UNITS * jj + n
                    a_col = a_now[:, g, jp:jp + 1]
                    act.wait_ge(state_ready, u - 1 if not isinstance(u, int) or u > 0 else 0)
                    for h in range(2):
                        act.wait_ge(dt_spread, 2 * u + h + 1)
                        nc.scalar.activation(da[b][:, sl(h)], dt_bank[h][:, :], ACT.Exp, scale=a_col)\
                            .then_inc(decay_ready, 1)

                columns(0)
                for n in range(UNITS):
                    decay(0, n)
                with act.Fori(1, STEPS) as jj:
                    columns(jj)
                    for n in range(UNITS):
                        decay(jj, n)

            @block.vector
            def _(dve):
                nc.vector.memset(zero[:, :], 0.0).then_inc(zeroed, 1)

                def make_input(u, b):
                    for h in range(2):
                        dve.wait_ge(dtx_spread, 2 * u + h + 1)
                        nc.vector.tensor_tensor(inp[b][:, sl(h)], bt[:, b * SEQ + h * BLK:b * SEQ + (h + 1) * BLK],
                                                dtx_bank[h][:, :], ALU.mult).then_inc(input_ready, 1)

                def scan(u, b):
                    dve.wait_ge(decay_ready, 2 * u + 2)
                    dve.wait_ge(input_ready, 2 * u + 2)
                    dve.wait_ge(hc_ready, u - 1 if not isinstance(u, int) or u > 0 else 0)
                    nc.vector.tensor_tensor_scan(st[b][:, :], da[b][:, :], inp[b][:, :], 0.0, ALU.mult, ALU.add)\
                        .then_inc(state_ready, 1)

                def unit(jj, n, last):
                    u = UNITS * jj + n
                    if not last:
                        dve.wait_ge(state_ready, u)
                        make_input(u + 1, (n + 1) % 2)
                    scan(u, n % 2)

                make_input(0, 0)
                for n in range(UNITS):
                    unit(0, n, False)
                with dve.Fori(1, STEPS - 1) as jj:
                    for n in range(UNITS):
                        unit(jj, n, False)
                for n in range(UNITS):
                    unit(STEPS - 1, n, n == UNITS - 1)

            @block.gpsimd
            def _(pool):
                def unit(jj, n):
                    jp, g, b = where(n)
                    u = UNITS * jj + n
                    if n % 8 == 0:
                        j = 2 * jj + jp
                        pool.wait_ge(summed, 8 * j - 8 if not isinstance(j, int) or j > 0 else 0)
                        nc.gpsimd.tensor_copy(col[jp][:, :], onehot[:, bass.ds(j, 1), :].rearrange("p a c -> p (a c)"))\
                            .then_inc(col_ready, 1)
                    pool.wait_ge(state_ready, u + 1)
                    pool.wait_ge(summed, u - 1 if not isinstance(u, int) or u > 0 else 0)
                    nc.gpsimd.tensor_tensor(hc[b][:, :], st[b][:, :], ct[:, b * SEQ:(b + 1) * SEQ], ALU.mult)\
                        .then_inc(hc_ready, 1)

                for n in range(UNITS):
                    unit(0, n)
                with pool.Fori(1, STEPS) as jj:
                    for n in range(UNITS):
                        unit(jj, n)
        with nc.Block() as block:
            @block.vector
            def _(dve):
                for b in range(2):
                    for h in range(2):
                        cols = slice(b * SEQ + h * BLK, b * SEQ + (h + 1) * BLK)
                        nc.vector.scalar_tensor_tensor(ssm_in[:, cols], k.hn[:, cols], k.c("Dp"), y_bank[b][h][:, :],
                                                       ALU.mult, ALU.add)


def merge_and_glu(k, attn_t, ssm_in):
    nc = k.nc
    with ExitStack() as ctx:
        x1 = k.sb("x1", [128, T], ctx=ctx)
        xf = k.sb("xf", [128, T], ctx=ctx)
        products(k, "merge", [
            ("dve", [(slice(0, 128), slice(0, BLK), k.m("Wo"), attn_t[:, sl(b)], True, False),
                     (slice(0, 128), slice(0, BLK), k.m("Wout"), ssm_in[:, sl(b)], False, True)],
             lambda p, b=b: nc.vector.scalar_tensor_tensor(x1[:, sl(b)], p, 0.5, k.hn[:, sl(b)], ALU.mult, ALU.add))
            for b in blocks(T)])
        normalise(k, "rms_f", x1, T, [(xf, k.c("norm_ffn_w"))], eps=1e-6)
        silu = [k.sb(f"silu{i}", [128, BLK], ctx=ctx) for i in range(2)]
        hid = [k.sb(f"glu_hid{i}", [128, BLK], ctx=ctx) for i in range(2)]
        up = k.sem("glu_up")
        gated = k.sem("glu_silu")
        hid_ready = k.sem("glu_hid_ready")
        down = k.sem("glu_down")
        added = k.sem("glu_added")
        res = k.sem("glu_res")
        NC = FF0 // 128
        N = NBLK * NC
        with nc.Block() as block:
            @block.tensor
            def _(pe):
                def lower(n):
                    b, c = n // NC, n % NC
                    pe.wait_ge(hid_ready, n + 1)
                    if c == 0 and b >= 2:
                        pe.wait_ge(added, b - 1)
                    nc.tensor.matmul(k.bank[4 + b % 2][:, :], k.m("W2", lo=c * 128, n=128), hid[n % 2][:, :],
                                     start=c == 0, stop=c == NC - 1).then_inc(down, 1)
                for n in range(N):
                    b, c = n // NC, n % NC
                    if n >= 2:
                        pe.wait_ge(hid_ready, n - 1)
                    nc.tensor.matmul(k.bank[n % 2][:, :], k.m("W1", lo=c * 128, n=128), xf[:, sl(b)], start=True,
                                     stop=True)
                    nc.tensor.matmul(k.bank[2 + n % 2][:, :], k.m("W1", lo=FF0 + c * 128, n=128), xf[:, sl(b)],
                                     start=True, stop=True).then_inc(up, 1)
                    if n >= 1:
                        lower(n - 1)
                lower(N - 1)

            @block.scalar
            def _(act):
                for n in range(N):
                    act.wait_ge(up, n + 1)
                    if n >= 2:
                        act.wait_ge(hid_ready, n - 1)
                    nc.scalar.activation(silu[n % 2][:, :], k.bank[n % 2][:, :], ACT.Silu).then_inc(gated, 1)

            @block.vector
            def _(dve):
                nc.vector.tensor_tensor(x1[:, :], x1[:, :], k.x[:, :], ALU.add).then_inc(res, 1)
                dve.wait_ge(res, 1)
                for n in range(N + 1):
                    if n < N:
                        dve.wait_ge(gated, n + 1)
                        if n >= 2:
                            dve.wait_ge(down, n - 1)
                        nc.vector.tensor_tensor(hid[n % 2][:, :], silu[n % 2][:, :], k.bank[2 + n % 2][:, :], ALU.mult)\
                            .then_inc(hid_ready, 1)
                    if n >= NC and n % NC == 0:
                        b = n // NC - 1
                        dve.wait_ge(down, n)
                        nc.vector.tensor_tensor(k.x[:, sl(b)], x1[:, sl(b)], k.bank[4 + b % 2][:, :], ALU.add)\
                            .then_inc(added, 1)


def one_hot_weights(k, tag, idx, wgt, ntile, wt, tmp):
    nc = k.nc
    own = k.sem(f"{tag}_own")
    with nc.Block() as block:
        @block.vector
        def _(dve):
            link = linker(dve, own)
            shape = [128, ntile, EXPERTS]
            iota = k.m("iota8").unsqueeze(1).to_broadcast(shape)
            for c in range(2):
                link(nc.vector.tensor_tensor(tmp[:, :, c, :], idx[:, :, c:c + 1].to_broadcast(shape), iota,
                                             ALU.is_equal))
                link(nc.vector.tensor_tensor(tmp[:, :, c, :], tmp[:, :, c, :],
                                             wgt[:, :, c:c + 1].to_broadcast(shape), ALU.mult))
            link(nc.vector.tensor_tensor(wt[:, :, :], tmp[:, :, 0, :], tmp[:, :, 1, :], ALU.add))


def spread_weights(k, tag, wt, ntile, dst):
    nc = k.nc
    steps = []
    per = BLK // TILE
    for e in range(EXPERTS):
        for b in range(ntile // per):
            mms = [(slice(0, 128), sl(j, TILE), wt[:, b * per + j, e:e + 1].to_broadcast([128, 128]), k.m("ident"),
                    True, True) for j in range(per)]
            if len(steps) % 2:
                steps.append(("act", mms, lambda p, e=e, b=b: nc.scalar.copy(dst[:, e, sl(b)], p)))
            else:
                steps.append(("dve", mms, lambda p, e=e, b=b: nc.vector.tensor_copy(dst[:, e, sl(b)], p)))
    products(k, tag, steps)


def experts_of_layer0(k, d):
    nc = k.nc
    NC = FF0 // 128
    with ExitStack() as ctx:
        w1 = k.sb("moe_w1", [128, EXPERTS, FF0], ctx=ctx)
        w2 = k.sb("moe_w2", [128, EXPERTS, NC, 128], ctx=ctx)
        h = k.sb("moe_h", [128, MOE_T], ctx=ctx)
        hs = k.sb("moe_hs", [128, MOE_T], ctx=ctx)
        nt = MOE_T // TILE
        idx_i = k.sb("moe_idx_i", [128, nt, 2], I32, ctx)
        idx = k.sb("moe_idx", [128, nt, 2], ctx=ctx)
        wgt = k.sb("moe_wgt", [128, nt, 2], ctx=ctx)
        tmp = k.sb("moe_tmp", [128, nt, 2, EXPERTS], ctx=ctx)
        wt = k.sb("moe_wt", [128, nt, EXPERTS], ctx=ctx)
        wbc = k.sb("moe_wbc", [128, EXPERTS, MOE_T], ctx=ctx)
        hid = [k.sb(f"moe_hid{i}", [128, MOE_T], ctx=ctx) for i in range(4)]
        part = k.sb("moe_part", [128, 2, MOE_T], ctx=ctx)
        arrived = k.sem("moe_arrived")
        small = k.sem("moe_small")
        with nc.Block() as block:
            @block.sync
            def _(sp):
                sp.dma_start(idx_i[:, :, :], d["moe_idx"]).then_inc(small, 16)
                sp.dma_start(wgt[:, :, :], d["moe_wgt"]).then_inc(small, 16)
                sp.dma_start(w1[:, :, :], d["moe_w1"]).then_inc(arrived, 16)
                sp.dma_start(w2[:, :, :, :], d["moe_w2"]).then_inc(arrived, 16)

            @block.vector
            def _(dve):
                dve.wait_ge(small, 32)
                nc.vector.tensor_copy(idx[:, :, :], idx_i[:, :, :])
        one_hot_weights(k, "moe_oh", idx, wgt, nt, wt, tmp)
        spread_weights(k, "moe_sw", wt, nt, wbc)
        normalise(k, "ln_moe", h, MOE_T, [(hs, None)], centre=k.x)
        up = k.sem("moe_up")
        act_done = k.sem("moe_act_done")
        down = k.sem("moe_down")
        expert_out = k.sem("moe_expert_out")
        taken = k.sem("moe_taken")
        summed = k.sem("moe_summed")
        N = EXPERTS * NC
        LAG = 2
        with nc.Block() as block:
            @block.tensor
            def _(pe):
                pe.wait_ge(arrived, 32)

                def lower(n):
                    e, c = n // NC, n % NC
                    pe.wait_ge(act_done, n + 1)
                    if c == 0 and e >= 2:
                        pe.wait_ge(taken, e - 1)
                    ins = nc.tensor.matmul(k.bank[4 + e % 2][:, :], w2[:, e, c, :], hid[n % 4][:, :], start=c == 0,
                                           stop=c == NC - 1).then_inc(down, 1)
                for n in range(N):
                    e, c = n // NC, n % NC
                    if n >= 4:
                        pe.wait_ge(act_done, n - 3)
                    nc.tensor.matmul(k.bank[n % 4][:, :], w1[:, e, sl(c, 128)], hs[:, :], start=True, stop=True)\
                        .then_inc(up, 1)
                    if n >= LAG:
                        lower(n - LAG)
                for n in range(N - LAG, N):
                    lower(n)

            @block.scalar
            def _(act):
                for n in range(N):
                    act.wait_ge(up, n + 1)
                    if n >= 4:
                        act.wait_ge(down, n - 3)
                    nc.scalar.activation(hid[n % 4][:, :], k.bank[n % 4][:, :], ACT.Gelu).then_inc(act_done, 1)

            @block.vector
            def _(dve):
                nc.vector.tensor_scalar_add(k.x[:, :], k.x[:, :], k.c("moe_bias")).then_inc(summed, 1)
                for e in range(EXPERTS):
                    dve.wait_ge(down, NC * (e + 1))
                    dve.wait_ge(summed, max(e - 1, 0) + 1)
                    nc.vector.tensor_tensor(part[:, e % 2, :], wbc[:, e, :], k.bank[4 + e % 2][:, :], ALU.mult)\
                        .then_inc(taken, 1)
                    dve.wait_ge(taken, e + 1)
                    dve.wait_ge(summed, e + 1)
                    nc.vector.tensor_tensor(k.x[:, 0:MOE_T], k.x[:, 0:MOE_T], part[:, e % 2, :], ALU.add)\
                        .then_inc(summed, 1)


def latent_attention(k, d):
    nc = k.nc
    with ExitStack() as ctx:
        v_aug = k.sb("v_aug1", [128, NT, HEADS, 32], ctx=ctx)
        attn_t = k.sb("attn_t1", [128, T], ctx=ctx)
        cleared = k.sem("v1_cleared")
        with nc.Block() as block:
            @block.gpsimd
            def _(pool):
                nc.gpsimd.memset(v_aug[:, :, :, :], 0.0).then_inc(cleared, 1)
                pool.wait_ge(cleared, 1)
                nc.gpsimd.memset(v_aug[:, :, :, HD:HD + 1], 1.0)
        with ExitStack() as pre:
            hc = k.sb("lat_hc", [128, T], ctx=pre)
            normalise(k, "ln_lat", hc, T, [(k.hn, None)], centre=k.x)
        with ExitStack() as pre:
            ckv = k.sb("ckv", [32, T], ctx=pre)
            zq = k.sb("zq", [32, T], ctx=pre)
            qf = k.sb("qf1", [128, T], ctx=pre)
            kf = k.sb("kf1", [128, T], ctx=pre)
            tmp = k.sb("ltmp", [128, T], ctx=pre)
            m1 = k.sb("m1", [128, 128], ctx=pre)
            keff = k.sb("keff", [32, 128], ctx=pre)
            veff = k.sb("veff", [32, 128], ctx=pre)
            parts = [k.sb(f"lparts{i}", [128, T], BF16, pre) for i in range(3)]
            rows32, cols128 = slice(0, 32), slice(0, 128)
            steps = [("dve", one(k.m("W_uqT", 32), k.m("W_dq", 32), cols=cols128),
                      lambda p: nc.vector.tensor_copy(m1[:, :], p[:, 0:128])),
                     ("dve", one(k.m("W_uv"), k.m("W_oT"), rows=rows32, cols=cols128),
                      lambda p: nc.vector.tensor_copy(veff[:, :], p[0:32, 0:128]))]
            for b in blocks(T):
                steps += [("act", one(k.m("W_dkvT"), k.hn[:, sl(b)], rows=rows32),
                           lambda p, b=b: nc.scalar.copy(ckv[:, sl(b)], p[0:32, :])),
                          ("dve", one(k.m("W_dqT"), k.hn[:, sl(b)], rows=rows32),
                           lambda p, b=b: nc.vector.tensor_copy(zq[:, sl(b)], p[0:32, :]))]
            products(k, "lat_p1", steps)
            products(k, "lat_p2", [("dve", one(k.m("W_uk"), m1[:, :], rows=rows32, cols=cols128),
                                    lambda p: nc.vector.tensor_copy(keff[:, :], p[0:32, 0:128]))])
            steps = []
            for b in blocks(T):
                steps += [("act", one(k.m("W_uqT", 32), zq[:, sl(b)]), lambda p, b=b: nc.scalar.copy(qf[:, sl(b)], p)),
                          ("dve", one(keff[:, :], ckv[:, sl(b)]),
                           lambda p, b=b: nc.vector.tensor_copy(kf[:, sl(b)], p)),
                          ("act", [(slice(0, 128), sl(j, TILE), ckv[:, sl(4 * b + j, TILE)], veff[:, :], True, True)
                                   for j in range(4)],
                           lambda p, b=b: nc.scalar.copy(v_aug[:, 4 * b:4 * b + 4, :, 0:HD].rearrange("p t h d -> p (t h) d"),
                                                         p.rearrange("p (a d) -> p a d", d=HD)))]
            products(k, "lat_p3", steps)
            split3(k, "split_q1", qf, parts, tmp, T, send_linear(k, d["q_lin"], parts))
            split3(k, "split_k1", kf, parts, tmp, T, send_linear(k, d["k_lin"], parts))
            replicate_terms(k, "rep_q1", d["q_lin"], d["q_full"], Q_ORDER)
            replicate_terms(k, "rep_k1", d["k_lin"], d["k_full"], K_ORDER)
        attention(k, "attn1", d["q_full"], d["k_full"], HEADS, v_aug, True, attn_t)
        with nc.Block() as block:
            @block.vector
            def _(dve):
                nc.vector.tensor_tensor(k.x[:, :], k.x[:, :], attn_t[:, :], ALU.add)


def experts_of_layer1(k, d, y):
    nc = k.nc
    FB = 256
    NB = T // FB
    S = EXPERTS + 1
    xi = k.hn
    with ExitStack() as ctx:
        w9 = k.sb("w9", [128, S, T], ctx=ctx)
        w2p = k.sb("ew2_pad", [128, EXPERTS, 3 * D], ctx=ctx)
        eb2h = k.sb("eb2_half", [128, 3 * S], ctx=ctx)
        hb2 = k.sb("hb2_half", [128, 1], ctx=ctx)
        arrived = k.sem("ew2_arrived")
        with nc.Block() as block:
            @block.sync
            def _(sp):
                sp.dma_start(w2p[:, :, :], d["ew2_pad"]).then_inc(arrived, 16)

            @block.vector
            def _(dve):
                o = CI["eb2_0_0"]
                nc.vector.tensor_scalar_mul(eb2h[:, 0:24], k.cols[:, o:o + 24], 0.5)
                o = CI["b_s2_0"]
                nc.vector.tensor_scalar_mul(eb2h[:, 24:27], k.cols[:, o:o + 3], 0.5)
                nc.vector.tensor_scalar_mul(hb2[:, :], k.c("b_h2"), 0.5)
        with ExitStack() as pre:
            hc = k.sb("ffn_hc", [128, T], ctx=pre)
            normalise(k, "ln_ffn", hc, T, [(xi, None)], centre=k.x)
        with ExitStack() as pre:
            route(k, pre, w9)
        with ExitStack() as pre:
            refine(k, pre, xi, w9, w2p, eb2h, hb2, arrived, FB, NB, S)
        with nc.Block() as block:
            done = k.sem("y_done")
            sent = k.sem("y_sent")

            @block.vector
            def _(dve):
                for b in blocks(T):
                    nc.vector.tensor_tensor(k.x[:, sl(b)], k.x[:, sl(b)], xi[:, sl(b)], ALU.add).then_inc(done, 1)

            @block.sync
            def _(sp):
                for b in blocks(T):
                    sp.wait_ge(done, b + 1)
                    sp.dma_start(y[:, sl(b)], k.x[:, sl(b)]).then_inc(sent, 16)
                sp.wait_ge(sent, 16 * NBLK)


def route(k, ctx, w9):
    nc = k.nc
    g1 = k.sb("route_g1", [32, T], ctx=ctx)
    lg = k.sb("route_logits", [128, NT, EXPERTS], ctx=ctx)
    t8 = k.sb("route_t8", [128, NT, EXPERTS], ctx=ctx)
    best = k.sb("route_best", [128, NT, 2], ctx=ctx)
    idx = k.sb("route_idx", [128, NT, 2], ctx=ctx)
    prob = k.sb("route_prob", [128, NT, 2], ctx=ctx)
    tmp = k.sb("route_tmp", [128, NT, 2, EXPERTS], ctx=ctx)
    wt = k.sb("route_wt", [128, NT, EXPERTS], ctx=ctx)
    sw = k.sb("route_sw", [128, 2], ctx=ctx)
    own = k.sem("route_own")
    steps = [("act", one(k.m("w_r1"), k.hn[:, sl(b)], rows=slice(0, 32)),
              lambda p, b=b: nc.scalar.activation(g1[:, sl(b)], p[0:32, :], ACT.Gelu, bias=k.c("b_r1", 32)))
             for b in blocks(T)]
    products(k, "route_p1", steps)
    b_r2 = k.m("b_r2").unsqueeze(1).to_broadcast([128, NT, EXPERTS])
    products(k, "route_p2", [
        ("dve", [(slice(0, 128), sl(t, EXPERTS), g1[:, sl(t, TILE)], k.m("w_r2", 32), True, True) for t in range(NT)],
         lambda p: nc.vector.tensor_tensor(lg[:, :, :], b_r2,
                                           p[:, 0:NT * EXPERTS].rearrange("p (t e) -> p t e", e=EXPERTS), ALU.add))])
    exps = k.sem("route_exps")
    diff = k.sem("route_diff")
    with nc.Block() as block:
        @block.vector
        def _(dve):
            link = linker(dve, own)
            shape = [128, NT, EXPERTS]
            iota = k.m("iota8").unsqueeze(1).to_broadcast(shape)
            for c in range(2):
                link(nc.vector.tensor_reduce(best[:, :, c], lg[:, :, :], AX.X, ALU.max))
                link(nc.vector.tensor_tensor(t8[:, :, :], lg[:, :, :], best[:, :, c:c + 1].to_broadcast(shape),
                                             ALU.is_lt))
                link(nc.vector.scalar_tensor_tensor(t8[:, :, :], t8[:, :, :], 8.0, iota, ALU.mult, ALU.add))
                link(nc.vector.tensor_reduce(idx[:, :, c], t8[:, :, :], AX.X, ALU.min))
                if c == 0:
                    link(nc.vector.tensor_tensor(t8[:, :, :], idx[:, :, 0:1].to_broadcast(shape), iota, ALU.is_equal))
                    link(nc.vector.scalar_tensor_tensor(lg[:, :, :], t8[:, :, :], -BIG, lg[:, :, :], ALU.mult,
                                                        ALU.add))
            nc.vector.tensor_tensor(best[:, :, 1], best[:, :, 1], best[:, :, 0], ALU.subtract).then_inc(diff, 1)
            dve.wait_ge(exps, 2)
            link(nc.vector.tensor_scalar_add(prob[:, :, 1], best[:, :, 1], 1.0))
            link(nc.vector.reciprocal(prob[:, :, 0], prob[:, :, 1]))
            link(nc.vector.tensor_tensor(prob[:, :, 1], best[:, :, 1], prob[:, :, 0], ALU.mult))
            link(nc.vector.tensor_scalar(sw[:, 1:2], sw[:, 0:1], -1.0, 1.0, ALU.mult, ALU.add))
            link(nc.vector.tensor_scalar_mul(prob[:, :, :], prob[:, :, :], sw[:, 1:2]))

        @block.scalar
        def _(act):
            nc.scalar.activation(sw[:, 0:1], k.c("shared_weight"), ACT.Sigmoid).then_inc(exps, 1)
            act.wait_ge(diff, 1)
            nc.scalar.activation(best[:, :, 1], best[:, :, 1], ACT.Exp).then_inc(exps, 1)
    one_hot_weights(k, "route_oh", idx, prob, NT, wt, tmp)
    spread_weights(k, "route_sw", wt, NT, w9)
    with nc.Block() as block:
        @block.vector
        def _(dve):
            nc.vector.memset(w9[:, EXPERTS, :], 1.0).then_inc(own, 1)
            dve.wait_ge(own, 16)
            nc.vector.tensor_scalar_mul(w9[:, EXPERTS, :], w9[:, EXPERTS, :], sw[:, 0:1])


def refine(k, ctx, xi, w9, w2p, eb2h, hb2, arrived, FB, NB, S):
    nc = k.nc
    v = k.sb("vel", [128, T], ctx=ctx)
    hid = [k.sb(f"hid{i}", [128, 5, FB], ctx=ctx) for i in range(2)]
    beta = [k.sb(f"beta{i}", [128, S, FB], ctx=ctx) for i in range(2)]
    gate = [k.sb(f"gate{i}", [128, S, FB], ctx=ctx) for i in range(2)]
    alpha = k.sb("alpha", [128, S, FB], ctx=ctx)
    err = k.sb("err", [128, FB], ctx=ctx)
    sum_g = k.sb("sum_g", [128, FB], ctx=ctx)
    sum_b = k.sb("sum_b", [128, FB], ctx=ctx)
    xn = [k.sb(f"x_next{i}", [128, FB], ctx=ctx) for i in range(2)]
    hh = k.sb("halt_hid", [32, FB], ctx=ctx)
    fh = k.sb("ref_hid", [128, 2, FB], ctx=ctx)
    halt = k.sb("halt", [128, FB], ctx=ctx)
    ref = k.sb("refined", [128, FB], ctx=ctx)

    hid_scored = k.sem("hid_scored")
    hid_ready = k.sem("hid_ready")
    gate_made = k.sem("gate_made")
    beta_made = k.sem("beta_made")
    alpha_made = k.sem("alpha_made")
    gate_ready = k.sem("gate_ready")
    alpha_ready = k.sem("alpha_ready")
    beta_raw = k.sem("beta_raw")
    clipped = k.sem("beta_clipped")
    exped = k.sem("beta_exped")
    logged = k.sem("beta_logged")
    beta_ready = k.sem("beta_ready")
    err_ready = k.sem("err_ready")
    weighted = k.sem("weighted")
    pushed = k.sem("pushed")
    mixed = k.sem("mixed")
    xn_ready = k.sem("xn_ready")
    unit_done = k.sem("unit_done")
    halt_scored = k.sem("halt_scored")
    halt_hid = k.sem("halt_hid_ready")
    halt_ready = k.sem("halt_ready")
    refined = k.sem("refined_ready")
    xi_ready = k.sem("xi_ready")
    own_dve = k.sem("refine_own_dve")
    raw = k.sb("beta_raw", [128, S, FB], ctx=ctx)

    half = "p (c f) -> p c f"
    pairs_bank = [k.bank[p].rearrange(half, f=FB) for p in range(2)]
    shared_bank = k.bank[2][:, 0:FB]
    halt_hid_bank = k.bank[2][0:32, FB:2 * FB]
    gate_bank = k.bank[3].rearrange(half, f=FB)
    beta_bank = k.bank[4].rearrange(half, f=FB)
    alpha_bank = k.bank[5].rearrange(half, f=FB)
    f1_bank = k.bank[6].rearrange(half, f=FB)
    halt_bank = k.bank[6][:, 0:FB]
    ref_bank = k.bank[7][:, 0:FB]
    PAIRS = (S + 1) // 2

    def slots(q):
        return [e for e in (2 * q, 2 * q + 1) if e < S]

    def weights(e, comp):
        if e == EXPERTS:
            return k.m("w_s2", EH, lo=comp * D, n=D)
        return w2p[:, e, comp * D:(comp + 1) * D]

    def bias(e, comp):
        return k.c(f"b_s2_{comp}") if e == EXPERTS else k.c(f"eb2_{e}_{comp}")

    def half_bias(e, comp):
        return eb2h[:, 3 * e + comp:3 * e + comp + 1]

    def each(eng, body, end):
        body(False, 0, 0, 0)
        body(False, 0, 1, 1)
        with eng.Fori(1, NB // 2) as i:
            for par in range(2):
                body(False, i, par, 2 * i + par)
        body(True, 0, 0, NB)
        body(True, 0, 1, NB + 1)
        with eng.Fori(1, NB // 2) as i:
            for par in range(2):
                body(True, i, par, 2 * i + par + NB)
        end(2 * NB - 1)

    def cols(i, par):
        if isinstance(i, int):
            return slice((2 * i + par) * FB, (2 * i + par + 1) * FB)
        return bass.ds((2 * i + par) * FB, FB)

    with nc.Block() as block:
        @block.tensor
        def _(pe):
            def halting(u, par):
                pe.wait_ge(xn_ready, u + 1)
                nc.tensor.matmul(halt_hid_bank, k.m("w_h1"), xn[par][:, :], start=True, stop=True)
                for c in range(2):
                    last = nc.tensor.matmul(f1_bank[:, c, :], k.m("w_f1", lo=c * 128, n=128), xn[par][:, :],
                                            start=True, stop=True)
                last.then_inc(halt_scored, 1)
                pe.wait_ge(halt_hid, 3 * u + 3)
                pe.wait_ge(xi_ready, u)
                nc.tensor.matmul(halt_bank, k.m("w_h2", 32).to_broadcast([32, 128]), hh[:, :], start=True, stop=True)
                for c in range(2):
                    last = nc.tensor.matmul(ref_bank, k.m("w_f2", lo=c * 128, n=128), fh[:, c, :], start=c == 0,
                                            stop=c == 1)
                last.then_inc(halt_scored, 1)

            def body(second, i, par, u):
                cc = cols(i, par)
                pe.wait_ge(hid_ready, 5 * u)
                if second:
                    pe.wait_ge(xi_ready, u - NB + 1)
                for p in range(5):
                    if p < 4:
                        out, lx, lv = pairs_bank[p // 2][:, p % 2, :], k.m("ew1", lo=p * 128, n=128), \
                            k.m("ew1", lo=512 + p * 128, n=128)
                    else:
                        out, lx, lv = shared_bank[0:EH, :], k.m("w_s1", lo=0, n=EH), k.m("w_s1", lo=EH, n=EH)
                    ins = nc.tensor.matmul(out, lx, xi[:, cc], start=True, stop=not second)
                    if second:
                        ins = nc.tensor.matmul(out, lv, v[:, cc], start=False, stop=True)
                    if p in (1, 3, 4):
                        ins.then_inc(hid_scored, 1)
                for q in range(PAIRS):
                    pe.wait_ge(hid_ready, 5 * u + q + 1)
                    read = S * u + 2 * q
                    for comp, bank, free, value, made in (
                            (2, gate_bank, gate_ready, read, gate_made), (1, beta_bank, beta_raw, read, beta_made),
                            (0, alpha_bank, alpha_ready, read - S * NB, alpha_made))[:3 if second else 2]:
                        pe.wait_ge(free, value)
                        for e in slots(q):
                            h = hid[par][:, e // 2, :] if e < EXPERTS else hid[par][0:EH, 4, :]
                            last = nc.tensor.matmul(bank[:, e % 2, :], weights(e, comp), h, start=True, stop=True)
                        last.then_inc(made, 1)
                if not (isinstance(u, int) and u == 0):
                    halting(u - 1, 1 - par)

            pe.wait_ge(arrived, 16)
            each(pe, body, lambda u: halting(u, 1))

        @block.scalar
        def _(act):
            def halting(u, par):
                act.wait_ge(halt_scored, 2 * u + 1)
                nc.scalar.activation(hh[:, :], halt_hid_bank, ACT.Gelu, bias=k.c("b_h1", 32)).then_inc(halt_hid, 1)
                for c in range(2):
                    nc.scalar.activation(fh[:, c, :], f1_bank[:, c, :], ACT.Gelu, bias=k.c(f"b_f1_{c}"))\
                        .then_inc(halt_hid, 1)
                act.wait_ge(halt_scored, 2 * u + 2)
                act.wait_ge(xi_ready, u)
                nc.scalar.activation(halt[:, :], halt_bank, ACT.Tanh, bias=hb2[:, :], scale=0.5).then_inc(halt_ready, 1)

            def body(second, i, par, u):
                for p in range(5):
                    act.wait_ge(hid_scored, 3 * u + p // 2 + 1)
                    act.wait_ge(beta_made, PAIRS * u)
                    if second:
                        act.wait_ge(alpha_made, PAIRS * (u - NB))
                    if p < 4:
                        nc.scalar.activation(hid[par][:, p, :], pairs_bank[p // 2][:, p % 2, :], ACT.Gelu,
                                             bias=k.c(f"eb1_{p}")).then_inc(hid_ready, 1)
                    else:
                        nc.scalar.activation(hid[par][0:EH, 4, :], shared_bank[0:EH, :], ACT.Gelu,
                                             bias=k.c("b_s1", EH)).then_inc(hid_ready, 1)
                act.wait_ge(unit_done, u - 1 if not isinstance(u, int) or u > 0 else 0)
                if second:
                    act.wait_ge(unit_done, u)
                for q in range(PAIRS):
                    act.wait_ge(gate_made, PAIRS * u + q + 1)
                    for e in slots(q):
                        nc.scalar.activation(gate[par][:, e, :], gate_bank[:, e % 2, :], ACT.Tanh,
                                             bias=half_bias(e, 2), scale=0.5).then_inc(gate_ready, 1)
                    if second:
                        act.wait_ge(alpha_made, PAIRS * (u - NB) + q + 1)
                        for e in slots(q):
                            nc.scalar.activation(alpha[:, e, :], alpha_bank[:, e % 2, :], ACT.Tanh,
                                                 bias=half_bias(e, 0), scale=0.5).then_inc(alpha_ready, 1)
                if not (isinstance(u, int) and u == 0):
                    halting(u - 1, 1 - par)
                act.wait_ge(clipped, u + 1)
                nc.scalar.activation(beta[par][:, :, :], beta[par][:, :, :], ACT.Exp).then_inc(exped, 1)
                act.wait_ge(exped, u + 1)
                nc.scalar.activation(beta[par][:, :, :], beta[par][:, :, :], ACT.Ln, bias=1.0).then_inc(logged, 1)

            each(act, body, lambda u: halting(u, 1))

        @block.gpsimd
        def _(pool):
            def body(second, i, par, u):
                cc = cols(i, par)
                if not second:
                    pool.wait_ge(beta_ready, u + 1)
                    nc.gpsimd.tensor_tensor(beta[par][:, :, :], beta[par][:, :, :], w9[:, :, cc], ALU.mult)\
                        .then_inc(weighted, 1)
                else:
                    pool.wait_ge(beta_ready, u + 1)
                    pool.wait_ge(err_ready, u + 1)
                    nc.gpsimd.tensor_tensor(beta[par][:, :, :], beta[par][:, :, :],
                                            err[:, :].unsqueeze(1).to_broadcast([128, S, FB]), ALU.mult)\
                        .then_inc(pushed, 1)
                    pool.wait_ge(mixed, u - NB + 1)
                    nc.gpsimd.tensor_tensor(alpha[:, :, :], alpha[:, :, :], w9[:, :, cc], ALU.mult)\
                        .then_inc(weighted, 1)
            each(pool, body, lambda u: None)

        @block.vector
        def _(dve):
            def halting(u, i, par):
                cc = cols(i, par)
                dve.wait_ge(halt_scored, 2 * u + 2)
                nc.vector.tensor_scalar(ref[:, :], ref_bank, k.c("b_f2"), k.c("iw"), ALU.add, ALU.mult)\
                    .then_inc(refined, 1)
                dve.wait_ge(refined, 2 * u + 1)
                dve.wait_ge(halt_ready, u + 1)
                nc.vector.scalar_tensor_tensor(ref[:, :], halt[:, :], 1.0, ref[:, :], ALU.add, ALU.mult)\
                    .then_inc(refined, 1)
                dve.wait_ge(refined, 2 * u + 2)
                nc.vector.scalar_tensor_tensor(xi[:, cc], ref[:, :], 0.5, xi[:, cc], ALU.mult, ALU.add)\
                    .then_inc(xi_ready, 1)
                dve.wait_ge(xi_ready, u + 1)

            def previous(i, par):
                if par:
                    return i, 0
                return (NB // 2 - 1 if isinstance(i, int) and i == 0 else i - 1), 1

            def body(second, i, par, u):
                cc = cols(i, par)
                dve.wait_ge(unit_done, u)
                nc.vector.tensor_scalar_sub(err[:, :], xi[:, cc], k.c("mu")).then_inc(err_ready, 1)
                for e in range(S):
                    dve.wait_ge(beta_made, PAIRS * u + e // 2 + 1)
                    nc.vector.tensor_scalar_add(raw[:, e, :], beta_bank[:, e % 2, :], bias(e, 1)).then_inc(beta_raw, 1)
                dve.wait_ge(beta_raw, S * (u + 1))
                nc.vector.tensor_scalar_min(beta[par][:, :, :], raw[:, :, :], 40.0).then_inc(clipped, 1)
                if not (isinstance(u, int) and u == 0):
                    halting(u - 1, *previous(i, par))
                if second:
                    dve.wait_ge(alpha_ready, S * (u - NB + 1))
                    link(nc.vector.scalar_tensor_tensor(alpha[:, :, :], alpha[:, :, :], 1.0,
                                                        v[:, cc].unsqueeze(1).to_broadcast([128, S, FB]),
                                                        ALU.add, ALU.mult), own_base(second, u) + 1)
                dve.wait_ge(logged, u + 1)
                nc.vector.tensor_tensor(beta[par][:, :, :], beta[par][:, :, :], raw[:, :, :], ALU.max)\
                    .then_inc(beta_ready, 1)
                dve.wait_ge(gate_ready, S * (u + 1))
                if not second:
                    dve.wait_ge(weighted, u + 1)
                    base = own_base(second, u)
                    link(nc.vector.scalar_tensor_tensor(gate[par][:, :, :], gate[par][:, :, :], 1.0,
                                                        beta[par][:, :, :], ALU.add, ALU.mult), base + 1)
                    link(nc.vector.tensor_reduce(sum_g[:, :], gate[par][:, :, :].rearrange("p e f -> p f e"), AX.X,
                                                 ALU.add), base + 2)
                    link(nc.vector.tensor_reduce(sum_b[:, :], beta[par][:, :, :].rearrange("p e f -> p f e"), AX.X,
                                                 ALU.add), base + 3)
                    link(nc.vector.tensor_tensor(sum_g[:, :], sum_g[:, :], err[:, :], ALU.mult), base + 4)
                    link(nc.vector.scalar_tensor_tensor(v[:, cc], sum_b[:, :], -1.0, err[:, :], ALU.mult, ALU.mult),
                         base + 5)
                    nc.vector.scalar_tensor_tensor(xn[par][:, :], sum_g[:, :], -0.05, xi[:, cc], ALU.mult, ALU.add)\
                        .then_inc(xn_ready, 1)
                else:
                    base = own_base(second, u)
                    dve.wait_ge(pushed, u - NB + 1)
                    nc.vector.scalar_tensor_tensor(alpha[:, :, :], alpha[:, :, :], 0.5, beta[par][:, :, :], ALU.mult,
                                                   ALU.subtract).then_inc(mixed, 1)
                    dve.wait_ge(weighted, u + 1)
                    link(nc.vector.scalar_tensor_tensor(gate[par][:, :, :], gate[par][:, :, :], 1.0, alpha[:, :, :],
                                                        ALU.add, ALU.mult), base + 2)
                    link(nc.vector.tensor_reduce(sum_g[:, :], gate[par][:, :, :].rearrange("p e f -> p f e"), AX.X,
                                                 ALU.add), base + 3)
                    nc.vector.scalar_tensor_tensor(xn[par][:, :], sum_g[:, :], 0.05, xi[:, cc], ALU.mult, ALU.add)\
                        .then_inc(xn_ready, 1)
                dve.wait_ge(xn_ready, u + 1)
                dve.sem_inc(unit_done, 1)

            def own_base(second, u):
                return 5 * u if not second else 5 * NB + 3 * (u - NB)

            def link(ins, value):
                ins.then_inc(own_dve, 1)
                dve.wait_ge(own_dve, value)

            each(dve, body, lambda u: halting(u, NB // 2 - 1, 1))


def build_program(nc, d, y, upto=4):
    with ExitStack() as ctx:
        k = Core(nc, ctx)
        scratch = {}
        for name, rows in (("q", HEADS), ("k", HEADS)):
            scratch[f"{name}_lin"] = nc.dram_tensor(f"{name}_lin", [3, rows * HD, T], BF16, kind="Internal").ap()
            scratch[f"{name}_full"] = nc.dram_tensor(f"{name}_full", [9 * HD, rows, T], BF16, kind="Internal").ap()
        d = {**d, **scratch}
        arrived = k.sem("inputs_arrived")
        with nc.Block() as block:
            @block.sync
            def _(sp):
                sp.dma_start(k.x[:, :], d["x"]).then_inc(arrived, 16)
                sp.dma_start(k.mats[:, :], d["mats"]).then_inc(arrived, 16)
                sp.dma_start(k.cols[:, :], d["cols"]).then_inc(arrived, 16)
                sp.wait_ge(arrived, 48)
        with ExitStack() as layer:
            hc = k.sb("ln0_c", [128, T], ctx=layer)
            normalise(k, "ln0", hc, T, [(k.hn, None)], centre=k.x)
        with ExitStack() as layer:
            attn_t = k.sb("attn_t", [128, T], ctx=layer)
            ssm_in = k.sb("ssm_in", [128, T], ctx=layer)
            with k.scope():
                hybrid_attention(k, d, d["rope_q"], d["rope_k"], attn_t)
            with k.scope():
                state_space(k, ssm_in)
            with k.scope():
                merge_and_glu(k, attn_t, ssm_in)
        if upto >= 2:
            with k.scope():
                experts_of_layer0(k, d)
        if upto >= 3:
            with k.scope():
                latent_attention(k, d)
        if upto >= 4:
            with k.scope():
                experts_of_layer1(k, d, y)
        else:
            with nc.Block() as block:
                @block.sync
                def _(sp):
                    sp.dma_start(y, k.x[:, :]).then_inc(arrived, 16)
                    sp.wait_ge(arrived, 64)


def constants():
    i = np.arange(128)
    m = {"ident": np.eye(128), "center": np.eye(128) - 1.0 / D,
         "mean8": (i[:, None] // HD == np.arange(16)[None]) / float(HD), "mean128": np.full((128, 1), 1.0 / D),
         "eye96": i[:, None] % 32 == np.arange(32)[None], "iota8": np.tile(np.arange(8.0), (128, 1)),
         "mask_kq": np.where(i[:, None] > i[None], -BIG, 0.0), "mask_qk": np.where(i[None] > i[:, None], -BIG, 0.0)}
    rot = np.zeros((128, 128))
    for r in range(128):
        if r % HD < HD // 2:
            rot[r + HD // 2, r] = -1.0
        else:
            rot[r - HD // 2, r] = 1.0
    m["rot"] = rot
    inv_freq = (np.float32(1.0) / np.float32(10000.0) ** (np.arange(0, HD, 2, dtype=np.float32) / np.float32(HD)))
    ang = np.arange(SEQ, dtype=np.float32)[None] * inv_freq.astype(np.float32)[i % 4][:, None]
    rope_q = np.stack([np.cos(ang), np.sin(ang)], 1).astype(np.float32)
    rope_k = np.stack([rope_q[32 * c:32 * c + 32, :, (c % 2) * BLK:(c % 2 + 1) * BLK] for c in range(4)], 0)
    return {n: v.astype(np.float32) for n, v in m.items()}, rope_q, rope_k.reshape(128, 2, BLK)


def lay_out(inp):
    a = {n: np.asarray(v) for n, v in inp.items()}
    h = {n[8:]: v for n, v in a.items() if n.startswith("L0_attn_")}
    e = {n[7:]: v for n, v in a.items() if n.startswith("L0_ffn_")}
    l = {n[8:]: v for n, v in a.items() if n.startswith("L1_attn_")}
    f = {n[7:]: v for n, v in a.items() if n.startswith("L1_ffn_")}
    m, rope_q, rope_k = constants()
    for n in ("Wq", "Wk", "Wv", "Wo", "Wx", "Wdt", "Wsel", "Wimp", "Wg", "Wout", "W1"):
        m[n] = h[n]
    m["W2"] = h["W2"].reshape(4, 128, 128).transpose(1, 0, 2).reshape(128, 512)
    m["A_log"] = h["A_log"].T
    m.update({"W_dqT": l["W_dq"].T, "W_dkvT": l["W_dkv"].T, "W_dq": l["W_dq"], "W_uqT": l["W_uq"].T,
              "W_uk": l["W_uk"], "W_uv": l["W_uv"], "W_oT": l["W_o"].T})
    m.update({"w_r1": f["w_r1"], "w_r2": f["w_r2"], "b_r2": np.tile(f["b_r2"], (128, 1)), "w_h1": f["w_h1"],
              "w_h2": f["w_h2"], "w_s1": np.concatenate([f["w_s1"][:D], f["w_s1"][D:]], 1), "w_s2": f["w_s2"],
              "w_f1": f["w_f1"], "w_f2": np.concatenate([f["w_f2"][:128], f["w_f2"][128:]], 1),
              "ew1": f["expert_w1"].reshape(EXPERTS, 2, D, EH).transpose(2, 1, 0, 3).reshape(D, 2 * EXPERTS * EH)})
    mats = np.zeros((128, MTOT), np.float32)
    for n, w in MATS.items():
        mats[:m[n].shape[0], MOFF[n]:MOFF[n] + w] = m[n]
    cols = np.zeros((128, len(COLS)), np.float32)

    def put(name, v):
        cols[:len(v), CI[name]] = v
    for n in ("norm_attn_w", "ssm_norm_w", "bdt", "Dp", "bsel", "sel_gate", "bimp", "bg", "norm_ffn_w"):
        put(n, h[n])
    put("qn", np.tile(h["qn_w"], 16))
    put("kn", np.tile(h["kn_w"], 16))
    put("moe_bias", e["bias"])
    put("b_r1", f["b_r1"])
    put("b_h1", f["b_h1"])
    put("b_f1_0", f["b_f1"][:128])
    put("b_f1_1", f["b_f1"][128:])
    put("b_f2", f["b_f2"])
    put("iw", f["integration_weight"])
    put("mu", f["mu"])
    put("b_h2", np.tile(f["b_h2"], 128))
    put("shared_weight", np.tile(f["shared_weight"].reshape(1), 128))
    put("b_s1", f["b_s1"])
    for c in range(3):
        put(f"b_s2_{c}", f["b_s2"][c * D:(c + 1) * D])
    for p in range(4):
        put(f"eb1_{p}", f["expert_b1"][2 * p:2 * p + 2].reshape(128))
    for x in range(EXPERTS):
        for c in range(3):
            put(f"eb2_{x}_{c}", f["expert_b2"][x, c * D:(c + 1) * D])
    ew2 = np.zeros((128, EXPERTS, 3 * D), np.float32)
    for x in range(EXPERTS):
        ew2[EH * (x % 2):EH * (x % 2) + EH, x] = f["expert_w2"][x]
    nt = MOE_T // TILE
    return {
        "x": h["x"].reshape(T, D).T, "mats": mats, "cols": cols, "rope_q": rope_q, "rope_k": rope_k,
        "moe_w1": e["w1"].transpose(1, 0, 2), "moe_w2": e["w2"].reshape(EXPERTS, FF0 // 128, 128, D).transpose(2, 0, 1, 3),
        "moe_idx": e["expert_indices"].astype(np.int32).reshape(nt, TILE, 2).transpose(1, 0, 2),
        "moe_wgt": e["expert_weights"].reshape(nt, TILE, 2).transpose(1, 0, 2), "ew2_pad": ew2}


def kernel(**inputs):
    import concourse.bacc as bacc
    from concourse.bass_utils import run_bass_kernel_spmd

    nc = bacc.Bacc("TRN2", target_bir_lowering=False, num_devices=1)
    arrays, d = {}, {}
    for name, value in lay_out(inputs).items():
        value = np.ascontiguousarray(value)
        arrays[f"in_{name}"] = value
        d[name] = nc.dram_tensor(f"in_{name}", value.shape, mybir.dt.from_np(value.dtype), kind="ExternalInput").ap()
    y = nc.dram_tensor("out_y", [D, T], F32, kind="ExternalOutput").ap()
    build_program(nc, d, y)
    r = run_bass_kernel_spmd(nc, [arrays], core_ids=[0])
    return r.results[0]["out_y"].T.reshape(BATCH, SEQ, D).copy()
```

```python
import numpy as np
import concourse.bass as bass
from concourse import mybir
from contextlib import ExitStack, contextmanager

F32 = mybir.dt.float32
BF16 = mybir.dt.bfloat16
I32 = mybir.dt.int32
ALU = mybir.AluOpType
ACT = mybir.ActivationFunctionType
AX = mybir.AxisListType

D = 128
BATCH, SEQ = 2, 1024
T = BATCH * SEQ
BLK = 512
NBLK = T // BLK
TILE = 128
NT = T // TILE
HEADS, KV, HD = 16, 4, 8
GROUPS = 4
N_STATE = 128
R_DT = 64
FF0 = 512
EXPERTS = 8
MOE_T = 512
EH = 64
BIG = 1.0e30

COLS = ["norm_attn_w", "ssm_norm_w", "bdt", "Dp", "bsel", "sel_gate", "bimp", "bg", "norm_ffn_w", "qn", "kn",
        "moe_bias", "b_r1", "b_h1", "b_f1_0", "b_f1_1", "b_f2", "iw", "mu", "b_h2", "shared_weight", "b_s1",
        "b_s2_0", "b_s2_1", "b_s2_2"] + [f"eb1_{p}" for p in range(4)] + [f"eb2_{e}_{c}" for e in range(8) for c in range(3)]
CI = {n: i for i, n in enumerate(COLS)}

MATS = {"ident": 128, "center": 128, "rot": 128, "mean8": 16, "mean128": 1, "eye96": 32, "iota8": 8,
        "mask_kq": 128, "mask_qk": 128,
        "Wq": 128, "Wk": 32, "Wv": 32, "Wo": 128, "Wx": R_DT + 2 * N_STATE, "Wdt": 128, "Wsel": 128, "Wimp": 128,
        "Wg": 128, "Wout": 128, "W1": 1024, "W2": 512, "A_log": 128,
        "W_dqT": 32, "W_dkvT": 32, "W_dq": 128, "W_uqT": 128, "W_uk": 32, "W_uv": 32, "W_oT": 128,
        "w_r1": 32, "w_r2": 8, "b_r2": 8, "w_h1": 32, "w_h2": 1, "w_s1": 128, "w_s2": 384, "w_f1": 256, "w_f2": 256,
        "ew1": 1024}
MOFF, _o = {}, 0
for _n, _w in MATS.items():
    MOFF[_n] = _o
    _o += _w
MTOT = _o


class Core:

    def __init__(self, nc, ctx):
        self.nc, self.ctx = nc, ctx
        self.sem_ctx, self.sems = ctx, []
        pairs = [ctx.enter_context(nc.psum_tensor(f"banks{2 * i}_{2 * i + 1}", [128, 2, BLK], F32)) for i in range(4)]
        self.pair = [p[:, :, :] for p in pairs]
        self.bank = [pairs[i // 2][:, i % 2, :] for i in range(8)]
        self.warm = self.sb("warm", [1, 1])
        self.mats = self.sb("mats", [128, MTOT])
        self.cols = self.sb("cols", [128, len(COLS)])
        self.x = self.sb("x", [128, T])
        self.hn = self.sb("hn", [128, T])

    def sb(self, name, shape, dt=F32, ctx=None):
        return (ctx or self.ctx).enter_context(self.nc.sbuf_tensor(name, shape, dt))

    def sem(self, name):
        s = self.sem_ctx.enter_context(self.nc.semaphore(name))
        self.sems.append(s)
        return s

    @contextmanager
    def scope(self):
        outer = self.sem_ctx, self.sems
        with ExitStack() as ctx:
            self.sem_ctx, self.sems = ctx, []
            yield
            sems = self.sems
            with self.nc.Block() as block:
                @block.gpsimd
                def _(pool):
                    for s in sems:
                        pool.sem_clear(s)
        self.sem_ctx, self.sems = outer

    def retired(self, used, n):
        o = MOFF["Wq"] + used
        assert o + n <= MOFF["w_r1"]
        return self.mats[:, o:o + n]

    def m(self, name, rows=128, lo=0, n=None):
        o = MOFF[name] + lo
        return self.mats[0:rows, o:o + (MATS[name] - lo if n is None else n)]

    def c(self, name, rows=128):
        i = CI[name]
        return self.cols[0:rows, i:i + 1]


def linker(eng, sem):
    n = [0]

    def link(ins):
        n[0] += 1
        ins.then_inc(sem, 1)
        eng.wait_ge(sem, n[0])
    return link


def blocks(n):
    return range(n // BLK)


def sl(i, w=BLK):
    return slice(i * w, (i + 1) * w)


def normalise(k, tag, src, ncols, outs, groups=1, eps=1e-5, centre=None):
    nc = k.nc
    nb, nt = ncols // BLK, ncols // TILE
    width = nt * groups
    with ExitStack() as ctx:
        sq = k.sb(f"{tag}_sq", [128, ncols], ctx=ctx)
        ve = k.sb(f"{tag}_ve", [128, width], ctx=ctx)
        sd = k.sb(f"{tag}_sd", [128, width], ctx=ctx)
        r = k.sb(f"{tag}_r", [128, width], ctx=ctx)
        t = k.sb(f"{tag}_t", [128, width], ctx=ctx)
        rx = r if groups == 1 else k.sb(f"{tag}_rx", [128, width, HD], ctx=ctx)
        centred = k.sem(f"{tag}_centred")
        src_ready = k.sem(f"{tag}_src_ready")
        squared = k.sem(f"{tag}_squared")
        stat_done = k.sem(f"{tag}_stat_done")
        var_ready = k.sem(f"{tag}_var_ready")
        sd_ready = k.sem(f"{tag}_sd_ready")
        r_ready = k.sem(f"{tag}_r_ready")
        spread = k.sem(f"{tag}_spread")
        scaled = k.sem(f"{tag}_scaled")
        own = k.sem(f"{tag}_own")
        stat = k.bank[6][:, 0:width]
        mean = k.m("mean128") if groups == 1 else k.m("mean8")
        per = BLK // TILE
        with nc.Block() as block:
            @block.tensor
            def _(pe):
                if centre is not None:
                    for b in range(nb):
                        nc.tensor.matmul(k.bank[b][:, :], k.m("center"), centre[:, sl(b)], start=True, stop=True)\
                            .then_inc(centred, 1)
                for b in range(nb):
                    pe.wait_ge(squared, b + 1)
                    for j in range(b * per, (b + 1) * per):
                        last = nc.tensor.matmul(stat[:, j * groups:(j + 1) * groups], sq[:, sl(j, TILE)], mean,
                                                start=True, stop=True)
                last.then_inc(stat_done, 1)
                pe.wait_ge(r_ready, 1)
                for b in range(nb):
                    if b >= 2:
                        pe.wait_ge(scaled, (b - 1) * len(outs))
                    elif centre is not None:
                        pe.wait_ge(src_ready, nb)
                    for j in range(per):
                        jt = b * per + j
                        if groups == 1:
                            lhs = r[:, jt:jt + 1].to_broadcast([128, 128])
                        else:
                            lhs = rx[:, jt * groups:(jt + 1) * groups, :].rearrange("p g d -> p (g d)")
                        last = nc.tensor.matmul(k.bank[4 + b % 2][:, sl(j, TILE)], lhs, k.m("ident"),
                                                start=True, stop=True)
                    last.then_inc(spread, 1)

            @block.scalar
            def _(act):
                for b in range(nb):
                    if centre is not None:
                        act.wait_ge(src_ready, b + 1)
                    nc.scalar.activation(sq[:, sl(b)], src[:, sl(b)], ACT.Square).then_inc(squared, 1)
                act.wait_ge(var_ready, 1)
                nc.scalar.activation(sd[:, :], ve[:, :], ACT.Sqrt).then_inc(sd_ready, 1)

            @block.vector
            def _(dve):
                link = linker(dve, own)
                if centre is not None:
                    for b in range(nb):
                        dve.wait_ge(centred, b + 1)
                        nc.vector.tensor_copy(src[:, sl(b)], k.bank[b][:, :]).then_inc(src_ready, 1)
                dve.wait_ge(stat_done, 1)
                nc.vector.tensor_scalar_add(ve[:, :], stat, eps).then_inc(var_ready, 1)
                dve.wait_ge(sd_ready, 1)
                link(nc.vector.reciprocal(r[:, :], sd[:, :]))
                link(nc.vector.tensor_tensor(t[:, :], r[:, :], r[:, :], ALU.mult))
                link(nc.vector.tensor_tensor(t[:, :], t[:, :], ve[:, :], ALU.mult))
                link(nc.vector.tensor_scalar(t[:, :], t[:, :], -0.5, 1.5, ALU.mult, ALU.add))
                if groups == 1:
                    nc.vector.tensor_tensor(r[:, :], r[:, :], t[:, :], ALU.mult).then_inc(r_ready, 1)
                else:
                    wide = [128, width, HD]
                    nc.vector.tensor_tensor(rx[:, :, :], r[:, :].unsqueeze(2).to_broadcast(wide),
                                            t[:, :].unsqueeze(2).to_broadcast(wide), ALU.mult).then_inc(r_ready, 1)
                if centre is not None:
                    dve.wait_ge(src_ready, nb)
                for b in range(nb):
                    dve.wait_ge(spread, b + 1)
                    for out, w in outs:
                        nc.vector.scalar_tensor_tensor(out[:, sl(b)], src[:, sl(b)], 1.0 if w is None else w,
                                                       k.bank[4 + b % 2][:, :], ALU.mult, ALU.mult)\
                            .then_inc(scaled, 1)


def split3(k, tag, src, parts, tmp, ncols, dst_dma):
    nc = k.nc
    hi = k.sem(f"{tag}_hi")
    r1 = k.sem(f"{tag}_r1")
    mid = k.sem(f"{tag}_mid")
    lo = k.sem(f"{tag}_lo")
    sent = k.sem(f"{tag}_sent")
    nb = ncols // BLK
    with nc.Block() as block:
        @block.scalar
        def _(act):
            for b in range(nb):
                nc.scalar.copy(parts[0][:, sl(b)], src[:, sl(b)]).then_inc(hi, 1)
            for b in range(nb):
                act.wait_ge(r1, b + 1)
                nc.scalar.copy(parts[1][:, sl(b)], tmp[:, sl(b)]).then_inc(mid, 1)

        @block.vector
        def _(dve):
            for b in range(nb):
                dve.wait_ge(hi, b + 1)
                nc.vector.tensor_tensor(tmp[:, sl(b)], src[:, sl(b)], parts[0][:, sl(b)], ALU.subtract).then_inc(r1, 1)
            for b in range(nb):
                dve.wait_ge(mid, b + 1)
                nc.vector.tensor_tensor(parts[2][:, sl(b)], tmp[:, sl(b)], parts[1][:, sl(b)], ALU.subtract).then_inc(lo, 1)

        @block.sync
        def _(sp):
            n = 0
            for p, (s, v) in enumerate(((hi, nb), (mid, nb), (lo, nb))):
                sp.wait_ge(s, v)
                n += dst_dma(sp, p, sent)
            sp.wait_ge(sent, 16 * n)


def replicate_terms(k, tag, lin, full, order):
    nc = k.nc
    done = k.sem(f"{tag}_done")
    with nc.Block() as block:
        @block.sync
        def _(sp):
            for j, p in enumerate(order):
                sp.dma_start(full[8 * j:8 * j + 8], lin[p].rearrange("(h d) t -> d h t", d=8)).then_inc(done, 16)
            sp.wait_ge(done, 16 * len(order))


def attention(k, tag, q_full, k_full, k_heads, v_aug, causal, attn_t):
    nc = k.nc
    scale = float(HD) ** -0.5
    shared = k_heads == GROUPS
    nk = 1 if shared else 4
    ROWS = 9 * HD
    MROW = 96
    KROWS = MROW + 3
    QT = SEQ // TILE
    with ExitStack() as ctx:
        qa = [k.sb(f"{tag}_qa{i}", [KROWS, 4, SEQ], BF16, ctx) for i in range(2)]
        ka = [k.sb(f"{tag}_ka{i}", [KROWS, nk, SEQ], BF16, ctx) for i in range(2)]
        probs = [k.sb(f"{tag}_probs{i}", [128, 2, BLK], F32, ctx) for i in range(4)]
        mx = k.sb(f"{tag}_mx", [128, QT * 4, 2], F32, ctx)
        mneg = k.sb(f"{tag}_mneg", [128, QT, 4], F32, ctx)
        mres = k.sb(f"{tag}_mres", [128, QT, 4], F32, ctx)
        mparts = k.sb(f"{tag}_mparts", [128, QT, 3, 4], BF16, ctx)
        mrow = k.sb(f"{tag}_mrow", [12, 2, BLK], BF16, ctx)
        osb = k.sb(f"{tag}_osb", [128, BLK], F32, ctx)
        rden = k.sb(f"{tag}_rden", [128, 4, 4], F32, ctx)
        attn_tok = k.sb(f"{tag}_tok", [128, NT, HEADS * HD], F32, ctx)
        ident_b = k.sb(f"{tag}_identb", [128, 128], BF16, ctx)
        mask_kq = k.sb(f"{tag}_maskkq", [128, 128], BF16, ctx)
        mask_qk = k.sb(f"{tag}_maskqk", [128, 128], BF16, ctx)
        scores_max = [k.bank[0], k.bank[1]]
        scores_exp = [k.bank[2], k.bank[3], k.bank[4], k.bank[5]]
        out_acc = k.bank[6]
        turned = k.bank[7]

        max_units = []
        for qt in range(QT):
            for j in range(4):
                for half in range(2):
                    n = BLK if not causal else min(BLK, (qt + 1) * TILE - half * BLK)
                    if n > 0:
                        max_units.append((qt, j, half, n))
        exp_units = []
        for qb in range(2):
            for kt in range(QT if not causal else 4 * (qb + 1)):
                c0 = max(0, kt * TILE - qb * BLK) if causal else 0
                for hp in range(2):
                    exp_units.append((qb, kt, hp, c0))
        NM, NE = len(max_units), len(exp_units)
        half_end = [max(s for s, u in enumerate(exp_units) if u[0] == qb) for qb in range(2)]
        MID = half_end[0] + 1
        DUE = MID - 6 if not causal else MID - 5
        cost = [n + 70 for _, _, _, n in max_units]
        own_from = min(n for n in range(NM + 1) if sum(cost[n:]) * NE <= sum(cost) * (DUE + 1))
        stream = [(0, n) for n in range(own_from, NM)] + [(1, n) for n in range(own_from)]
        places, done, spent = [], 0, 0
        for place in range(2 * NE):
            upto = done
            while upto < NM and spent + cost[stream[upto][1]] / 2 <= sum(cost) * (place + 1) / (2 * NE):
                spent += cost[stream[upto][1]]
                upto += 1
            places.append(stream[done:upto])
            done = upto
        assert done == NM
        first_half = sum(1 for u in max_units if u[0] < QT // 2)
        assert own_from >= first_half

        def slot_of(unit):
            return next(p for p in range(2 * NE) if unit in places[p]) // 2

        done_half = [slot_of((1, first_half - 1)), slot_of((0, NM - 1))]

        loaded = k.sem(f"{tag}_loaded")
        const_ready = k.sem(f"{tag}_const")
        max_scored = k.sem(f"{tag}_max_scored")
        max_taken = k.sem(f"{tag}_max_taken")
        mparts_ready = [k.sem(f"{tag}_mparts_ready{h}") for h in range(2)]
        mturned = [k.sem(f"{tag}_mturned{h}") for h in range(2)]
        mrow_ready = [k.sem(f"{tag}_mrow_ready{h}") for h in range(2)]
        mrow_sent = [k.sem(f"{tag}_mrow_sent{h}") for h in range(2)]
        exp_scored = k.sem(f"{tag}_exp_scored")
        probs_ready = k.sem(f"{tag}_probs_ready")
        pv_done = k.sem(f"{tag}_pv_done")
        osb_ready = k.sem(f"{tag}_osb_ready")
        oturned = k.sem(f"{tag}_oturned")
        normed = k.sem(f"{tag}_normed")
        own_dve = k.sem(f"{tag}_own_dve")
        own_norm = k.sem(f"{tag}_own_norm")
        own_pool = k.sem(f"{tag}_own_pool")
        final_turned = k.sem(f"{tag}_final_turned")
        final_copied = k.sem(f"{tag}_final_copied")

        vst = [k.sb(f"{tag}_vst{i}", [128, QT, nk, 32], F32, ctx) for i in range(2)]
        vstaged = k.sem(f"{tag}_vstaged")

        with nc.Block() as block:
            @block.sync
            def _(sp):
                def load(i, g, b):
                    toks = slice(b * SEQ, (b + 1) * SEQ)
                    sp.dma_start(qa[b][0:ROWS, :, :], q_full[:, bass.ds(4 * g, 4), toks]).then_inc(loaded, 16)
                    ks = bass.ds(g, 1) if shared else bass.ds(4 * g, 4)
                    sp.dma_start(ka[b][0:ROWS, :, :], k_full[:, ks, toks]).then_inc(loaded, 16)

                def rows(i, b, half):
                    sp.wait_ge(mrow_ready[half], i + 1)
                    for p in range(3):
                        sp.dma_start(qa[b][MROW + p:MROW + p + 1, :, sl(half)],
                                     mrow[4 * p:4 * p + 4, half, :]).then_inc(mrow_sent[half], 16)

                def body(g, b, last, first=False):
                    i = 2 * g + b
                    if not last:
                        if not first:
                            sp.wait_ge(exp_scored, NE * i)
                        load(i + 1, g if b == 0 else g + 1, 1 - b)
                    rows(i, b, 1)
                    if not last:
                        rows(i + 1, 1 - b, 0)

                sp.wait_ge(const_ready, 2)
                load(0, 0, 0)
                rows(0, 0, 0)
                body(0, 0, False, True)
                body(0, 1, False)
                with sp.Fori(1, GROUPS - 1) as g:
                    body(g, 0, False)
                    body(g, 1, False)
                body(GROUPS - 1, 0, False)
                body(GROUPS - 1, 1, True)

            @block.gpsimd
            def _(pool):
                link = linker(pool, own_pool)
                for b in range(2):
                    link(nc.gpsimd.memset(qa[b][64:KROWS, :, :], 0.0))
                    link(nc.gpsimd.memset(ka[b][64:96, :, :], 0.0))
                    link(nc.gpsimd.memset(ka[b][MROW:KROWS, :, :], 1.0))
                    pool.sem_inc(const_ready, 1)
                nc.gpsimd.tensor_copy(ident_b[:, :], k.m("ident")).then_inc(const_ready, 1)
                nc.gpsimd.tensor_copy(mask_kq[:, :], k.m("mask_kq")).then_inc(const_ready, 1)
                nc.gpsimd.tensor_copy(mask_qk[:, :], k.m("mask_qk")).then_inc(const_ready, 1)

            @block.tensor
            def _(pe):
                def kj(j):
                    return 0 if shared else j

                def max_unit(i, b, n):
                    qt, j, half, w = max_units[n]
                    if n == 0:
                        pe.wait_ge(loaded, 32 * (i + 1))
                    pe.wait_ge(max_taken, NM * i + max(n - 1, 0))
                    diag = causal and half * BLK + w == (qt + 1) * TILE
                    out = scores_max[n % 2]
                    ins = nc.tensor.matmul(out[:, 0:w], qa[b][0:ROWS, j, sl(qt, TILE)],
                                           ka[b][0:ROWS, kj(j), half * BLK:half * BLK + w], start=True, stop=not diag)
                    if diag:
                        ins = nc.tensor.matmul(out[:, w - TILE:w], ident_b[:, :], mask_qk[:, :], start=False, stop=True)
                    ins.then_inc(max_scored, 1)

                def turn_max(i, half):
                    pe.wait_ge(mparts_ready[half], i + 1)
                    if not (isinstance(i, int) and i == 0):
                        pe.wait_ge(normed, 2 * i - 1 + half)
                    for t in range(4):
                        last = nc.tensor.matmul(turned[0:12, sl(t, TILE)],
                                                mparts[:, 4 * half + t, :, :].rearrange("p a j -> p (a j)"),
                                                ident_b[:, :], start=True, stop=True)
                    last.then_inc(mturned[half], 1)

                def exp_unit(i, b, s):
                    qb, kt, hp, c0 = exp_units[s]
                    if s == 0:
                        pe.wait_ge(mrow_sent[0], 48 * (i + 1))
                    if s == MID:
                        pe.wait_ge(mrow_sent[1], 48 * (i + 1))
                    pe.wait_ge(probs_ready, NE * i + max(s - 1, 0))
                    for jj in range(2):
                        j = 2 * hp + jj
                        out = scores_exp[2 * (s % 2) + jj]
                        diag = causal and kt // 4 == qb
                        ins = nc.tensor.matmul(out[:, c0:BLK], ka[b][:, kj(j), sl(kt, TILE)],
                                               qa[b][:, j, qb * BLK + c0:(qb + 1) * BLK], start=True, stop=not diag)
                        if diag:
                            ins = nc.tensor.matmul(out[:, c0:c0 + TILE], ident_b[:, :], mask_kq[:, :],
                                                   start=False, stop=True)
                    ins.then_inc(exp_scored, 1)

                def pv_quad(i, kt_slot, vstage, part):
                    qb, kt, _, c0 = exp_units[kt_slot]
                    if part == 0:
                        pe.wait_ge(probs_ready, NE * i + kt_slot + 2)
                        if kt_slot == 0:
                            pe.wait_ge(vstaged, i + 1)
                        if kt_slot == 0 or kt_slot == MID:
                            pe.wait_ge(osb_ready, 2 * i + qb)
                    mid = (c0 + BLK) // 2
                    cols = slice(c0, mid) if part == 0 else slice(mid, BLK)
                    for j in range(4):
                        last = nc.tensor.matmul(out_acc[32 * j:32 * j + 32, cols], vstage[:, kt, kj(j), :],
                                                probs[(kt_slot + j // 2) % 4][:, j % 2, cols],
                                                start=kt == 0 and part == 0,
                                                stop=kt_slot + 1 == half_end[qb], skip_group_check=True)
                    if part == 1:
                        last.then_inc(pv_done, 2)

                def turn_out(i, qb):
                    pe.wait_ge(osb_ready, 2 * i + qb + 1)
                    pe.wait_ge(normed, 2 * i + qb)
                    if qb == 0:
                        pe.wait_ge(mrow_ready[1], i + 1)
                    elif not (isinstance(i, int) and i == 2 * GROUPS - 1):
                        pe.wait_ge(mrow_ready[0], i + 2)
                    for t in range(4):
                        last = nc.tensor.matmul(turned[:, sl(t, TILE)], osb[:, sl(t, TILE)], k.m("ident"),
                                                start=True, stop=True)
                    last.then_inc(oturned, 1)

                def first_pass(i, b, place, last):
                    for ahead, n in places[place]:
                        if ahead == 0:
                            max_unit(i, b, n)
                        elif not last:
                            max_unit(i + 1, 1 - b, n)

                def body(g, b, last, first=False):
                    i = 2 * g + b
                    for s in range(NE):
                        odd = s % 2 == 1
                        if odd and s > 1:
                            products_with_v = (i, s - 3, vst[b])
                        elif odd and not first:
                            products_with_v = (i - 1, NE - 2, vst[1 - b])
                        else:
                            products_with_v = None
                        if products_with_v:
                            pv_quad(*products_with_v, 0)
                        first_pass(i, b, 2 * s, last)
                        exp_unit(i, b, s)
                        if s == done_half[1] + 2:
                            turn_max(i, 1)
                        if s == done_half[0] + 2 and not last:
                            turn_max(i + 1, 0)
                        first_pass(i, b, 2 * s + 1, last)
                        if products_with_v:
                            pv_quad(*products_with_v, 1)
                        if s == 3 and not first:
                            turn_out(i - 1, 1)
                        if s == MID + 3:
                            turn_out(i, 0)

                pe.wait_ge(const_ready, 5)
                for n in range(own_from):
                    max_unit(0, 0, n)
                    if n == first_half + 1:
                        turn_max(0, 0)
                body(0, 0, False, True)
                body(0, 1, False)
                with pe.Fori(1, GROUPS - 1) as g:
                    body(g, 0, False)
                    body(g, 1, False)
                body(GROUPS - 1, 0, False)
                body(GROUPS - 1, 1, True)
                for part in range(2):
                    pv_quad(2 * GROUPS - 1, NE - 2, vst[1], part)
                turn_out(2 * GROUPS - 1, 1)
                pe.wait_ge(normed, 16)
                for n in range(NBLK):
                    if n >= 2:
                        pe.wait_ge(final_copied, n - 1)
                    for t in range(4):
                        last = nc.tensor.matmul(scores_max[n % 2][:, sl(t, TILE)], attn_tok[:, 4 * n + t, :],
                                                k.m("ident"), start=True, stop=True)
                    last.then_inc(final_turned, 1)

            @block.scalar
            def _(act):
                def rows(i, half):
                    act.wait_ge(mturned[half], i + 1)
                    if not (isinstance(i, int) and i == 0):
                        act.wait_ge(mrow_sent[half], 48 * i)
                    nc.scalar.copy(mrow[:, half, :], turned[0:12, :]).then_inc(mrow_ready[half], 1)

                def out_copy(i, qb):
                    act.wait_ge(pv_done, NE * i + half_end[qb] + 1)
                    act.wait_ge(oturned, 2 * i + qb)
                    nc.scalar.copy(osb[:, :], out_acc[:, :]).then_inc(osb_ready, 1)

                def body(g, b, last, first=False):
                    i = 2 * g + b
                    for s in range(NE):
                        qb, kt, hp, c0 = exp_units[s]
                        act.wait_ge(exp_scored, NE * i + s + 1)
                        if not (first and s < 4):
                            act.wait_ge(pv_done, NE * i + s - 3)
                        src = k.pair[1 + s % 2][:, :, c0:BLK]
                        nc.scalar.activation(probs[s % 4][:, :, c0:BLK], src, ACT.Exp, scale=scale)\
                            .then_inc(probs_ready, 1)
                        if s == 1 and not first:
                            out_copy(i - 1, 1)
                        if s == MID + 1:
                            out_copy(i, 0)
                        if s == 3 and not last:
                            stage_next(g, b)
                        if s == done_half[1] + 2:
                            rows(i, 1)
                        if s == done_half[0] + 2 and not last:
                            rows(i + 1, 0)

                def stage_next(g, b):
                    i = 2 * g + b
                    act.wait_ge(pv_done, NE * i)
                    g1 = g if b == 0 else g + 1
                    vs = bass.ds(g1, 1) if shared else bass.ds(4 * g1, 4)
                    nb_ = 1 - b
                    nc.scalar.copy(vst[nb_][:, :, :, :], v_aug[:, nb_ * QT:(nb_ + 1) * QT, vs, :]).then_inc(vstaged, 1)

                nc.scalar.activation(k.warm[:, :], k.m("ident")[0:1, 0:1], ACT.Exp)
                vs = slice(0, 1) if shared else slice(0, 4)
                nc.scalar.copy(vst[0][:, :, :, :], v_aug[:, 0:QT, vs, :]).then_inc(vstaged, 1)
                rows(0, 0)
                body(0, 0, False, True)
                body(0, 1, False)
                with act.Fori(1, GROUPS - 1) as g:
                    body(g, 0, False)
                    body(g, 1, False)
                body(GROUPS - 1, 0, False)
                body(GROUPS - 1, 1, True)
                out_copy(2 * GROUPS - 1, 1)
                for n in range(NBLK):
                    act.wait_ge(final_turned, n + 1)
                    nc.scalar.copy(attn_t[:, sl(n)], scores_max[n % 2][:, :]).then_inc(final_copied, 1)

            @block.vector
            def _(dve):
                def link(ins, value, sem=own_dve):
                    ins.then_inc(sem, 1)
                    dve.wait_ge(sem, value)

                def take_max(i, n):
                    qt, j, half, w = max_units[n]
                    dve.wait_ge(max_scored, NM * i + n + 1)
                    nc.vector.reduce_max(mx[:, 4 * qt + j, half:half + 1], scores_max[n % 2][:, 0:w], AX.X)\
                        .then_inc(max_taken, 1)

                def combine(i, half):
                    base = 10 * i + 5 * half + 1
                    qts = slice(4 * half, 4 * half + 4)
                    mn, mr, mp = mneg[:, qts, :], mres[:, qts, :], mparts[:, qts, :, :]
                    dve.wait_ge(max_taken, NM * i + (first_half if half == 0 else NM))
                    if not (isinstance(i, int) and i == 0):
                        dve.wait_ge(mturned[half], i)
                    link(nc.vector.tensor_reduce(mn, mx[:, 16 * half:16 * half + 16, :]
                                                 .rearrange("p (q j) h -> p q j h", q=4), AX.X, ALU.max), base + 1)
                    link(nc.vector.tensor_scalar_mul(mn, mn, -1.0), base + 2)
                    link(nc.vector.tensor_copy(mp[:, :, 0, :], mn), base + 3)
                    link(nc.vector.tensor_tensor(mr, mn, mp[:, :, 0, :], ALU.subtract), base + 4)
                    link(nc.vector.tensor_copy(mp[:, :, 1, :], mr), base + 5)
                    nc.vector.tensor_tensor(mp[:, :, 2, :], mr, mp[:, :, 1, :], ALU.subtract)\
                        .then_inc(mparts_ready[half], 1)
                    dve.wait_ge(mparts_ready[half], i + 1)

                def out_norm(i, g, b, qb):
                    dve.wait_ge(oturned, 2 * i + qb + 1)
                    dve.wait_ge(normed, 2 * i + qb)
                    tv = turned[:, :].rearrange("p (t j c) -> p t j c", t=4, j=4)
                    link(nc.vector.reciprocal(rden[:, :, :], tv[:, :, :, 8]), 2 * i + qb + 1, own_norm)
                    t0 = b * QT + 4 * qb
                    dst = attn_tok[:, t0:t0 + 4, bass.ds(32 * g, 32)].rearrange("p t (j c) -> p t j c", j=4)
                    nc.vector.tensor_tensor(dst, tv[:, :, :, 0:8],
                                            rden[:, :, :].unsqueeze(3).to_broadcast([128, 4, 4, 8]), ALU.mult)\
                        .then_inc(normed, 1)

                def body(g, b, last, first=False):
                    i = 2 * g + b
                    for s in range(NE):
                        for ahead, n in places[2 * s] + places[2 * s + 1]:
                            if ahead == 0:
                                take_max(i, n)
                            elif not last:
                                take_max(i + 1, n)
                            if (ahead, n) == (0, NM - 1):
                                combine(i, 1)
                            if (ahead, n) == (1, first_half - 1) and not last:
                                combine(i + 1, 0)
                        if s == 3 and not first:
                            out_norm(i - 1, g if b == 1 else g - 1, 1 - b, 1)
                        if s == MID + 3:
                            out_norm(i, g, b, 0)

                link(nc.vector.memset(mx[:, :, :], -BIG), 1)
                for n in range(own_from):
                    take_max(0, n)
                    if n == first_half - 1:
                        combine(0, 0)
                body(0, 0, False, True)
                body(0, 1, False)
                with dve.Fori(1, GROUPS - 1) as g:
                    body(g, 0, False)
                    body(g, 1, False)
                body(GROUPS - 1, 0, False)
                body(GROUPS - 1, 1, True)
                out_norm(2 * GROUPS - 1, GROUPS - 1, 1, 1)


def products(k, tag, steps):
    nc = k.nc
    made = k.sem(f"{tag}_made")
    taken = {e: k.sem(f"{tag}_taken_{e}") for e in ("act", "dve")}

    def before(n, engine):
        return sum(1 for s in steps[:n] if s[0] == engine)

    def takers(eng, name):
        for n, (engine, _, take) in enumerate(steps):
            if engine == name:
                eng.wait_ge(made, n + 1)
                take(k.bank[n % 8]).then_inc(taken[name], 1)

    with nc.Block() as block:
        @block.tensor
        def _(pe):
            for n, (_, mms, _) in enumerate(steps):
                if n >= 8:
                    engine = steps[n - 8][0]
                    pe.wait_ge(taken[engine], before(n - 7, engine))
                for rows, cols, lhs, rhs, first, last in mms:
                    ins = nc.tensor.matmul(k.bank[n % 8][rows, cols], lhs, rhs, start=first, stop=last)
                ins.then_inc(made, 1)

        @block.scalar
        def _(act):
            takers(act, "act")

        @block.vector
        def _(dve):
            takers(dve, "dve")


def one(lhs, rhs, rows=slice(0, 128), cols=slice(0, BLK)):
    return [(rows, cols, lhs, rhs, True, True)]


def project_qkv(k, xa, qf, kf, v_aug):
    nc = k.nc
    cleared = k.sem("v_cleared")
    with nc.Block() as block:
        @block.gpsimd
        def _(pool):
            nc.gpsimd.memset(v_aug[:, :, :, :], 0.0).then_inc(cleared, 1)
            pool.wait_ge(cleared, 1)
            nc.gpsimd.memset(v_aug[:, :, :, HD:HD + 1], 1.0).then_inc(cleared, 1)
    steps = []
    for b in blocks(T):
        steps.append(("act", one(k.m("Wq"), xa[:, sl(b)]), lambda p, b=b: nc.scalar.copy(qf[:, sl(b)], p)))
    steps.append(("dve", [(slice(32 * b, 32 * b + 32), slice(0, BLK), k.m("Wk"), xa[:, sl(b)], True, True)
                          for b in blocks(T)], lambda p: nc.vector.tensor_copy(kf[:, :], p)))
    steps.append(("dve", [(slice(0, 128), sl(t, 32), xa[:, sl(t, TILE)], k.m("Wv"), True, True) for t in range(NT)],
                  lambda p: nc.vector.tensor_copy(v_aug[:, :, :, 0:HD],
                                                  p.rearrange("p (t g d) -> p t g d", t=NT, g=KV))))
    products(k, "qkv", steps)


def rope(k, tag, src, table, ncols, period, t1):
    nc = k.nc
    rotated = k.sem(f"{tag}_rotated")
    cos_done = k.sem(f"{tag}_cos_done")
    sin_done = k.sem(f"{tag}_sin_done")
    nb = ncols // BLK
    with nc.Block() as block:
        @block.tensor
        def _(pe):
            for b in range(nb):
                nc.tensor.matmul(k.bank[b][:, :], k.m("rot"), src[:, sl(b)], start=True, stop=True).then_inc(rotated, 1)

        @block.gpsimd
        def _(pool):
            for b in range(nb):
                nc.gpsimd.tensor_tensor(t1[:, sl(b)], src[:, sl(b)], table[:, 0, sl(b % (period // BLK))], ALU.mult)\
                    .then_inc(cos_done, 1)

        @block.vector
        def _(dve):
            for b in range(nb):
                dve.wait_ge(rotated, b + 1)
                dve.wait_ge(cos_done, b + 1)
                nc.vector.tensor_tensor(src[:, sl(b)], table[:, 1, sl(b % (period // BLK))], k.bank[b][:, :], ALU.mult)\
                    .then_inc(sin_done, 1)
            for b in range(nb):
                dve.wait_ge(sin_done, b + 1)
                nc.vector.tensor_tensor(src[:, sl(b)], src[:, sl(b)], t1[:, sl(b)], ALU.add)


def send_linear(k, lin, parts):
    def send(eng, p, sem):
        eng.dma_start(lin[p], parts[p][:, :]).then_inc(sem, 16)
        return 1
    return send


Q_ORDER = [0, 0, 0, 1, 1, 1, 2, 2, 2]
K_ORDER = [0, 1, 2] * 3


def hybrid_attention(k, d, rope_q, rope_k, attn_t):
    nc = k.nc
    with ExitStack() as ctx:
        v_aug = k.sb("v_aug", [128, NT, KV, 32], ctx=ctx)
        with ExitStack() as pre:
            xa = k.sb("xa", [128, T], ctx=pre)
            qf = k.sb("qf", [128, T], ctx=pre)
            kf = k.sb("kf", [128, BLK], ctx=pre)
            tmp = k.sb("rtmp", [128, T], ctx=pre)
            tq = k.sb("rope_q", [128, 2, SEQ], ctx=pre)
            tk = k.sb("rope_k", [128, 2, BLK], ctx=pre)
            parts = [k.sb(f"qparts{i}", [128, T], BF16, pre) for i in range(3)]
            tables = k.sem("rope_tables")
            with nc.Block() as block:
                @block.sync
                def _(sp):
                    sp.dma_start(tq[:, :, :], rope_q).then_inc(tables, 16)
                    sp.dma_start(tk[:, :, :], rope_k).then_inc(tables, 16)
                    sp.wait_ge(tables, 32)
            normalise(k, "rms_a", k.hn, T, [(xa, k.c("norm_attn_w"))], eps=1e-6)
            project_qkv(k, xa, qf, kf, v_aug)
            normalise(k, "rms_q", qf, T, [(qf, k.c("qn"))], groups=16, eps=1e-6)
            normalise(k, "rms_k", kf, BLK, [(kf, k.c("kn"))], groups=16, eps=1e-6)
            rope(k, "rope_q", qf, tq, T, SEQ, tmp)
            rope(k, "rope_k", kf, tk, BLK, BLK, tmp)
            split3(k, "split_q", qf, parts, tmp, T, send_linear(k, d["q_lin"], parts))

            def send_k(eng, p, sem):
                for b in blocks(T):
                    eng.dma_start(d["k_lin"][p, 0:32, sl(b)], parts[p][32 * b:32 * b + 32, 0:BLK]).then_inc(sem, 16)
                return NBLK
            split3(k, "split_k", kf, parts, tmp, BLK, send_k)
            replicate_terms(k, "rep_q", d["q_lin"], d["q_full"], Q_ORDER)
            replicate_terms(k, "rep_k", d["k_lin"][:, 0:32], d["k_full"][:, 0:KV], K_ORDER)
        attention(k, "attn0", d["q_full"], d["k_full"], KV, v_aug, False, attn_t)


def softplus(k, tag, z, out, tmp):
    nc = k.nc
    own = k.sem(f"{tag}_own")
    logs = k.sem(f"{tag}_logs")
    with nc.Block() as block:
        @block.scalar
        def _(act):
            link = linker(act, own)
            link(nc.scalar.activation(tmp, z, ACT.Abs))
            link(nc.scalar.activation(tmp, tmp, ACT.Exp, scale=-1.0))
            nc.scalar.activation(tmp, tmp, ACT.Ln, bias=1.0).then_inc(logs, 1)

        @block.vector
        def _(dve):
            dve.wait_ge(logs, 1)
            nc.vector.scalar_tensor_tensor(out, z, 0.0, tmp, ALU.max, ALU.add)


def state_space(k, ssm_in):
    nc = k.nc
    with ExitStack() as ctx:
        bt = k.sb("bt", [128, T], ctx=ctx)
        ct = k.sb("ct", [128, T], ctx=ctx)
        a_neg = k.sb("a_neg", [128, 128], ctx=ctx)
        dparts = k.sb("dparts", [96, 4, T], BF16, ctx)
        xparts = k.sb("xparts", [96, 4, T], BF16, ctx)
        sel = k.sb("sel", [96, 32, 128], BF16, ctx)
        onehot = k.sb("onehot", [128, 32, 32], F32, ctx)
        with ExitStack() as pre:
            xn = k.sb("xn", [128, T], ctx=pre)
            gate = k.sb("gate", [128, T], ctx=pre)
            delta = k.sb("delta", [128, T], ctx=pre)
            dr = k.sb("dr", [R_DT, T], ctx=pre)
            tmp = k.sb("stmp", [128, T], ctx=pre)
            bsg = k.sb("bsg", [128, 1], ctx=pre)
            parts = [k.sb(f"sparts{i}", [128, T], BF16, pre) for i in range(3)]
            prep = k.sem("ssm_prep")
            one_sem = k.sem("ssm_onehot")
            with nc.Block() as block:
                @block.scalar
                def _(act):
                    nc.scalar.activation(a_neg[:, :], k.m("A_log"), ACT.Exp).then_inc(prep, 1)

                @block.vector
                def _(dve):
                    nc.vector.tensor_tensor(bsg[:, :], k.c("bsel"), k.c("sel_gate"), ALU.mult)
                    nc.vector.tensor_copy(sel[:, :, :], k.m("eye96", 96).unsqueeze(2).to_broadcast([96, 32, 128]))
                    dve.wait_ge(prep, 1)
                    nc.vector.tensor_scalar_mul(a_neg[:, :], a_neg[:, :], -1.0)

                @block.gpsimd
                def _(pool):
                    nc.gpsimd.memset(onehot[:, :, :], 0.0).then_inc(one_sem, 1)
                    pool.wait_ge(one_sem, 1)
                    nc.gpsimd.affine_select(out=onehot[:, :, :], in_=onehot[:, :, :], compare_op=ALU.not_equal,
                                            fill=1.0, base=0, pattern=[[1, 32], [-1, 32]], channel_multiplier=0)
            normalise(k, "rms_s", k.hn, T, [(xn, k.c("ssm_norm_w"))], eps=1e-6)
            steps = []
            for b in blocks(T):
                x = xn[:, sl(b)]
                steps += [
                    ("act", one(k.m("Wx", lo=0, n=R_DT), x, rows=slice(0, R_DT)),
                     lambda p, b=b: nc.scalar.copy(dr[:, sl(b)], p[0:R_DT, :])),
                    ("dve", one(k.m("Wx", lo=R_DT, n=N_STATE), x),
                     lambda p, b=b: nc.vector.tensor_copy(bt[:, sl(b)], p)),
                    ("act", one(k.m("Wsel"), x),
                     lambda p, b=b: nc.scalar.activation(gate[:, sl(b)], p, ACT.Sigmoid, bias=bsg[:, :],
                                                         scale=k.c("sel_gate"))),
                    ("dve", one(k.m("Wx", lo=R_DT + N_STATE, n=N_STATE), x),
                     lambda p, b=b: nc.vector.tensor_copy(ct[:, sl(b)], p))]
            products(k, "ssm_p1", steps)
            with nc.Block() as block:
                @block.vector
                def _(dve):
                    nc.vector.tensor_tensor(xn[:, :], xn[:, :], gate[:, :], ALU.mult)
            steps = []
            for b in blocks(T):
                x = xn[:, sl(b)]
                steps += [
                    ("dve", one(k.m("Wdt", R_DT), dr[:, sl(b)]),
                     lambda p, b=b: nc.vector.tensor_scalar_add(delta[:, sl(b)], p, k.c("bdt"))),
                    ("act", one(k.m("Wimp"), x),
                     lambda p, b=b: nc.scalar.activation(tmp[:, sl(b)], p, ACT.Sigmoid, bias=k.c("bimp"))),
                    ("act", one(k.m("Wg"), x),
                     lambda p, b=b: nc.scalar.activation(gate[:, sl(b)], p, ACT.Sigmoid, bias=k.c("bg")))]
            products(k, "ssm_p2", steps)
            with nc.Block() as block:
                @block.vector
                def _(dve):
                    nc.vector.tensor_tensor(bt[:, :], bt[:, :], tmp[:, :], ALU.mult)
                    nc.vector.tensor_tensor(xn[:, :], xn[:, :], gate[:, :], ALU.mult)

                @block.gpsimd
                def _(pool):
                    nc.gpsimd.tensor_tensor(ct[:, :], ct[:, :], tmp[:, :], ALU.mult)
            softplus(k, "delta", delta[:, :], delta[:, :], tmp[:, :])
            with nc.Block() as block:
                @block.vector
                def _(dve):
                    nc.vector.tensor_tensor(xn[:, :], xn[:, :], delta[:, :], ALU.mult)

            def spread_to(dst):
                def send(eng, p, sem):
                    for g in range(4):
                        eng.dma_start(dst[32 * p:32 * p + 32, g, :], parts[p][32 * g:32 * g + 32, :]).then_inc(sem, 16)
                    return 4
                return send
            split3(k, "split_dt", delta, parts, tmp, T, spread_to(dparts))
            split3(k, "split_dtx", xn, parts, tmp, T, spread_to(xparts))
        scan_states(k, bt, ct, a_neg, dparts, xparts, sel, onehot, ssm_in)


def scan_states(k, bt, ct, a_neg, dparts, xparts, sel, onehot, ssm_in):
    nc = k.nc
    with ExitStack() as ctx:
        da = [k.sb(f"da{i}", [128, SEQ], ctx=ctx) for i in range(2)]
        inp = [k.sb(f"inp{i}", [128, SEQ], ctx=ctx) for i in range(2)]
        st = [k.sb(f"st{i}", [128, SEQ], ctx=ctx) for i in range(2)]
        hc = [k.sb(f"hc{i}", [128, SEQ], ctx=ctx) for i in range(2)]
        col = [k.sb(f"onecol{i}", [128, 32], ctx=ctx) for i in range(2)]
        zero = k.sb("zero_b", [128, BLK], BF16, ctx)
        a_now = k.sb("a_now", [128, 4, 2], ctx=ctx)
        a_copied = k.sem("scan_a_copied")
        zeroed = k.sem("scan_zeroed")
        dt_spread = k.sem("scan_dt_spread")
        dtx_spread = k.sem("scan_dtx_spread")
        decay_ready = k.sem("scan_decay_ready")
        input_ready = k.sem("scan_input_ready")
        state_ready = k.sem("scan_state_ready")
        hc_ready = k.sem("scan_hc_ready")
        summed = k.sem("scan_summed")
        col_ready = k.sem("scan_col_ready")
        closed = k.sem("scan_closed")
        AHEAD = 3
        UNITS = 16
        STEPS = 16
        y_bank = [[k.bank[0], k.bank[1]], [k.bank[2], k.bank[3]]]
        dt_bank = [k.bank[4], k.bank[5]]
        dtx_bank = [k.bank[6], k.bank[7]]

        def where(n):
            return n // 8, (n // 2) % 4, n % 2

        with nc.Block() as block:
            @block.tensor
            def _(pe):
                def spread(jj, n):
                    jp, g, b = where(n)
                    u = UNITS * jj + n
                    w = sel[:, bass.ds(2 * jj + jp, 1), :].rearrange("p a m -> p (a m)")
                    for h in range(2):
                        cols = slice(b * SEQ + h * BLK, b * SEQ + (h + 1) * BLK)
                        pe.wait_ge(decay_ready, first_zero(2 * u + h - 1, u))
                        nc.tensor.matmul(dt_bank[h][:, :], w, dparts[:, g, cols], start=True, stop=True)\
                            .then_inc(dt_spread, 1)
                        pe.wait_ge(input_ready, first_zero(2 * u + h - 1, u))
                        nc.tensor.matmul(dtx_bank[h][:, :], w, xparts[:, g, cols], start=True, stop=True)\
                            .then_inc(dtx_spread, 1)

                def first_zero(value, u):
                    return max(value, 0) if isinstance(u, int) else value

                def reduce(jj, n):
                    jp, g, b = where(n)
                    u = UNITS * jj + n
                    if n % 8 == 0:
                        pe.wait_ge(col_ready, 2 * jj + jp + 1)
                    pe.wait_ge(hc_ready, u + 1)
                    for h in range(2):
                        last = nc.tensor.matmul(y_bank[b][h][32 * g:32 * g + 32, :], col[jp][:, :],
                                                hc[b][:, sl(h)], start=False, stop=False, skip_group_check=True)
                    last.then_inc(summed, 1)

                pe.wait_ge(zeroed, 1)
                for b in range(2):
                    for h in range(2):
                        nc.tensor.matmul(y_bank[b][h][:, :], zero[:, 0:128], zero[:, :], start=True, stop=False,
                                         skip_group_check=True)
                for n in range(AHEAD):
                    spread(0, n)

                def step(jj, last):
                    for n in range(UNITS):
                        if n + AHEAD < UNITS:
                            spread(jj, n + AHEAD)
                        elif not last:
                            spread(jj + 1, n + AHEAD - UNITS)
                        reduce(jj, n)

                step(0, False)
                with pe.Fori(1, STEPS - 1) as jj:
                    step(jj, False)
                step(STEPS - 1, True)
                for b in range(2):
                    for h in range(2):
                        last = nc.tensor.matmul(y_bank[b][h][:, :], zero[:, 0:128], zero[:, :], start=False, stop=True,
                                                skip_group_check=True)
                last.then_inc(closed, 1)

            @block.scalar
            def _(act):
                nc.scalar.activation(k.warm[:, :], k.m("ident")[0:1, 0:1], ACT.Exp)

                def columns(jj):
                    act.wait_ge(decay_ready, 2 * UNITS * jj)
                    src = a_neg[:, :].rearrange("p (g j) -> p g j", g=4)[:, :, bass.ds(2 * jj, 2)]
                    nc.scalar.copy(a_now[:, :, :], src).then_inc(a_copied, 1)
                    act.wait_ge(a_copied, jj + 1)

                def decay(jj, n):
                    jp, g, b = where(n)
                    u = UNITS * jj + n
                    a_col = a_now[:, g, jp:jp + 1]
                    act.wait_ge(state_ready, u - 1 if not isinstance(u, int) or u > 0 else 0)
                    for h in range(2):
                        act.wait_ge(dt_spread, 2 * u + h + 1)
                        nc.scalar.activation(da[b][:, sl(h)], dt_bank[h][:, :], ACT.Exp, scale=a_col)\
                            .then_inc(decay_ready, 1)

                columns(0)
                for n in range(UNITS):
                    decay(0, n)
                with act.Fori(1, STEPS) as jj:
                    columns(jj)
                    for n in range(UNITS):
                        decay(jj, n)

            @block.vector
            def _(dve):
                nc.vector.memset(zero[:, :], 0.0).then_inc(zeroed, 1)

                def make_input(u, b):
                    for h in range(2):
                        dve.wait_ge(dtx_spread, 2 * u + h + 1)
                        nc.vector.tensor_tensor(inp[b][:, sl(h)], bt[:, b * SEQ + h * BLK:b * SEQ + (h + 1) * BLK],
                                                dtx_bank[h][:, :], ALU.mult).then_inc(input_ready, 1)

                def scan(u, b):
                    dve.wait_ge(decay_ready, 2 * u + 2)
                    dve.wait_ge(input_ready, 2 * u + 2)
                    dve.wait_ge(hc_ready, u - 1 if not isinstance(u, int) or u > 0 else 0)
                    nc.vector.tensor_tensor_scan(st[b][:, :], da[b][:, :], inp[b][:, :], 0.0, ALU.mult, ALU.add)\
                        .then_inc(state_ready, 1)

                def unit(jj, n, last):
                    u = UNITS * jj + n
                    if not last:
                        dve.wait_ge(state_ready, u)
                        make_input(u + 1, (n + 1) % 2)
                    scan(u, n % 2)

                make_input(0, 0)
                for n in range(UNITS):
                    unit(0, n, False)
                with dve.Fori(1, STEPS - 1) as jj:
                    for n in range(UNITS):
                        unit(jj, n, False)
                for n in range(UNITS):
                    unit(STEPS - 1, n, n == UNITS - 1)

            @block.gpsimd
            def _(pool):
                def unit(jj, n):
                    jp, g, b = where(n)
                    u = UNITS * jj + n
                    if n % 8 == 0:
                        j = 2 * jj + jp
                        pool.wait_ge(summed, 8 * j - 8 if not isinstance(j, int) or j > 0 else 0)
                        nc.gpsimd.tensor_copy(col[jp][:, :], onehot[:, bass.ds(j, 1), :].rearrange("p a c -> p (a c)"))\
                            .then_inc(col_ready, 1)
                    pool.wait_ge(state_ready, u + 1)
                    pool.wait_ge(summed, u - 1 if not isinstance(u, int) or u > 0 else 0)
                    nc.gpsimd.tensor_tensor(hc[b][:, :], st[b][:, :], ct[:, b * SEQ:(b + 1) * SEQ], ALU.mult)\
                        .then_inc(hc_ready, 1)

                for n in range(UNITS):
                    unit(0, n)
                with pool.Fori(1, STEPS) as jj:
                    for n in range(UNITS):
                        unit(jj, n)
        with nc.Block() as block:
            @block.vector
            def _(dve):
                for b in range(2):
                    for h in range(2):
                        cols = slice(b * SEQ + h * BLK, b * SEQ + (h + 1) * BLK)
                        nc.vector.scalar_tensor_tensor(ssm_in[:, cols], k.hn[:, cols], k.c("Dp"), y_bank[b][h][:, :],
                                                       ALU.mult, ALU.add)


def merge_and_glu(k, attn_t, ssm_in):
    nc = k.nc
    with ExitStack() as ctx:
        x1 = k.sb("x1", [128, T], ctx=ctx)
        xf = k.sb("xf", [128, T], ctx=ctx)
        products(k, "merge", [
            ("dve", [(slice(0, 128), slice(0, BLK), k.m("Wo"), attn_t[:, sl(b)], True, False),
                     (slice(0, 128), slice(0, BLK), k.m("Wout"), ssm_in[:, sl(b)], False, True)],
             lambda p, b=b: nc.vector.scalar_tensor_tensor(x1[:, sl(b)], p, 0.5, k.hn[:, sl(b)], ALU.mult, ALU.add))
            for b in blocks(T)])
        normalise(k, "rms_f", x1, T, [(xf, k.c("norm_ffn_w"))], eps=1e-6)
        silu = [k.sb(f"silu{i}", [128, BLK], ctx=ctx) for i in range(2)]
        hid = [k.sb(f"glu_hid{i}", [128, BLK], ctx=ctx) for i in range(2)]
        up = k.sem("glu_up")
        gated = k.sem("glu_silu")
        hid_ready = k.sem("glu_hid_ready")
        down = k.sem("glu_down")
        added = k.sem("glu_added")
        res = k.sem("glu_res")
        NC = FF0 // 128
        N = NBLK * NC
        with nc.Block() as block:
            @block.tensor
            def _(pe):
                def lower(n):
                    b, c = n // NC, n % NC
                    pe.wait_ge(hid_ready, n + 1)
                    if c == 0 and b >= 2:
                        pe.wait_ge(added, b - 1)
                    nc.tensor.matmul(k.bank[4 + b % 2][:, :], k.m("W2", lo=c * 128, n=128), hid[n % 2][:, :],
                                     start=c == 0, stop=c == NC - 1).then_inc(down, 1)
                for n in range(N):
                    b, c = n // NC, n % NC
                    if n >= 2:
                        pe.wait_ge(hid_ready, n - 1)
                    nc.tensor.matmul(k.bank[n % 2][:, :], k.m("W1", lo=c * 128, n=128), xf[:, sl(b)], start=True,
                                     stop=True)
                    nc.tensor.matmul(k.bank[2 + n % 2][:, :], k.m("W1", lo=FF0 + c * 128, n=128), xf[:, sl(b)],
                                     start=True, stop=True).then_inc(up, 1)
                    if n >= 1:
                        lower(n - 1)
                lower(N - 1)

            @block.scalar
            def _(act):
                for n in range(N):
                    act.wait_ge(up, n + 1)
                    if n >= 2:
                        act.wait_ge(hid_ready, n - 1)
                    nc.scalar.activation(silu[n % 2][:, :], k.bank[n % 2][:, :], ACT.Silu).then_inc(gated, 1)

            @block.vector
            def _(dve):
                nc.vector.tensor_tensor(x1[:, :], x1[:, :], k.x[:, :], ALU.add).then_inc(res, 1)
                dve.wait_ge(res, 1)
                for n in range(N + 1):
                    if n < N:
                        dve.wait_ge(gated, n + 1)
                        if n >= 2:
                            dve.wait_ge(down, n - 1)
                        nc.vector.tensor_tensor(hid[n % 2][:, :], silu[n % 2][:, :], k.bank[2 + n % 2][:, :], ALU.mult)\
                            .then_inc(hid_ready, 1)
                    if n >= NC and n % NC == 0:
                        b = n // NC - 1
                        dve.wait_ge(down, n)
                        nc.vector.tensor_tensor(k.x[:, sl(b)], x1[:, sl(b)], k.bank[4 + b % 2][:, :], ALU.add)\
                            .then_inc(added, 1)


def one_hot_weights(k, tag, idx, wgt, ntile, wt, tmp):
    nc = k.nc
    own = k.sem(f"{tag}_own")
    with nc.Block() as block:
        @block.vector
        def _(dve):
            link = linker(dve, own)
            shape = [128, ntile, EXPERTS]
            iota = k.m("iota8").unsqueeze(1).to_broadcast(shape)
            for c in range(2):
                link(nc.vector.tensor_tensor(tmp[:, :, c, :], idx[:, :, c:c + 1].to_broadcast(shape), iota,
                                             ALU.is_equal))
                link(nc.vector.tensor_tensor(tmp[:, :, c, :], tmp[:, :, c, :],
                                             wgt[:, :, c:c + 1].to_broadcast(shape), ALU.mult))
            link(nc.vector.tensor_tensor(wt[:, :, :], tmp[:, :, 0, :], tmp[:, :, 1, :], ALU.add))


def spread_weights(k, tag, wt, ntile, dst):
    nc = k.nc
    steps = []
    per = BLK // TILE
    for e in range(EXPERTS):
        for b in range(ntile // per):
            mms = [(slice(0, 128), sl(j, TILE), wt[:, b * per + j, e:e + 1].to_broadcast([128, 128]), k.m("ident"),
                    True, True) for j in range(per)]
            if len(steps) % 2:
                steps.append(("act", mms, lambda p, e=e, b=b: nc.scalar.copy(dst[:, e, sl(b)], p)))
            else:
                steps.append(("dve", mms, lambda p, e=e, b=b: nc.vector.tensor_copy(dst[:, e, sl(b)], p)))
    products(k, tag, steps)


def experts_of_layer0(k, d):
    nc = k.nc
    NC = FF0 // 128
    with ExitStack() as ctx:
        w1 = k.sb("moe_w1", [128, EXPERTS, FF0], ctx=ctx)
        w2 = k.sb("moe_w2", [128, EXPERTS, NC, 128], ctx=ctx)
        h = k.sb("moe_h", [128, MOE_T], ctx=ctx)
        hs = k.sb("moe_hs", [128, MOE_T], ctx=ctx)
        nt = MOE_T // TILE
        idx_i = k.sb("moe_idx_i", [128, nt, 2], I32, ctx)
        idx = k.sb("moe_idx", [128, nt, 2], ctx=ctx)
        wgt = k.sb("moe_wgt", [128, nt, 2], ctx=ctx)
        tmp = k.sb("moe_tmp", [128, nt, 2, EXPERTS], ctx=ctx)
        wt = k.sb("moe_wt", [128, nt, EXPERTS], ctx=ctx)
        wbc = k.sb("moe_wbc", [128, EXPERTS, MOE_T], ctx=ctx)
        hid = [k.sb(f"moe_hid{i}", [128, MOE_T], ctx=ctx) for i in range(4)]
        part = k.sb("moe_part", [128, 2, MOE_T], ctx=ctx)
        arrived = k.sem("moe_arrived")
        small = k.sem("moe_small")
        with nc.Block() as block:
            @block.sync
            def _(sp):
                sp.dma_start(idx_i[:, :, :], d["moe_idx"]).then_inc(small, 16)
                sp.dma_start(wgt[:, :, :], d["moe_wgt"]).then_inc(small, 16)
                sp.dma_start(w1[:, :, :], d["moe_w1"]).then_inc(arrived, 16)
                sp.dma_start(w2[:, :, :, :], d["moe_w2"]).then_inc(arrived, 16)

            @block.vector
            def _(dve):
                dve.wait_ge(small, 32)
                nc.vector.tensor_copy(idx[:, :, :], idx_i[:, :, :])
        one_hot_weights(k, "moe_oh", idx, wgt, nt, wt, tmp)
        spread_weights(k, "moe_sw", wt, nt, wbc)
        normalise(k, "ln_moe", h, MOE_T, [(hs, None)], centre=k.x)
        up = k.sem("moe_up")
        act_done = k.sem("moe_act_done")
        down = k.sem("moe_down")
        expert_out = k.sem("moe_expert_out")
        taken = k.sem("moe_taken")
        summed = k.sem("moe_summed")
        N = EXPERTS * NC
        LAG = 2
        with nc.Block() as block:
            @block.tensor
            def _(pe):
                pe.wait_ge(arrived, 32)

                def lower(n):
                    e, c = n // NC, n % NC
                    pe.wait_ge(act_done, n + 1)
                    if c == 0 and e >= 2:
                        pe.wait_ge(taken, e - 1)
                    ins = nc.tensor.matmul(k.bank[4 + e % 2][:, :], w2[:, e, c, :], hid[n % 4][:, :], start=c == 0,
                                           stop=c == NC - 1).then_inc(down, 1)
                for n in range(N):
                    e, c = n // NC, n % NC
                    if n >= 4:
                        pe.wait_ge(act_done, n - 3)
                    nc.tensor.matmul(k.bank[n % 4][:, :], w1[:, e, sl(c, 128)], hs[:, :], start=True, stop=True)\
                        .then_inc(up, 1)
                    if n >= LAG:
                        lower(n - LAG)
                for n in range(N - LAG, N):
                    lower(n)

            @block.scalar
            def _(act):
                for n in range(N):
                    act.wait_ge(up, n + 1)
                    if n >= 4:
                        act.wait_ge(down, n - 3)
                    nc.scalar.activation(hid[n % 4][:, :], k.bank[n % 4][:, :], ACT.Gelu).then_inc(act_done, 1)

            @block.vector
            def _(dve):
                nc.vector.tensor_scalar_add(k.x[:, :], k.x[:, :], k.c("moe_bias")).then_inc(summed, 1)
                for e in range(EXPERTS):
                    dve.wait_ge(down, NC * (e + 1))
                    dve.wait_ge(summed, max(e - 1, 0) + 1)
                    nc.vector.tensor_tensor(part[:, e % 2, :], wbc[:, e, :], k.bank[4 + e % 2][:, :], ALU.mult)\
                        .then_inc(taken, 1)
                    dve.wait_ge(taken, e + 1)
                    dve.wait_ge(summed, e + 1)
                    nc.vector.tensor_tensor(k.x[:, 0:MOE_T], k.x[:, 0:MOE_T], part[:, e % 2, :], ALU.add)\
                        .then_inc(summed, 1)


def latent_attention(k, d):
    nc = k.nc
    with ExitStack() as ctx:
        v_aug = k.sb("v_aug1", [128, NT, HEADS, 32], ctx=ctx)
        attn_t = k.sb("attn_t1", [128, T], ctx=ctx)
        cleared = k.sem("v1_cleared")
        with nc.Block() as block:
            @block.gpsimd
            def _(pool):
                nc.gpsimd.memset(v_aug[:, :, :, :], 0.0).then_inc(cleared, 1)
                pool.wait_ge(cleared, 1)
                nc.gpsimd.memset(v_aug[:, :, :, HD:HD + 1], 1.0)
        with ExitStack() as pre:
            hc = k.sb("lat_hc", [128, T], ctx=pre)
            normalise(k, "ln_lat", hc, T, [(k.hn, None)], centre=k.x)
        with ExitStack() as pre:
            ckv = k.sb("ckv", [32, T], ctx=pre)
            zq = k.sb("zq", [32, T], ctx=pre)
            qf = k.sb("qf1", [128, T], ctx=pre)
            kf = k.sb("kf1", [128, T], ctx=pre)
            tmp = k.sb("ltmp", [128, T], ctx=pre)
            m1 = k.sb("m1", [128, 128], ctx=pre)
            keff = k.sb("keff", [32, 128], ctx=pre)
            veff = k.sb("veff", [32, 128], ctx=pre)
            parts = [k.sb(f"lparts{i}", [128, T], BF16, pre) for i in range(3)]
            rows32, cols128 = slice(0, 32), slice(0, 128)
            steps = [("dve", one(k.m("W_uqT", 32), k.m("W_dq", 32), cols=cols128),
                      lambda p: nc.vector.tensor_copy(m1[:, :], p[:, 0:128])),
                     ("dve", one(k.m("W_uv"), k.m("W_oT"), rows=rows32, cols=cols128),
                      lambda p: nc.vector.tensor_copy(veff[:, :], p[0:32, 0:128]))]
            for b in blocks(T):
                steps += [("act", one(k.m("W_dkvT"), k.hn[:, sl(b)], rows=rows32),
                           lambda p, b=b: nc.scalar.copy(ckv[:, sl(b)], p[0:32, :])),
                          ("dve", one(k.m("W_dqT"), k.hn[:, sl(b)], rows=rows32),
                           lambda p, b=b: nc.vector.tensor_copy(zq[:, sl(b)], p[0:32, :]))]
            products(k, "lat_p1", steps)
            products(k, "lat_p2", [("dve", one(k.m("W_uk"), m1[:, :], rows=rows32, cols=cols128),
                                    lambda p: nc.vector.tensor_copy(keff[:, :], p[0:32, 0:128]))])
            steps = []
            for b in blocks(T):
                steps += [("act", one(k.m("W_uqT", 32), zq[:, sl(b)]), lambda p, b=b: nc.scalar.copy(qf[:, sl(b)], p)),
                          ("dve", one(keff[:, :], ckv[:, sl(b)]),
                           lambda p, b=b: nc.vector.tensor_copy(kf[:, sl(b)], p)),
                          ("act", [(slice(0, 128), sl(j, TILE), ckv[:, sl(4 * b + j, TILE)], veff[:, :], True, True)
                                   for j in range(4)],
                           lambda p, b=b: nc.scalar.copy(v_aug[:, 4 * b:4 * b + 4, :, 0:HD].rearrange("p t h d -> p (t h) d"),
                                                         p.rearrange("p (a d) -> p a d", d=HD)))]
            products(k, "lat_p3", steps)
            split3(k, "split_q1", qf, parts, tmp, T, send_linear(k, d["q_lin"], parts))
            split3(k, "split_k1", kf, parts, tmp, T, send_linear(k, d["k_lin"], parts))
            replicate_terms(k, "rep_q1", d["q_lin"], d["q_full"], Q_ORDER)
            replicate_terms(k, "rep_k1", d["k_lin"], d["k_full"], K_ORDER)
        attention(k, "attn1", d["q_full"], d["k_full"], HEADS, v_aug, True, attn_t)
        with nc.Block() as block:
            @block.vector
            def _(dve):
                nc.vector.tensor_tensor(k.x[:, :], k.x[:, :], attn_t[:, :], ALU.add)


def experts_of_layer1(k, d, y):
    nc = k.nc
    FB = 256
    NB = T // FB
    S = EXPERTS + 1
    xi = k.hn
    with ExitStack() as ctx:
        w9 = k.sb("w9", [128, EXPERTS, T], ctx=ctx)
        shared_w = k.sb("shared_w", [128, 1], ctx=ctx)
        w2p = k.sb("ew2_pad", [128, EXPERTS, 3 * D], ctx=ctx)
        eb2h = k.sb("eb2_half", [128, 3 * S], ctx=ctx)
        hb2 = k.sb("hb2_half", [128, 1], ctx=ctx)
        arrived = k.sem("ew2_arrived")
        with nc.Block() as block:
            @block.sync
            def _(sp):
                sp.dma_start(w2p[:, :, :], d["ew2_pad"]).then_inc(arrived, 16)

            @block.vector
            def _(dve):
                o = CI["eb2_0_0"]
                nc.vector.tensor_scalar_mul(eb2h[:, 0:24], k.cols[:, o:o + 24], 0.5)
                o = CI["b_s2_0"]
                nc.vector.tensor_scalar_mul(eb2h[:, 24:27], k.cols[:, o:o + 3], 0.5)
                nc.vector.tensor_scalar_mul(hb2[:, :], k.c("b_h2"), 0.5)
        with ExitStack() as pre:
            hc = k.sb("ffn_hc", [128, T], ctx=pre)
            normalise(k, "ln_ffn", hc, T, [(xi, None)], centre=k.x)
        with ExitStack() as pre:
            route(k, pre, w9, shared_w)
        with ExitStack() as pre:
            refine(k, pre, xi, w9, shared_w, w2p, eb2h, hb2, arrived, FB, NB, S)
        with nc.Block() as block:
            done = k.sem("y_done")
            sent = k.sem("y_sent")

            @block.vector
            def _(dve):
                for b in blocks(T):
                    nc.vector.tensor_tensor(k.x[:, sl(b)], k.x[:, sl(b)], xi[:, sl(b)], ALU.add).then_inc(done, 1)

            @block.sync
            def _(sp):
                for b in blocks(T):
                    sp.wait_ge(done, b + 1)
                    sp.dma_start(y[:, sl(b)], k.x[:, sl(b)]).then_inc(sent, 16)
                sp.wait_ge(sent, 16 * NBLK)


def route(k, ctx, w9, shared_w):
    nc = k.nc
    g1 = k.sb("route_g1", [32, T], ctx=ctx)
    lg = k.sb("route_logits", [128, NT, EXPERTS], ctx=ctx)
    t8 = k.sb("route_t8", [128, NT, EXPERTS], ctx=ctx)
    best = k.sb("route_best", [128, NT, 2], ctx=ctx)
    idx = k.sb("route_idx", [128, NT, 2], ctx=ctx)
    prob = k.sb("route_prob", [128, NT, 2], ctx=ctx)
    tmp = k.sb("route_tmp", [128, NT, 2, EXPERTS], ctx=ctx)
    wt = k.sb("route_wt", [128, NT, EXPERTS], ctx=ctx)
    sw = k.sb("route_sw", [128, 2], ctx=ctx)
    own = k.sem("route_own")
    steps = [("act", one(k.m("w_r1"), k.hn[:, sl(b)], rows=slice(0, 32)),
              lambda p, b=b: nc.scalar.activation(g1[:, sl(b)], p[0:32, :], ACT.Gelu, bias=k.c("b_r1", 32)))
             for b in blocks(T)]
    products(k, "route_p1", steps)
    b_r2 = k.m("b_r2").unsqueeze(1).to_broadcast([128, NT, EXPERTS])
    products(k, "route_p2", [
        ("dve", [(slice(0, 128), sl(t, EXPERTS), g1[:, sl(t, TILE)], k.m("w_r2", 32), True, True) for t in range(NT)],
         lambda p: nc.vector.tensor_tensor(lg[:, :, :], b_r2,
                                           p[:, 0:NT * EXPERTS].rearrange("p (t e) -> p t e", e=EXPERTS), ALU.add))])
    exps = k.sem("route_exps")
    diff = k.sem("route_diff")
    with nc.Block() as block:
        @block.vector
        def _(dve):
            link = linker(dve, own)
            shape = [128, NT, EXPERTS]
            iota = k.m("iota8").unsqueeze(1).to_broadcast(shape)
            for c in range(2):
                link(nc.vector.tensor_reduce(best[:, :, c], lg[:, :, :], AX.X, ALU.max))
                link(nc.vector.tensor_tensor(t8[:, :, :], lg[:, :, :], best[:, :, c:c + 1].to_broadcast(shape),
                                             ALU.is_lt))
                link(nc.vector.scalar_tensor_tensor(t8[:, :, :], t8[:, :, :], 8.0, iota, ALU.mult, ALU.add))
                link(nc.vector.tensor_reduce(idx[:, :, c], t8[:, :, :], AX.X, ALU.min))
                if c == 0:
                    link(nc.vector.tensor_tensor(t8[:, :, :], idx[:, :, 0:1].to_broadcast(shape), iota, ALU.is_equal))
                    link(nc.vector.scalar_tensor_tensor(lg[:, :, :], t8[:, :, :], -BIG, lg[:, :, :], ALU.mult,
                                                        ALU.add))
            nc.vector.tensor_tensor(best[:, :, 1], best[:, :, 1], best[:, :, 0], ALU.subtract).then_inc(diff, 1)
            dve.wait_ge(exps, 2)
            link(nc.vector.tensor_scalar_add(prob[:, :, 1], best[:, :, 1], 1.0))
            link(nc.vector.reciprocal(prob[:, :, 0], prob[:, :, 1]))
            link(nc.vector.tensor_tensor(prob[:, :, 1], best[:, :, 1], prob[:, :, 0], ALU.mult))
            link(nc.vector.tensor_scalar(sw[:, 1:2], sw[:, 0:1], -1.0, 1.0, ALU.mult, ALU.add))
            link(nc.vector.tensor_scalar_mul(prob[:, :, :], prob[:, :, :], sw[:, 1:2]))

        @block.scalar
        def _(act):
            nc.scalar.activation(sw[:, 0:1], k.c("shared_weight"), ACT.Sigmoid).then_inc(exps, 1)
            act.wait_ge(diff, 1)
            nc.scalar.activation(best[:, :, 1], best[:, :, 1], ACT.Exp).then_inc(exps, 1)
    one_hot_weights(k, "route_oh", idx, prob, NT, wt, tmp)
    spread_weights(k, "route_sw", wt, NT, w9)
    with nc.Block() as block:
        @block.vector
        def _(dve):
            nc.vector.tensor_copy(shared_w[:, :], sw[:, 0:1])


def refine(k, ctx, xi, w9, shared_w, w2p, eb2h, hb2, arrived, FB, NB, S):
    nc = k.nc
    v = k.sb("vel", [128, T], ctx=ctx)
    hid = [k.sb(f"hid{i}", [128, 5, FB], ctx=ctx) for i in range(2)]
    beta = [k.sb(f"beta{i}", [128, S, FB], ctx=ctx) for i in range(2)]
    gate = [k.sb(f"gate{i}", [128, S, FB], ctx=ctx) for i in range(2)]
    alpha = [k.sb(f"alpha{i}", [128, S, FB], ctx=ctx) for i in range(2)]
    spare = k.retired(0, (S + 4) * FB).rearrange("p (s f) -> p s f", f=FB)
    raw = [k.sb("beta_raw0", [128, S, FB], ctx=ctx)[:, :, :], spare[:, 0:S, :]]
    sum_g, sum_b, halt, ref = [spare[:, S + n, :] for n in range(4)]
    err = [k.sb(f"err{i}", [128, FB], ctx=ctx) for i in range(2)]
    xn = [k.sb(f"x_next{i}", [128, FB], ctx=ctx) for i in range(2)]
    hh = k.sb("halt_hid", [32, FB], ctx=ctx)
    fh = k.sb("ref_hid", [128, 2, FB], ctx=ctx)

    hid_scored = k.sem("hid_scored")
    hid_ready = k.sem("hid_ready")
    gate_made = k.sem("gate_made")
    beta_made = k.sem("beta_made")
    alpha_made = k.sem("alpha_made")
    gate_ready = k.sem("gate_ready")
    alpha_ready = k.sem("alpha_ready")
    beta_raw = k.sem("beta_raw")
    clipped = k.sem("beta_clipped")
    exped = k.sem("beta_exped")
    logged = k.sem("beta_logged")
    beta_ready = k.sem("beta_ready")
    err_ready = k.sem("err_ready")
    weighted = k.sem("weighted")
    pushed = k.sem("pushed")
    mixed = k.sem("mixed")
    xn_ready = k.sem("xn_ready")
    halt_scored = k.sem("halt_scored")
    halt_hid = k.sem("halt_hid_ready")
    halt_ready = k.sem("halt_ready")
    refined = k.sem("refined_ready")
    xi_ready = k.sem("xi_ready")
    own_dve = k.sem("refine_own_dve")

    half = "p (c f) -> p c f"
    pairs_bank = [k.bank[p].rearrange(half, f=FB) for p in range(2)]
    shared_bank = k.bank[2][:, 0:FB]
    halt_hid_bank = k.bank[7][0:32, FB:2 * FB]
    gate_bank = k.bank[3].rearrange(half, f=FB)
    beta_bank = k.bank[4].rearrange(half, f=FB)
    alpha_bank = k.bank[5].rearrange(half, f=FB)
    f1_bank = k.bank[6].rearrange(half, f=FB)
    halt_bank = k.bank[6][:, 0:FB]
    ref_bank = k.bank[7][:, 0:FB]
    PAIRS = (S + 1) // 2

    def slots(q):
        return [e for e in (2 * q, 2 * q + 1) if e < S]

    def weights(e, comp):
        if e == EXPERTS:
            return k.m("w_s2", EH, lo=comp * D, n=D)
        return w2p[:, e, comp * D:(comp + 1) * D]

    def bias(e, comp):
        return k.c(f"b_s2_{comp}") if e == EXPERTS else k.c(f"eb2_{e}_{comp}")

    def half_bias(e, comp):
        return eb2h[:, 3 * e + comp:3 * e + comp + 1]

    def before(unit):
        if unit is None:
            return None
        second, i, par, u = unit
        if par:
            return second, i, 0, u - 1
        if isinstance(i, int) and i == 0:
            return (False, NB // 2 - 1, 1, u - 1) if second else None
        return second, i - 1, 1, u - 1

    def each(eng, step):
        for second in (False, True):
            for par in range(2):
                unit = (second, 0, par, NB * second + par)
                step(unit, before(unit), before(before(unit)))
            with eng.Fori(1, NB // 2) as i:
                for par in range(2):
                    unit = (second, i, par, 2 * i + par + NB * second)
                    step(unit, before(unit), before(before(unit)))
        last = (True, NB // 2 - 1, 1, 2 * NB - 1)
        step(None, last, before(last))
        step(None, None, last)

    def since(eng, sem, value, unit, n):
        u = unit[3]
        if not isinstance(u, int) or u >= n:
            eng.wait_ge(sem, value)

    def cols(i, par):
        if isinstance(i, int):
            return slice((2 * i + par) * FB, (2 * i + par + 1) * FB)
        return bass.ds((2 * i + par) * FB, FB)

    with nc.Block() as block:
        @block.tensor
        def _(pe):
            def hidden(unit):
                second, i, par, u = unit
                cc = cols(i, par)
                since(pe, hid_ready, 5 * u, unit, 1)
                if second:
                    pe.wait_ge(xi_ready, u - NB + 1)
                for p in range(5):
                    if p < 4:
                        out, lx, lv = pairs_bank[p // 2][:, p % 2, :], k.m("ew1", lo=p * 128, n=128), \
                            k.m("ew1", lo=512 + p * 128, n=128)
                    else:
                        out, lx, lv = shared_bank[0:EH, :], k.m("w_s1", lo=0, n=EH), k.m("w_s1", lo=EH, n=EH)
                    ins = nc.tensor.matmul(out, lx, xi[:, cc], start=True, stop=not second)
                    if second:
                        ins = nc.tensor.matmul(out, lv, v[:, cc], start=False, stop=True)
                    if p in (1, 3, 4):
                        ins.then_inc(hid_scored, 1)

            def outputs(unit, q):
                second, i, par, u = unit
                pe.wait_ge(hid_ready, 5 * u + q + 1)
                read = S * u + 2 * q
                for comp, bank, free, value, made in (
                        (1, beta_bank, beta_raw, read, beta_made), (2, gate_bank, gate_ready, read, gate_made),
                        (0, alpha_bank, alpha_ready, read - S * NB, alpha_made))[:3 if second else 2]:
                    pe.wait_ge(free, value)
                    for e in slots(q):
                        h = hid[par][:, e // 2, :] if e < EXPERTS else hid[par][0:EH, 4, :]
                        last = nc.tensor.matmul(bank[:, e % 2, :], weights(e, comp), h, start=True, stop=True)
                    last.then_inc(made, 1)

            def halting_hidden(unit):
                _, _, par, u = unit
                pe.wait_ge(xn_ready, u + 1)
                since(pe, halt_ready, u, unit, 1)
                since(pe, xi_ready, u, unit, 1)
                nc.tensor.matmul(halt_hid_bank, k.m("w_h1"), xn[par][:, :], start=True, stop=True)
                for c in range(2):
                    last = nc.tensor.matmul(f1_bank[:, c, :], k.m("w_f1", lo=c * 128, n=128), xn[par][:, :],
                                            start=True, stop=True)
                last.then_inc(halt_scored, 1)

            def halting_outputs(unit):
                u = unit[3]
                pe.wait_ge(halt_hid, 3 * u + 3)
                nc.tensor.matmul(halt_bank, k.m("w_h2", 32).to_broadcast([32, 128]), hh[:, :], start=True, stop=True)
                for c in range(2):
                    last = nc.tensor.matmul(ref_bank, k.m("w_f2", lo=c * 128, n=128), fh[:, c, :], start=c == 0,
                                            stop=c == 1)
                last.then_inc(halt_scored, 1)

            def step(now, one_back, two_back):
                if now:
                    hidden(now)
                if two_back:
                    halting_hidden(two_back)
                if now:
                    outputs(now, 0)
                if two_back:
                    halting_outputs(two_back)
                for q in range(1, PAIRS):
                    if now:
                        outputs(now, q)

            pe.wait_ge(arrived, 16)
            each(pe, step)

        @block.scalar
        def _(act):
            def hidden(unit):
                second, _, par, u = unit
                since(act, gate_made, PAIRS * (u - 1), unit, 2)
                if second and not (isinstance(u, int) and u < NB + 2):
                    act.wait_ge(alpha_made, PAIRS * (u - NB - 1))
                for p in range(5):
                    act.wait_ge(hid_scored, 3 * u + p // 2 + 1)
                    if p < 4:
                        nc.scalar.activation(hid[par][:, p, :], pairs_bank[p // 2][:, p % 2, :], ACT.Gelu,
                                             bias=k.c(f"eb1_{p}")).then_inc(hid_ready, 1)
                    else:
                        nc.scalar.activation(hid[par][0:EH, 4, :], shared_bank[0:EH, :], ACT.Gelu,
                                             bias=k.c("b_s1", EH)).then_inc(hid_ready, 1)

            def halting_hidden(unit):
                u = unit[3]
                act.wait_ge(halt_scored, 2 * u + 1)
                nc.scalar.activation(hh[:, :], halt_hid_bank, ACT.Gelu, bias=k.c("b_h1", 32)).then_inc(halt_hid, 1)
                for c in range(2):
                    nc.scalar.activation(fh[:, c, :], f1_bank[:, c, :], ACT.Gelu, bias=k.c(f"b_f1_{c}"))\
                        .then_inc(halt_hid, 1)

            def log_exp(unit):
                _, _, par, u = unit
                act.wait_ge(clipped, u + 1)
                nc.scalar.activation(beta[par][:, :, :], beta[par][:, :, :], ACT.Exp).then_inc(exped, 1)
                act.wait_ge(exped, u + 1)
                nc.scalar.activation(beta[par][:, :, :], beta[par][:, :, :], ACT.Ln, bias=1.0).then_inc(logged, 1)

            def halting_gate(unit):
                u = unit[3]
                act.wait_ge(halt_scored, 2 * u + 2)
                since(act, xi_ready, u, unit, 1)
                nc.scalar.activation(halt[:, :], halt_bank, ACT.Tanh, bias=hb2[:, :], scale=0.5).then_inc(halt_ready, 1)

            def gates(unit):
                second, _, par, u = unit
                since(act, xn_ready, u - 1, unit, 2)
                for q in range(PAIRS):
                    act.wait_ge(gate_made, PAIRS * u + q + 1)
                    for e in slots(q):
                        nc.scalar.activation(gate[par][:, e, :], gate_bank[:, e % 2, :], ACT.Tanh,
                                             bias=half_bias(e, 2), scale=0.5).then_inc(gate_ready, 1)
                    if second:
                        act.wait_ge(alpha_made, PAIRS * (u - NB) + q + 1)
                        for e in slots(q):
                            nc.scalar.activation(alpha[par][:, e, :], alpha_bank[:, e % 2, :], ACT.Tanh,
                                                 bias=half_bias(e, 0), scale=0.5).then_inc(alpha_ready, 1)

            def step(now, one_back, two_back):
                if now:
                    hidden(now)
                if two_back:
                    halting_hidden(two_back)
                if one_back:
                    log_exp(one_back)
                if two_back:
                    halting_gate(two_back)
                if now:
                    gates(now)

            each(act, step)

        @block.gpsimd
        def _(pool):
            def weigh(z, cc):
                nc.gpsimd.tensor_tensor(z[:, 0:EXPERTS, :], z[:, 0:EXPERTS, :], w9[:, :, cc], ALU.mult)\
                    .then_inc(weighted, 1)
                nc.gpsimd.tensor_tensor(z[:, EXPERTS, :], z[:, EXPERTS, :], shared_w[:, :].to_broadcast([128, FB]),
                                        ALU.mult).then_inc(weighted, 1)

            def step(now, unit, two_back):
                if not unit:
                    return
                second, i, par, u = unit
                cc = cols(i, par)
                if not second:
                    pool.wait_ge(beta_ready, u + 1)
                    weigh(beta[par], cc)
                else:
                    pool.wait_ge(beta_ready, u + 1)
                    pool.wait_ge(err_ready, u + 1)
                    nc.gpsimd.tensor_tensor(beta[par][:, :, :], beta[par][:, :, :],
                                            err[par][:, :].unsqueeze(1).to_broadcast([128, S, FB]), ALU.mult)\
                        .then_inc(pushed, 1)
                    pool.wait_ge(mixed, u - NB + 1)
                    weigh(alpha[par], cc)

            each(pool, step)

        @block.vector
        def _(dve):
            def read_betas(unit, q):
                second, i, par, u = unit
                if q == 0:
                    since(dve, xn_ready, u - 1, unit, 2)
                    since(dve, beta_ready, u - 1, unit, 2)
                    nc.vector.tensor_scalar_sub(err[par][:, :], xi[:, cols(i, par)], k.c("mu")).then_inc(err_ready, 1)
                dve.wait_ge(beta_made, PAIRS * u + q + 1)
                for e in slots(q):
                    nc.vector.tensor_scalar_add(raw[par][:, e, :], beta_bank[:, e % 2, :], bias(e, 1))\
                        .then_inc(beta_raw, 1)
                if q == PAIRS - 1:
                    dve.wait_ge(beta_raw, S * (u + 1))
                    nc.vector.tensor_scalar_min(beta[par][:, :, :], raw[par][:, :, :], 40.0).then_inc(clipped, 1)

            def larger(unit):
                _, _, par, u = unit
                dve.wait_ge(logged, u + 1)
                nc.vector.tensor_tensor(beta[par][:, :, :], beta[par][:, :, :], raw[par][:, :, :], ALU.max)\
                    .then_inc(beta_ready, 1)

            def halting(unit):
                _, i, par, u = unit
                cc = cols(i, par)
                dve.wait_ge(halt_scored, 2 * u + 2)
                nc.vector.tensor_scalar(ref[:, :], ref_bank, k.c("b_f2"), k.c("iw"), ALU.add, ALU.mult)\
                    .then_inc(refined, 1)
                dve.wait_ge(refined, 2 * u + 1)
                dve.wait_ge(halt_ready, u + 1)
                nc.vector.scalar_tensor_tensor(ref[:, :], halt[:, :], 1.0, ref[:, :], ALU.add, ALU.mult)\
                    .then_inc(refined, 1)
                dve.wait_ge(refined, 2 * u + 2)
                nc.vector.scalar_tensor_tensor(xi[:, cc], ref[:, :], 0.5, xi[:, cc], ALU.mult, ALU.add)\
                    .then_inc(xi_ready, 1)
                dve.wait_ge(xi_ready, u + 1)

            def push(unit):
                second, i, par, u = unit
                if second:
                    dve.wait_ge(alpha_ready, S * (u - NB + 1))
                    link(nc.vector.scalar_tensor_tensor(alpha[par][:, :, :], alpha[par][:, :, :], 1.0,
                                                        v[:, cols(i, par)].unsqueeze(1).to_broadcast([128, S, FB]),
                                                        ALU.add, ALU.mult), own_base(second, u) + 1)

            def mix(unit):
                second, i, par, u = unit
                base = own_base(second, u)
                if second:
                    dve.wait_ge(pushed, u - NB + 1)
                    nc.vector.scalar_tensor_tensor(alpha[par][:, :, :], alpha[par][:, :, :], 0.5, beta[par][:, :, :],
                                                   ALU.mult, ALU.subtract).then_inc(mixed, 1)
                else:
                    dve.wait_ge(gate_ready, S * (u + 1))
                    dve.wait_ge(weighted, 2 * u + 2)
                    link(nc.vector.scalar_tensor_tensor(gate[par][:, :, :], gate[par][:, :, :], 1.0,
                                                        beta[par][:, :, :], ALU.add, ALU.mult), base + 1)

            def add_up(unit):
                second, i, par, u = unit
                base = own_base(second, u)
                cc = cols(i, par)
                gates = gate[par][:, :, :].rearrange("p e f -> p f e")
                if second:
                    dve.wait_ge(weighted, 2 * u + 2)
                    link(nc.vector.scalar_tensor_tensor(gate[par][:, :, :], gate[par][:, :, :], 1.0,
                                                        alpha[par][:, :, :], ALU.add, ALU.mult), base + 2)
                    link(nc.vector.tensor_reduce(sum_g[:, :], gates, AX.X, ALU.add), base + 3)
                    nc.vector.scalar_tensor_tensor(xn[par][:, :], sum_g[:, :], 0.05, xi[:, cc], ALU.mult, ALU.add)\
                        .then_inc(xn_ready, 1)
                else:
                    link(nc.vector.tensor_reduce(sum_g[:, :], gates, AX.X, ALU.add), base + 2)
                    link(nc.vector.tensor_reduce(sum_b[:, :], beta[par][:, :, :].rearrange("p e f -> p f e"), AX.X,
                                                 ALU.add), base + 3)
                    link(nc.vector.tensor_tensor(sum_g[:, :], sum_g[:, :], err[par][:, :], ALU.mult), base + 4)
                    link(nc.vector.scalar_tensor_tensor(v[:, cc], sum_b[:, :], -1.0, err[par][:, :], ALU.mult,
                                                        ALU.mult), base + 5)
                    nc.vector.scalar_tensor_tensor(xn[par][:, :], sum_g[:, :], -0.05, xi[:, cc], ALU.mult, ALU.add)\
                        .then_inc(xn_ready, 1)
                dve.wait_ge(xn_ready, u + 1)

            def own_base(second, u):
                return 5 * u if not second else 5 * NB + 3 * (u - NB)

            def link(ins, value):
                ins.then_inc(own_dve, 1)
                dve.wait_ge(own_dve, value)

            def step(now, one_back, two_back):
                between = [(larger, one_back), (halting, two_back), (push, one_back), (mix, one_back),
                           (add_up, one_back)]
                for q, (work, unit) in enumerate(between):
                    if now:
                        read_betas(now, q)
                    if unit:
                        work(unit)

            each(dve, step)


def build_program(nc, d, y, upto=4):
    with ExitStack() as ctx:
        k = Core(nc, ctx)
        scratch = {}
        for name, rows in (("q", HEADS), ("k", HEADS)):
            scratch[f"{name}_lin"] = nc.dram_tensor(f"{name}_lin", [3, rows * HD, T], BF16, kind="Internal").ap()
            scratch[f"{name}_full"] = nc.dram_tensor(f"{name}_full", [9 * HD, rows, T], BF16, kind="Internal").ap()
        d = {**d, **scratch}
        arrived = k.sem("inputs_arrived")
        with nc.Block() as block:
            @block.sync
            def _(sp):
                sp.dma_start(k.x[:, :], d["x"]).then_inc(arrived, 16)
                sp.dma_start(k.mats[:, :], d["mats"]).then_inc(arrived, 16)
                sp.dma_start(k.cols[:, :], d["cols"]).then_inc(arrived, 16)
                sp.wait_ge(arrived, 48)
        with ExitStack() as layer:
            hc = k.sb("ln0_c", [128, T], ctx=layer)
            normalise(k, "ln0", hc, T, [(k.hn, None)], centre=k.x)
        with ExitStack() as layer:
            attn_t = k.sb("attn_t", [128, T], ctx=layer)
            ssm_in = k.sb("ssm_in", [128, T], ctx=layer)
            with k.scope():
                hybrid_attention(k, d, d["rope_q"], d["rope_k"], attn_t)
            with k.scope():
                state_space(k, ssm_in)
            with k.scope():
                merge_and_glu(k, attn_t, ssm_in)
        if upto >= 2:
            with k.scope():
                experts_of_layer0(k, d)
        if upto >= 3:
            with k.scope():
                latent_attention(k, d)
        if upto >= 4:
            with k.scope():
                experts_of_layer1(k, d, y)
        else:
            with nc.Block() as block:
                @block.sync
                def _(sp):
                    sp.dma_start(y, k.x[:, :]).then_inc(arrived, 16)
                    sp.wait_ge(arrived, 64)


def constants():
    i = np.arange(128)
    m = {"ident": np.eye(128), "center": np.eye(128) - 1.0 / D,
         "mean8": (i[:, None] // HD == np.arange(16)[None]) / float(HD), "mean128": np.full((128, 1), 1.0 / D),
         "eye96": i[:, None] % 32 == np.arange(32)[None], "iota8": np.tile(np.arange(8.0), (128, 1)),
         "mask_kq": np.where(i[:, None] > i[None], -BIG, 0.0), "mask_qk": np.where(i[None] > i[:, None], -BIG, 0.0)}
    rot = np.zeros((128, 128))
    for r in range(128):
        if r % HD < HD // 2:
            rot[r + HD // 2, r] = -1.0
        else:
            rot[r - HD // 2, r] = 1.0
    m["rot"] = rot
    inv_freq = (np.float32(1.0) / np.float32(10000.0) ** (np.arange(0, HD, 2, dtype=np.float32) / np.float32(HD)))
    ang = np.arange(SEQ, dtype=np.float32)[None] * inv_freq.astype(np.float32)[i % 4][:, None]
    rope_q = np.stack([np.cos(ang), np.sin(ang)], 1).astype(np.float32)
    rope_k = np.stack([rope_q[32 * c:32 * c + 32, :, (c % 2) * BLK:(c % 2 + 1) * BLK] for c in range(4)], 0)
    return {n: v.astype(np.float32) for n, v in m.items()}, rope_q, rope_k.reshape(128, 2, BLK)


def lay_out(inp):
    a = {n: np.asarray(v) for n, v in inp.items()}
    h = {n[8:]: v for n, v in a.items() if n.startswith("L0_attn_")}
    e = {n[7:]: v for n, v in a.items() if n.startswith("L0_ffn_")}
    l = {n[8:]: v for n, v in a.items() if n.startswith("L1_attn_")}
    f = {n[7:]: v for n, v in a.items() if n.startswith("L1_ffn_")}
    m, rope_q, rope_k = constants()
    for n in ("Wq", "Wk", "Wv", "Wo", "Wx", "Wdt", "Wsel", "Wimp", "Wg", "Wout", "W1"):
        m[n] = h[n]
    m["W2"] = h["W2"].reshape(4, 128, 128).transpose(1, 0, 2).reshape(128, 512)
    m["A_log"] = h["A_log"].T
    m.update({"W_dqT": l["W_dq"].T, "W_dkvT": l["W_dkv"].T, "W_dq": l["W_dq"], "W_uqT": l["W_uq"].T,
              "W_uk": l["W_uk"], "W_uv": l["W_uv"], "W_oT": l["W_o"].T})
    m.update({"w_r1": f["w_r1"], "w_r2": f["w_r2"], "b_r2": np.tile(f["b_r2"], (128, 1)), "w_h1": f["w_h1"],
              "w_h2": f["w_h2"], "w_s1": np.concatenate([f["w_s1"][:D], f["w_s1"][D:]], 1), "w_s2": f["w_s2"],
              "w_f1": f["w_f1"], "w_f2": np.concatenate([f["w_f2"][:128], f["w_f2"][128:]], 1),
              "ew1": f["expert_w1"].reshape(EXPERTS, 2, D, EH).transpose(2, 1, 0, 3).reshape(D, 2 * EXPERTS * EH)})
    mats = np.zeros((128, MTOT), np.float32)
    for n, w in MATS.items():
        mats[:m[n].shape[0], MOFF[n]:MOFF[n] + w] = m[n]
    cols = np.zeros((128, len(COLS)), np.float32)

    def put(name, v):
        cols[:len(v), CI[name]] = v
    for n in ("norm_attn_w", "ssm_norm_w", "bdt", "Dp", "bsel", "sel_gate", "bimp", "bg", "norm_ffn_w"):
        put(n, h[n])
    put("qn", np.tile(h["qn_w"], 16))
    put("kn", np.tile(h["kn_w"], 16))
    put("moe_bias", e["bias"])
    put("b_r1", f["b_r1"])
    put("b_h1", f["b_h1"])
    put("b_f1_0", f["b_f1"][:128])
    put("b_f1_1", f["b_f1"][128:])
    put("b_f2", f["b_f2"])
    put("iw", f["integration_weight"])
    put("mu", f["mu"])
    put("b_h2", np.tile(f["b_h2"], 128))
    put("shared_weight", np.tile(f["shared_weight"].reshape(1), 128))
    put("b_s1", f["b_s1"])
    for c in range(3):
        put(f"b_s2_{c}", f["b_s2"][c * D:(c + 1) * D])
    for p in range(4):
        put(f"eb1_{p}", f["expert_b1"][2 * p:2 * p + 2].reshape(128))
    for x in range(EXPERTS):
        for c in range(3):
            put(f"eb2_{x}_{c}", f["expert_b2"][x, c * D:(c + 1) * D])
    ew2 = np.zeros((128, EXPERTS, 3 * D), np.float32)
    for x in range(EXPERTS):
        ew2[EH * (x % 2):EH * (x % 2) + EH, x] = f["expert_w2"][x]
    nt = MOE_T // TILE
    return {
        "x": h["x"].reshape(T, D).T, "mats": mats, "cols": cols, "rope_q": rope_q, "rope_k": rope_k,
        "moe_w1": e["w1"].transpose(1, 0, 2), "moe_w2": e["w2"].reshape(EXPERTS, FF0 // 128, 128, D).transpose(2, 0, 1, 3),
        "moe_idx": e["expert_indices"].astype(np.int32).reshape(nt, TILE, 2).transpose(1, 0, 2),
        "moe_wgt": e["expert_weights"].reshape(nt, TILE, 2).transpose(1, 0, 2), "ew2_pad": ew2}


def kernel(**inputs):
    import concourse.bacc as bacc
    from concourse.bass_utils import run_bass_kernel_spmd

    nc = bacc.Bacc("TRN2", target_bir_lowering=False, num_devices=1)
    arrays, d = {}, {}
    for name, value in lay_out(inputs).items():
        value = np.ascontiguousarray(value)
        arrays[f"in_{name}"] = value
        d[name] = nc.dram_tensor(f"in_{name}", value.shape, mybir.dt.from_np(value.dtype), kind="ExternalInput").ap()
    y = nc.dram_tensor("out_y", [D, T], F32, kind="ExternalOutput").ap()
    build_program(nc, d, y)
    r = run_bass_kernel_spmd(nc, [arrays], core_ids=[0])
    return r.results[0]["out_y"].T.reshape(BATCH, SEQ, D).copy()
```

```python
import numpy as np
import concourse.bass as bass
from concourse import mybir
from contextlib import ExitStack, contextmanager

F32 = mybir.dt.float32
BF16 = mybir.dt.bfloat16
I32 = mybir.dt.int32
ALU = mybir.AluOpType
ACT = mybir.ActivationFunctionType
AX = mybir.AxisListType

D = 128
BATCH, SEQ = 2, 1024
T = BATCH * SEQ
BLK = 512
NBLK = T // BLK
TILE = 128
NT = T // TILE
HEADS, KV, HD = 16, 4, 8
GROUPS = 4
N_STATE = 128
R_DT = 64
FF0 = 512
EXPERTS = 8
MOE_T = 512
EH = 64
BIG = 1.0e30

COLS = ["norm_attn_w", "ssm_norm_w", "bdt", "Dp", "bsel", "sel_gate", "bimp", "bg", "norm_ffn_w", "qn", "kn",
        "moe_bias", "b_r1", "b_h1", "b_f1_0", "b_f1_1", "b_f2", "iw", "one", "mu", "b_h2", "shared_weight", "b_s1",
        "b_s2_0", "b_s2_1", "b_s2_2"] + [f"eb1_{p}" for p in range(4)] + [f"eb2_{e}_{c}" for e in range(8) for c in range(3)]
CI = {n: i for i, n in enumerate(COLS)}

MATS = {"ident": 128, "center": 128, "rot": 128, "mean8": 16, "mean128": 1, "eye96": 32, "iota8": 8,
        "mask_kq": 128, "mask_qk": 128,
        "Wq": 128, "Wk": 32, "Wv": 32, "Wo": 128, "Wx": R_DT + 2 * N_STATE, "Wdt": 128, "Wsel": 128, "Wimp": 128,
        "Wg": 128, "Wout": 128, "W1": 1024, "W2": 512, "A_log": 128,
        "W_dqT": 32, "W_dkvT": 32, "W_dq": 128, "W_uqT": 128, "W_uk": 32, "W_uv": 32, "W_oT": 128,
        "w_r1": 32, "w_r2": 8, "b_r2": 8, "w_h1": 32, "w_h2": 1, "w_s1": 128, "w_s2": 384, "w_f1": 256, "w_f2": 256,
        "ew1": 1024}
MOFF, _o = {}, 0
for _n, _w in MATS.items():
    MOFF[_n] = _o
    _o += _w
MTOT = _o


class Core:

    def __init__(self, nc, ctx):
        self.nc, self.ctx = nc, ctx
        self.sem_ctx, self.sems = ctx, []
        pairs = [ctx.enter_context(nc.psum_tensor(f"banks{2 * i}_{2 * i + 1}", [128, 2, BLK], F32)) for i in range(4)]
        self.pair = [p[:, :, :] for p in pairs]
        self.bank = [pairs[i // 2][:, i % 2, :] for i in range(8)]
        self.warm = self.sb("warm", [1, 1])
        self.mats = self.sb("mats", [128, MTOT])
        self.cols = self.sb("cols", [128, len(COLS)])
        self.x = self.sb("x", [128, T])
        self.hn = self.sb("hn", [128, T])

    def sb(self, name, shape, dt=F32, ctx=None):
        return (ctx or self.ctx).enter_context(self.nc.sbuf_tensor(name, shape, dt))

    def sem(self, name):
        s = self.sem_ctx.enter_context(self.nc.semaphore(name))
        self.sems.append(s)
        return s

    @contextmanager
    def scope(self):
        outer = self.sem_ctx, self.sems
        with ExitStack() as ctx:
            self.sem_ctx, self.sems = ctx, []
            yield
            sems = self.sems
            with self.nc.Block() as block:
                @block.gpsimd
                def _(pool):
                    for s in sems:
                        pool.sem_clear(s)
        self.sem_ctx, self.sems = outer

    def retired(self, used, n):
        o = MOFF["Wq"] + used
        assert o + n <= MOFF["w_r1"]
        return self.mats[:, o:o + n]

    def m(self, name, rows=128, lo=0, n=None):
        o = MOFF[name] + lo
        return self.mats[0:rows, o:o + (MATS[name] - lo if n is None else n)]

    def c(self, name, rows=128):
        i = CI[name]
        return self.cols[0:rows, i:i + 1]


def linker(eng, sem):
    n = [0]

    def link(ins):
        n[0] += 1
        ins.then_inc(sem, 1)
        eng.wait_ge(sem, n[0])
    return link


def blocks(n):
    return range(n // BLK)


def sl(i, w=BLK):
    return slice(i * w, (i + 1) * w)


def normalise(k, tag, src, ncols, outs, groups=1, eps=1e-5, centre=None):
    nc = k.nc
    nb, nt = ncols // BLK, ncols // TILE
    width = nt * groups
    with ExitStack() as ctx:
        sq = k.sb(f"{tag}_sq", [128, ncols], ctx=ctx)
        ve = k.sb(f"{tag}_ve", [128, width], ctx=ctx)
        sd = k.sb(f"{tag}_sd", [128, width], ctx=ctx)
        r = k.sb(f"{tag}_r", [128, width], ctx=ctx)
        t = k.sb(f"{tag}_t", [128, width], ctx=ctx)
        rx = r if groups == 1 else k.sb(f"{tag}_rx", [128, width, HD], ctx=ctx)
        centred = k.sem(f"{tag}_centred")
        src_ready = k.sem(f"{tag}_src_ready")
        squared = k.sem(f"{tag}_squared")
        stat_done = k.sem(f"{tag}_stat_done")
        var_ready = k.sem(f"{tag}_var_ready")
        sd_ready = k.sem(f"{tag}_sd_ready")
        r_ready = k.sem(f"{tag}_r_ready")
        spread = k.sem(f"{tag}_spread")
        scaled = k.sem(f"{tag}_scaled")
        own = k.sem(f"{tag}_own")
        stat = k.bank[6][:, 0:width]
        mean = k.m("mean128") if groups == 1 else k.m("mean8")
        per = BLK // TILE
        with nc.Block() as block:
            @block.tensor
            def _(pe):
                if centre is not None:
                    for b in range(nb):
                        nc.tensor.matmul(k.bank[b][:, :], k.m("center"), centre[:, sl(b)], start=True, stop=True)\
                            .then_inc(centred, 1)
                for b in range(nb):
                    pe.wait_ge(squared, b + 1)
                    for j in range(b * per, (b + 1) * per):
                        last = nc.tensor.matmul(stat[:, j * groups:(j + 1) * groups], sq[:, sl(j, TILE)], mean,
                                                start=True, stop=True)
                last.then_inc(stat_done, 1)
                pe.wait_ge(r_ready, 1)
                for b in range(nb):
                    if b >= 2:
                        pe.wait_ge(scaled, (b - 1) * len(outs))
                    elif centre is not None:
                        pe.wait_ge(src_ready, nb)
                    for j in range(per):
                        jt = b * per + j
                        if groups == 1:
                            lhs = r[:, jt:jt + 1].to_broadcast([128, 128])
                        else:
                            lhs = rx[:, jt * groups:(jt + 1) * groups, :].rearrange("p g d -> p (g d)")
                        last = nc.tensor.matmul(k.bank[4 + b % 2][:, sl(j, TILE)], lhs, k.m("ident"),
                                                start=True, stop=True)
                    last.then_inc(spread, 1)

            @block.scalar
            def _(act):
                for b in range(nb):
                    if centre is not None:
                        act.wait_ge(src_ready, b + 1)
                    nc.scalar.activation(sq[:, sl(b)], src[:, sl(b)], ACT.Square).then_inc(squared, 1)
                act.wait_ge(var_ready, 1)
                nc.scalar.activation(sd[:, :], ve[:, :], ACT.Sqrt).then_inc(sd_ready, 1)

            @block.vector
            def _(dve):
                link = linker(dve, own)
                if centre is not None:
                    for b in range(nb):
                        dve.wait_ge(centred, b + 1)
                        nc.vector.tensor_copy(src[:, sl(b)], k.bank[b][:, :]).then_inc(src_ready, 1)
                dve.wait_ge(stat_done, 1)
                nc.vector.tensor_scalar_add(ve[:, :], stat, eps).then_inc(var_ready, 1)
                dve.wait_ge(sd_ready, 1)
                link(nc.vector.reciprocal(r[:, :], sd[:, :]))
                link(nc.vector.tensor_tensor(t[:, :], r[:, :], r[:, :], ALU.mult))
                link(nc.vector.tensor_tensor(t[:, :], t[:, :], ve[:, :], ALU.mult))
                link(nc.vector.tensor_scalar(t[:, :], t[:, :], -0.5, 1.5, ALU.mult, ALU.add))
                if groups == 1:
                    nc.vector.tensor_tensor(r[:, :], r[:, :], t[:, :], ALU.mult).then_inc(r_ready, 1)
                else:
                    wide = [128, width, HD]
                    nc.vector.tensor_tensor(rx[:, :, :], r[:, :].unsqueeze(2).to_broadcast(wide),
                                            t[:, :].unsqueeze(2).to_broadcast(wide), ALU.mult).then_inc(r_ready, 1)
                if centre is not None:
                    dve.wait_ge(src_ready, nb)
                for b in range(nb):
                    dve.wait_ge(spread, b + 1)
                    for out, w in outs:
                        nc.vector.scalar_tensor_tensor(out[:, sl(b)], src[:, sl(b)], 1.0 if w is None else w,
                                                       k.bank[4 + b % 2][:, :], ALU.mult, ALU.mult)\
                            .then_inc(scaled, 1)


def split3(k, tag, jobs, ncols, also=None):
    nc = k.nc
    hi = k.sem(f"{tag}_hi")
    r1 = k.sem(f"{tag}_r1")
    mid = k.sem(f"{tag}_mid")
    lo = k.sem(f"{tag}_lo")
    sent = k.sem(f"{tag}_sent")
    nb = ncols // BLK
    with nc.Block() as block:
        @block.scalar
        def _(act):
            for src, parts, _, _ in jobs:
                for b in range(nb):
                    nc.scalar.copy(parts[0][:, sl(b)], src[:, sl(b)]).then_inc(hi, 1)
            for n, (_, parts, tmp, _) in enumerate(jobs):
                for b in range(nb):
                    act.wait_ge(r1, nb * n + b + 1)
                    nc.scalar.copy(parts[1][:, sl(b)], tmp[:, sl(b)]).then_inc(mid, 1)

        @block.vector
        def _(dve):
            for n, (src, parts, tmp, _) in enumerate(jobs):
                for b in range(nb):
                    dve.wait_ge(hi, nb * n + b + 1)
                    nc.vector.tensor_tensor(tmp[:, sl(b)], src[:, sl(b)], parts[0][:, sl(b)], ALU.subtract)\
                        .then_inc(r1, 1)
            for n, (_, parts, tmp, _) in enumerate(jobs):
                for b in range(nb):
                    dve.wait_ge(mid, nb * n + b + 1)
                    nc.vector.tensor_tensor(parts[2][:, sl(b)], tmp[:, sl(b)], parts[1][:, sl(b)], ALU.subtract)\
                        .then_inc(lo, 1)

        @block.sync
        def _(sp):
            n = also(sp, sent) if also else 0
            for p, s in enumerate((hi, mid, lo)):
                for i, job in enumerate(jobs):
                    sp.wait_ge(s, nb * (i + 1))
                    n += job[3](sp, p, sent)
            sp.wait_ge(sent, 16 * n)


def replicate_terms(lin, full, order):
    def start(eng, sem):
        for j, p in enumerate(order):
            eng.dma_start(full[8 * j:8 * j + 8], lin[p].rearrange("(h d) t -> d h t", d=8)).then_inc(sem, 16)
        return len(order)
    return start


def attention(k, tag, q_full, k_full, k_heads, v_aug, causal, attn_t, also=None):
    nc = k.nc
    scale = float(HD) ** -0.5
    shared = k_heads == GROUPS
    nk = 1 if shared else 4
    ROWS = 9 * HD
    MROW = 96
    KROWS = MROW + 3
    QT = SEQ // TILE
    with ExitStack() as ctx:
        qa = [k.sb(f"{tag}_qa{i}", [KROWS, 4, SEQ], BF16, ctx) for i in range(2)]
        ka = [k.sb(f"{tag}_ka{i}", [KROWS, nk, SEQ], BF16, ctx) for i in range(2)]
        probs = [k.sb(f"{tag}_probs{i}", [128, 2, BLK], F32, ctx) for i in range(4)]
        mx = k.sb(f"{tag}_mx", [128, QT * 4, 2], F32, ctx)
        mneg = k.sb(f"{tag}_mneg", [128, QT, 4], F32, ctx)
        mres = k.sb(f"{tag}_mres", [128, QT, 4], F32, ctx)
        mparts = k.sb(f"{tag}_mparts", [128, QT, 3, 4], BF16, ctx)
        mrow = k.sb(f"{tag}_mrow", [12, 2, BLK], BF16, ctx)
        osb = k.sb(f"{tag}_osb", [128, BLK], F32, ctx)
        rden = k.sb(f"{tag}_rden", [128, 4, 4], F32, ctx)
        attn_tok = k.sb(f"{tag}_tok", [128, NT, HEADS * HD], F32, ctx)
        ident_b = k.sb(f"{tag}_identb", [128, 128], BF16, ctx)
        mask_kq = k.sb(f"{tag}_maskkq", [128, 128], BF16, ctx)
        mask_qk = k.sb(f"{tag}_maskqk", [128, 128], BF16, ctx)
        scores_max = [k.bank[0], k.bank[1]]
        scores_exp = [k.bank[2], k.bank[3], k.bank[4], k.bank[5]]
        out_acc = k.bank[6]
        turned = k.bank[7]

        max_units = []
        for qt in range(QT):
            for j in range(4):
                for half in range(2):
                    n = BLK if not causal else min(BLK, (qt + 1) * TILE - half * BLK)
                    if n > 0:
                        max_units.append((qt, j, half, n))
        exp_units = []
        for qb in range(2):
            for kt in range(QT if not causal else 4 * (qb + 1)):
                c0 = max(0, kt * TILE - qb * BLK) if causal else 0
                for hp in range(2):
                    exp_units.append((qb, kt, hp, c0))
        NM, NE = len(max_units), len(exp_units)
        half_end = [max(s for s, u in enumerate(exp_units) if u[0] == qb) for qb in range(2)]
        MID = half_end[0] + 1
        DUE = MID - 6 if not causal else MID - 5
        cost = [n + 70 for _, _, _, n in max_units]
        own_from = min(n for n in range(NM + 1) if sum(cost[n:]) * NE <= sum(cost) * (DUE + 1))
        stream = [(0, n) for n in range(own_from, NM)] + [(1, n) for n in range(own_from)]
        places, done, spent = [], 0, 0
        for place in range(2 * NE):
            upto = done
            while upto < NM and spent + cost[stream[upto][1]] / 2 <= sum(cost) * (place + 1) / (2 * NE):
                spent += cost[stream[upto][1]]
                upto += 1
            places.append(stream[done:upto])
            done = upto
        assert done == NM
        first_half = sum(1 for u in max_units if u[0] < QT // 2)
        assert own_from >= first_half

        def slot_of(unit):
            return next(p for p in range(2 * NE) if unit in places[p]) // 2

        done_half = [slot_of((1, first_half - 1)), slot_of((0, NM - 1))]

        loaded = k.sem(f"{tag}_loaded")
        const_ready = k.sem(f"{tag}_const")
        filled = k.sem(f"{tag}_filled")
        q_cleared = [k.sem(f"{tag}_q_cleared{i}") for i in range(2)]
        k_cleared = [k.sem(f"{tag}_k_cleared{i}") for i in range(2)]
        max_scored = k.sem(f"{tag}_max_scored")
        max_taken = k.sem(f"{tag}_max_taken")
        mparts_ready = [k.sem(f"{tag}_mparts_ready{h}") for h in range(2)]
        mturned = [k.sem(f"{tag}_mturned{h}") for h in range(2)]
        mrow_ready = [k.sem(f"{tag}_mrow_ready{h}") for h in range(2)]
        mrow_sent = [k.sem(f"{tag}_mrow_sent{h}") for h in range(2)]
        exp_scored = k.sem(f"{tag}_exp_scored")
        probs_ready = k.sem(f"{tag}_probs_ready")
        pv_done = k.sem(f"{tag}_pv_done")
        osb_ready = k.sem(f"{tag}_osb_ready")
        oturned = k.sem(f"{tag}_oturned")
        normed = k.sem(f"{tag}_normed")
        own_dve = k.sem(f"{tag}_own_dve")
        own_norm = k.sem(f"{tag}_own_norm")
        final_turned = k.sem(f"{tag}_final_turned")
        final_copied = k.sem(f"{tag}_final_copied")

        vst = [k.sb(f"{tag}_vst{i}", [128, QT, nk, 32], F32, ctx) for i in range(2)]
        vstaged = k.sem(f"{tag}_vstaged")

        with nc.Block() as block:
            @block.sync
            def _(sp):
                def load(i, g, b):
                    toks = slice(b * SEQ, (b + 1) * SEQ)
                    sp.dma_start(qa[b][0:ROWS, :, :], q_full[:, bass.ds(4 * g, 4), toks]).then_inc(loaded, 16)
                    ks = bass.ds(g, 1) if shared else bass.ds(4 * g, 4)
                    sp.dma_start(ka[b][0:ROWS, :, :], k_full[:, ks, toks]).then_inc(loaded, 16)

                def rows(i, b, half):
                    sp.wait_ge(mrow_ready[half], i + 1)
                    for p in range(3):
                        sp.dma_start(qa[b][MROW + p:MROW + p + 1, :, sl(half)],
                                     mrow[4 * p:4 * p + 4, half, :]).then_inc(mrow_sent[half], 16)

                def body(g, b, last, first=False):
                    i = 2 * g + b
                    if not last:
                        if first:
                            sp.wait_ge(q_cleared[1], 1)
                            sp.wait_ge(k_cleared[1], 2)
                        else:
                            sp.wait_ge(exp_scored, NE * i)
                        load(i + 1, g if b == 0 else g + 1, 1 - b)
                    rows(i, b, 1)
                    if not last:
                        rows(i + 1, 1 - b, 0)

                n = also(sp, filled) if also else 0
                sp.wait_ge(filled, 16 * n)
                sp.wait_ge(q_cleared[0], 1)
                sp.wait_ge(k_cleared[0], 2)
                load(0, 0, 0)
                rows(0, 0, 0)
                body(0, 0, False, True)
                body(0, 1, False)
                with sp.Fori(1, GROUPS - 1) as g:
                    body(g, 0, False)
                    body(g, 1, False)
                body(GROUPS - 1, 0, False)
                body(GROUPS - 1, 1, True)

            @block.gpsimd
            def _(pool):
                for b in range(2):
                    nc.gpsimd.memset(ka[b][64:96, :, :], 0.0).then_inc(k_cleared[b], 1)
                    pool.wait_ge(k_cleared[b], 1)
                    nc.gpsimd.memset(ka[b][MROW:KROWS, :, :], 1.0).then_inc(k_cleared[b], 1)
                    pool.wait_ge(k_cleared[b], 2)
                nc.gpsimd.tensor_copy(ident_b[:, :], k.m("ident")).then_inc(const_ready, 1)
                nc.gpsimd.tensor_copy(mask_kq[:, :], k.m("mask_kq")).then_inc(const_ready, 1)
                nc.gpsimd.tensor_copy(mask_qk[:, :], k.m("mask_qk")).then_inc(const_ready, 1)

            @block.tensor
            def _(pe):
                def kj(j):
                    return 0 if shared else j

                def max_unit(i, b, n):
                    qt, j, half, w = max_units[n]
                    if n == 0:
                        pe.wait_ge(loaded, 32 * (i + 1))
                    pe.wait_ge(max_taken, NM * i + max(n - 1, 0))
                    diag = causal and half * BLK + w == (qt + 1) * TILE
                    out = scores_max[n % 2]
                    ins = nc.tensor.matmul(out[:, 0:w], qa[b][0:ROWS, j, sl(qt, TILE)],
                                           ka[b][0:ROWS, kj(j), half * BLK:half * BLK + w], start=True, stop=not diag)
                    if diag:
                        ins = nc.tensor.matmul(out[:, w - TILE:w], ident_b[:, :], mask_qk[:, :], start=False, stop=True)
                    ins.then_inc(max_scored, 1)

                def turn_max(i, half):
                    pe.wait_ge(mparts_ready[half], i + 1)
                    if not (isinstance(i, int) and i == 0):
                        pe.wait_ge(normed, 2 * i - 1 + half)
                    for t in range(4):
                        last = nc.tensor.matmul(turned[0:12, sl(t, TILE)],
                                                mparts[:, 4 * half + t, :, :].rearrange("p a j -> p (a j)"),
                                                ident_b[:, :], start=True, stop=True)
                    last.then_inc(mturned[half], 1)

                def exp_unit(i, b, s):
                    qb, kt, hp, c0 = exp_units[s]
                    if s == 0:
                        pe.wait_ge(mrow_sent[0], 48 * (i + 1))
                    if s == MID:
                        pe.wait_ge(mrow_sent[1], 48 * (i + 1))
                    pe.wait_ge(probs_ready, NE * i + max(s - 1, 0))
                    for jj in range(2):
                        j = 2 * hp + jj
                        out = scores_exp[2 * (s % 2) + jj]
                        diag = causal and kt // 4 == qb
                        ins = nc.tensor.matmul(out[:, c0:BLK], ka[b][:, kj(j), sl(kt, TILE)],
                                               qa[b][:, j, qb * BLK + c0:(qb + 1) * BLK], start=True, stop=not diag)
                        if diag:
                            ins = nc.tensor.matmul(out[:, c0:c0 + TILE], ident_b[:, :], mask_kq[:, :],
                                                   start=False, stop=True)
                    ins.then_inc(exp_scored, 1)

                def pv_quad(i, kt_slot, vstage, part):
                    qb, kt, _, c0 = exp_units[kt_slot]
                    if part == 0:
                        pe.wait_ge(probs_ready, NE * i + kt_slot + 2)
                        if kt_slot == 0:
                            pe.wait_ge(vstaged, i + 1)
                        if kt_slot == 0 or kt_slot == MID:
                            pe.wait_ge(osb_ready, 2 * i + qb)
                    mid = (c0 + BLK) // 2
                    cols = slice(c0, mid) if part == 0 else slice(mid, BLK)
                    for j in range(4):
                        last = nc.tensor.matmul(out_acc[32 * j:32 * j + 32, cols], vstage[:, kt, kj(j), :],
                                                probs[(kt_slot + j // 2) % 4][:, j % 2, cols],
                                                start=kt == 0 and part == 0,
                                                stop=kt_slot + 1 == half_end[qb], skip_group_check=True)
                    if part == 1:
                        last.then_inc(pv_done, 2)

                def turn_out(i, qb):
                    pe.wait_ge(osb_ready, 2 * i + qb + 1)
                    pe.wait_ge(normed, 2 * i + qb)
                    if qb == 0:
                        pe.wait_ge(mrow_ready[1], i + 1)
                    elif not (isinstance(i, int) and i == 2 * GROUPS - 1):
                        pe.wait_ge(mrow_ready[0], i + 2)
                    for t in range(4):
                        last = nc.tensor.matmul(turned[:, sl(t, TILE)], osb[:, sl(t, TILE)], k.m("ident"),
                                                start=True, stop=True)
                    last.then_inc(oturned, 1)

                def first_pass(i, b, place, last):
                    for ahead, n in places[place]:
                        if ahead == 0:
                            max_unit(i, b, n)
                        elif not last:
                            max_unit(i + 1, 1 - b, n)

                def body(g, b, last, first=False):
                    i = 2 * g + b
                    for s in range(NE):
                        odd = s % 2 == 1
                        if odd and s > 1:
                            products_with_v = (i, s - 3, vst[b])
                        elif odd and not first:
                            products_with_v = (i - 1, NE - 2, vst[1 - b])
                        else:
                            products_with_v = None
                        if products_with_v:
                            pv_quad(*products_with_v, 0)
                        first_pass(i, b, 2 * s, last)
                        exp_unit(i, b, s)
                        if s == done_half[1] + 2:
                            turn_max(i, 1)
                        if s == done_half[0] + 2 and not last:
                            turn_max(i + 1, 0)
                        first_pass(i, b, 2 * s + 1, last)
                        if products_with_v:
                            pv_quad(*products_with_v, 1)
                        if s == 3 and not first:
                            turn_out(i - 1, 1)
                        if s == MID + 3:
                            turn_out(i, 0)

                pe.wait_ge(const_ready, 3)
                for n in range(own_from):
                    max_unit(0, 0, n)
                    if n == first_half + 1:
                        turn_max(0, 0)
                body(0, 0, False, True)
                body(0, 1, False)
                with pe.Fori(1, GROUPS - 1) as g:
                    body(g, 0, False)
                    body(g, 1, False)
                body(GROUPS - 1, 0, False)
                body(GROUPS - 1, 1, True)
                for part in range(2):
                    pv_quad(2 * GROUPS - 1, NE - 2, vst[1], part)
                turn_out(2 * GROUPS - 1, 1)
                pe.wait_ge(normed, 16)
                for n in range(NBLK):
                    if n >= 2:
                        pe.wait_ge(final_copied, n - 1)
                    for t in range(4):
                        last = nc.tensor.matmul(scores_max[n % 2][:, sl(t, TILE)], attn_tok[:, 4 * n + t, :],
                                                k.m("ident"), start=True, stop=True)
                    last.then_inc(final_turned, 1)

            @block.scalar
            def _(act):
                def rows(i, half):
                    act.wait_ge(mturned[half], i + 1)
                    if not (isinstance(i, int) and i == 0):
                        act.wait_ge(mrow_sent[half], 48 * i)
                    nc.scalar.copy(mrow[:, half, :], turned[0:12, :]).then_inc(mrow_ready[half], 1)

                def out_copy(i, qb):
                    act.wait_ge(pv_done, NE * i + half_end[qb] + 1)
                    act.wait_ge(oturned, 2 * i + qb)
                    nc.scalar.copy(osb[:, :], out_acc[:, :]).then_inc(osb_ready, 1)

                def body(g, b, last, first=False):
                    i = 2 * g + b
                    for s in range(NE):
                        qb, kt, hp, c0 = exp_units[s]
                        act.wait_ge(exp_scored, NE * i + s + 1)
                        if not (first and s < 4):
                            act.wait_ge(pv_done, NE * i + s - 3)
                        src = k.pair[1 + s % 2][:, :, c0:BLK]
                        nc.scalar.activation(probs[s % 4][:, :, c0:BLK], src, ACT.Exp, scale=scale)\
                            .then_inc(probs_ready, 1)
                        if s == 1 and not first:
                            out_copy(i - 1, 1)
                        if s == MID + 1:
                            out_copy(i, 0)
                        if s == 3 and not last:
                            stage_next(g, b)
                        if s == done_half[1] + 2:
                            rows(i, 1)
                        if s == done_half[0] + 2 and not last:
                            rows(i + 1, 0)

                def stage_next(g, b):
                    i = 2 * g + b
                    act.wait_ge(pv_done, NE * i)
                    g1 = g if b == 0 else g + 1
                    vs = bass.ds(g1, 1) if shared else bass.ds(4 * g1, 4)
                    nb_ = 1 - b
                    nc.scalar.copy(vst[nb_][:, :, :, :], v_aug[:, nb_ * QT:(nb_ + 1) * QT, vs, :]).then_inc(vstaged, 1)

                nc.scalar.activation(k.warm[:, :], k.m("ident")[0:1, 0:1], ACT.Exp)
                vs = slice(0, 1) if shared else slice(0, 4)
                nc.scalar.copy(vst[0][:, :, :, :], v_aug[:, 0:QT, vs, :]).then_inc(vstaged, 1)
                rows(0, 0)
                body(0, 0, False, True)
                body(0, 1, False)
                with act.Fori(1, GROUPS - 1) as g:
                    body(g, 0, False)
                    body(g, 1, False)
                body(GROUPS - 1, 0, False)
                body(GROUPS - 1, 1, True)
                out_copy(2 * GROUPS - 1, 1)
                for n in range(NBLK):
                    act.wait_ge(final_turned, n + 1)
                    nc.scalar.copy(attn_t[:, sl(n)], scores_max[n % 2][:, :]).then_inc(final_copied, 1)

            @block.vector
            def _(dve):
                def link(ins, value, sem=own_dve):
                    ins.then_inc(sem, 1)
                    dve.wait_ge(sem, value)

                def take_max(i, n):
                    qt, j, half, w = max_units[n]
                    dve.wait_ge(max_scored, NM * i + n + 1)
                    nc.vector.reduce_max(mx[:, 4 * qt + j, half:half + 1], scores_max[n % 2][:, 0:w], AX.X)\
                        .then_inc(max_taken, 1)

                def combine(i, half):
                    base = 10 * i + 5 * half + 1
                    qts = slice(4 * half, 4 * half + 4)
                    mn, mr, mp = mneg[:, qts, :], mres[:, qts, :], mparts[:, qts, :, :]
                    dve.wait_ge(max_taken, NM * i + (first_half if half == 0 else NM))
                    if not (isinstance(i, int) and i == 0):
                        dve.wait_ge(mturned[half], i)
                    link(nc.vector.tensor_reduce(mn, mx[:, 16 * half:16 * half + 16, :]
                                                 .rearrange("p (q j) h -> p q j h", q=4), AX.X, ALU.max), base + 1)
                    link(nc.vector.tensor_scalar_mul(mn, mn, -1.0), base + 2)
                    link(nc.vector.tensor_copy(mp[:, :, 0, :], mn), base + 3)
                    link(nc.vector.tensor_tensor(mr, mn, mp[:, :, 0, :], ALU.subtract), base + 4)
                    link(nc.vector.tensor_copy(mp[:, :, 1, :], mr), base + 5)
                    nc.vector.tensor_tensor(mp[:, :, 2, :], mr, mp[:, :, 1, :], ALU.subtract)\
                        .then_inc(mparts_ready[half], 1)
                    dve.wait_ge(mparts_ready[half], i + 1)

                def out_norm(i, g, b, qb):
                    dve.wait_ge(oturned, 2 * i + qb + 1)
                    dve.wait_ge(normed, 2 * i + qb)
                    tv = turned[:, :].rearrange("p (t j c) -> p t j c", t=4, j=4)
                    link(nc.vector.reciprocal(rden[:, :, :], tv[:, :, :, 8]), 2 * i + qb + 1, own_norm)
                    t0 = b * QT + 4 * qb
                    dst = attn_tok[:, t0:t0 + 4, bass.ds(32 * g, 32)].rearrange("p t (j c) -> p t j c", j=4)
                    nc.vector.tensor_tensor(dst, tv[:, :, :, 0:8],
                                            rden[:, :, :].unsqueeze(3).to_broadcast([128, 4, 4, 8]), ALU.mult)\
                        .then_inc(normed, 1)

                def body(g, b, last, first=False):
                    i = 2 * g + b
                    for s in range(NE):
                        for ahead, n in places[2 * s] + places[2 * s + 1]:
                            if ahead == 0:
                                take_max(i, n)
                            elif not last:
                                take_max(i + 1, n)
                            if (ahead, n) == (0, NM - 1):
                                combine(i, 1)
                            if (ahead, n) == (1, first_half - 1) and not last:
                                combine(i + 1, 0)
                        if s == 3 and not first:
                            out_norm(i - 1, g if b == 1 else g - 1, 1 - b, 1)
                        if s == MID + 3:
                            out_norm(i, g, b, 0)

                for b in range(2):
                    nc.vector.memset(qa[b][64:KROWS, :, :], 0.0).then_inc(q_cleared[b], 1)
                link(nc.vector.memset(mx[:, :, :], -BIG), 1)
                for n in range(own_from):
                    take_max(0, n)
                    if n == first_half - 1:
                        combine(0, 0)
                body(0, 0, False, True)
                body(0, 1, False)
                with dve.Fori(1, GROUPS - 1) as g:
                    body(g, 0, False)
                    body(g, 1, False)
                body(GROUPS - 1, 0, False)
                body(GROUPS - 1, 1, True)
                out_norm(2 * GROUPS - 1, GROUPS - 1, 1, 1)


def products(k, tag, steps):
    nc = k.nc
    made = k.sem(f"{tag}_made")
    taken = {e: k.sem(f"{tag}_taken_{e}") for e in ("act", "dve")}

    def before(n, engine):
        return sum(1 for s in steps[:n] if s[0] == engine)

    def takers(eng, name):
        for n, (engine, _, take) in enumerate(steps):
            if engine == name:
                eng.wait_ge(made, n + 1)
                take(k.bank[n % 8]).then_inc(taken[name], 1)

    with nc.Block() as block:
        @block.tensor
        def _(pe):
            for n, (_, mms, _) in enumerate(steps):
                if n >= 8:
                    engine = steps[n - 8][0]
                    pe.wait_ge(taken[engine], before(n - 7, engine))
                for rows, cols, lhs, rhs, first, last in mms:
                    ins = nc.tensor.matmul(k.bank[n % 8][rows, cols], lhs, rhs, start=first, stop=last)
                ins.then_inc(made, 1)

        @block.scalar
        def _(act):
            takers(act, "act")

        @block.vector
        def _(dve):
            takers(dve, "dve")


def one(lhs, rhs, rows=slice(0, 128), cols=slice(0, BLK)):
    return [(rows, cols, lhs, rhs, True, True)]


def project_qkv(k, xa, qf, kf, v_aug):
    nc = k.nc
    cleared = k.sem("v_cleared")
    with nc.Block() as block:
        @block.gpsimd
        def _(pool):
            nc.gpsimd.memset(v_aug[:, :, :, :], 0.0).then_inc(cleared, 1)
            pool.wait_ge(cleared, 1)
            nc.gpsimd.memset(v_aug[:, :, :, HD:HD + 1], 1.0).then_inc(cleared, 1)
    steps = []
    for b in blocks(T):
        steps.append(("act", one(k.m("Wq"), xa[:, sl(b)]), lambda p, b=b: nc.scalar.copy(qf[:, sl(b)], p)))
    steps.append(("dve", [(slice(32 * b, 32 * b + 32), slice(0, BLK), k.m("Wk"), xa[:, sl(b)], True, True)
                          for b in blocks(T)], lambda p: nc.vector.tensor_copy(kf[:, :], p)))
    steps.append(("dve", [(slice(0, 128), sl(t, 32), xa[:, sl(t, TILE)], k.m("Wv"), True, True) for t in range(NT)],
                  lambda p: nc.vector.tensor_copy(v_aug[:, :, :, 0:HD],
                                                  p.rearrange("p (t g d) -> p t g d", t=NT, g=KV))))
    products(k, "qkv", steps)


def rope(k, tag, src, table, ncols, period, t1):
    nc = k.nc
    rotated = k.sem(f"{tag}_rotated")
    cos_done = k.sem(f"{tag}_cos_done")
    sin_done = k.sem(f"{tag}_sin_done")
    nb = ncols // BLK
    with nc.Block() as block:
        @block.tensor
        def _(pe):
            for b in range(nb):
                nc.tensor.matmul(k.bank[b][:, :], k.m("rot"), src[:, sl(b)], start=True, stop=True).then_inc(rotated, 1)

        @block.gpsimd
        def _(pool):
            for b in range(nb):
                nc.gpsimd.tensor_tensor(t1[:, sl(b)], src[:, sl(b)], table[:, 0, sl(b % (period // BLK))], ALU.mult)\
                    .then_inc(cos_done, 1)

        @block.vector
        def _(dve):
            for b in range(nb):
                dve.wait_ge(rotated, b + 1)
                dve.wait_ge(cos_done, b + 1)
                nc.vector.tensor_tensor(src[:, sl(b)], table[:, 1, sl(b % (period // BLK))], k.bank[b][:, :], ALU.mult)\
                    .then_inc(sin_done, 1)
            for b in range(nb):
                dve.wait_ge(sin_done, b + 1)
                nc.vector.tensor_tensor(src[:, sl(b)], src[:, sl(b)], t1[:, sl(b)], ALU.add)


def send_linear(k, lin, parts):
    def send(eng, p, sem):
        eng.dma_start(lin[p], parts[p][:, :]).then_inc(sem, 16)
        return 1
    return send


Q_ORDER = [0, 0, 0, 1, 1, 1, 2, 2, 2]
K_ORDER = [0, 1, 2] * 3


def hybrid_attention(k, d, rope_q, rope_k, weights_arrived, attn_t):
    nc = k.nc
    with ExitStack() as ctx:
        v_aug = k.sb("v_aug", [128, NT, KV, 32], ctx=ctx)
        with ExitStack() as pre:
            xa = k.sb("xa", [128, T], ctx=pre)
            qf = k.sb("qf", [128, T], ctx=pre)
            kf = k.sb("kf", [128, BLK], ctx=pre)
            tmp = k.sb("rtmp", [128, T], ctx=pre)
            tq = k.sb("rope_q", [128, 2, SEQ], ctx=pre)
            tk = k.sb("rope_k", [128, 2, BLK], ctx=pre)
            parts = [k.sb(f"qparts{i}", [128, T], BF16, pre) for i in range(3)]
            tables = k.sem("rope_tables")
            with nc.Block() as block:
                @block.sync
                def _(sp):
                    sp.dma_start(tq[:, :, :], rope_q).then_inc(tables, 16)
                    sp.dma_start(tk[:, :, :], rope_k).then_inc(tables, 16)
                    sp.wait_ge(tables, 32)
                    sp.wait_ge(weights_arrived, 32)
            normalise(k, "rms_a", k.hn, T, [(xa, k.c("norm_attn_w"))], eps=1e-6)
            project_qkv(k, xa, qf, kf, v_aug)
            normalise(k, "rms_q", qf, T, [(qf, k.c("qn"))], groups=16, eps=1e-6)
            normalise(k, "rms_k", kf, BLK, [(kf, k.c("kn"))], groups=16, eps=1e-6)
            rope(k, "rope_q", qf, tq, T, SEQ, tmp)
            rope(k, "rope_k", kf, tk, BLK, BLK, tmp)
            split3(k, "split_q", [(qf, parts, tmp, send_linear(k, d["q_lin"], parts))], T)

            def send_k(eng, p, sem):
                for b in blocks(T):
                    eng.dma_start(d["k_lin"][p, 0:32, sl(b)], parts[p][32 * b:32 * b + 32, 0:BLK]).then_inc(sem, 16)
                return NBLK
            split3(k, "split_k", [(kf, parts, tmp, send_k)], BLK,
                   also=replicate_terms(d["q_lin"], d["q_full"], Q_ORDER))
        attention(k, "attn0", d["q_full"], d["k_full"], KV, v_aug, False, attn_t,
                  also=replicate_terms(d["k_lin"][:, 0:32], d["k_full"][:, 0:KV], K_ORDER))


def softplus(k, tag, z, out, tmp):
    nc = k.nc
    own = k.sem(f"{tag}_own")
    logs = k.sem(f"{tag}_logs")
    with nc.Block() as block:
        @block.scalar
        def _(act):
            link = linker(act, own)
            link(nc.scalar.activation(tmp, z, ACT.Abs))
            link(nc.scalar.activation(tmp, tmp, ACT.Exp, scale=-1.0))
            nc.scalar.activation(tmp, tmp, ACT.Ln, bias=1.0).then_inc(logs, 1)

        @block.vector
        def _(dve):
            dve.wait_ge(logs, 1)
            nc.vector.scalar_tensor_tensor(out, z, 0.0, tmp, ALU.max, ALU.add)


def state_space(k, ssm_in):
    nc = k.nc
    with ExitStack() as ctx:
        bt = k.sb("bt", [128, T], ctx=ctx)
        ct = k.sb("ct", [128, T], ctx=ctx)
        a_neg = k.sb("a_neg", [128, 128], ctx=ctx)
        dparts = k.sb("dparts", [96, 4, T], BF16, ctx)
        xparts = k.sb("xparts", [96, 4, T], BF16, ctx)
        sel = k.sb("sel", [96, 32, 128], BF16, ctx)
        onehot = k.sb("onehot", [128, 32, 32], F32, ctx)
        with ExitStack() as pre:
            xn = k.sb("xn", [128, T], ctx=pre)
            gate = k.sb("gate", [128, T], ctx=pre)
            delta = k.sb("delta", [128, T], ctx=pre)
            dr = k.sb("dr", [R_DT, T], ctx=pre)
            tmp = k.sb("stmp", [128, T], ctx=pre)
            bsg = k.sb("bsg", [128, 1], ctx=pre)
            parts = [k.sb(f"sparts{i}", [128, T], BF16, pre) for i in range(3)]
            prep = k.sem("ssm_prep")
            one_sem = k.sem("ssm_onehot")
            with nc.Block() as block:
                @block.scalar
                def _(act):
                    nc.scalar.activation(a_neg[:, :], k.m("A_log"), ACT.Exp).then_inc(prep, 1)

                @block.vector
                def _(dve):
                    nc.vector.tensor_tensor(bsg[:, :], k.c("bsel"), k.c("sel_gate"), ALU.mult)
                    nc.vector.tensor_copy(sel[:, :, :], k.m("eye96", 96).unsqueeze(2).to_broadcast([96, 32, 128]))
                    dve.wait_ge(prep, 1)
                    nc.vector.tensor_scalar_mul(a_neg[:, :], a_neg[:, :], -1.0)

                @block.gpsimd
                def _(pool):
                    nc.gpsimd.memset(onehot[:, :, :], 0.0).then_inc(one_sem, 1)
                    pool.wait_ge(one_sem, 1)
                    nc.gpsimd.affine_select(out=onehot[:, :, :], in_=onehot[:, :, :], compare_op=ALU.not_equal,
                                            fill=1.0, base=0, pattern=[[1, 32], [-1, 32]], channel_multiplier=0)
            normalise(k, "rms_s", k.hn, T, [(xn, k.c("ssm_norm_w"))], eps=1e-6)
            steps = []
            for b in blocks(T):
                x = xn[:, sl(b)]
                steps += [
                    ("act", one(k.m("Wx", lo=0, n=R_DT), x, rows=slice(0, R_DT)),
                     lambda p, b=b: nc.scalar.copy(dr[:, sl(b)], p[0:R_DT, :])),
                    ("dve", one(k.m("Wx", lo=R_DT, n=N_STATE), x),
                     lambda p, b=b: nc.vector.tensor_copy(bt[:, sl(b)], p)),
                    ("act", one(k.m("Wsel"), x),
                     lambda p, b=b: nc.scalar.activation(gate[:, sl(b)], p, ACT.Sigmoid, bias=bsg[:, :],
                                                         scale=k.c("sel_gate"))),
                    ("dve", one(k.m("Wx", lo=R_DT + N_STATE, n=N_STATE), x),
                     lambda p, b=b: nc.vector.tensor_copy(ct[:, sl(b)], p))]
            products(k, "ssm_p1", steps)
            with nc.Block() as block:
                @block.vector
                def _(dve):
                    nc.vector.tensor_tensor(xn[:, :], xn[:, :], gate[:, :], ALU.mult)
            steps = []
            for b in blocks(T):
                x = xn[:, sl(b)]
                steps += [
                    ("dve", one(k.m("Wdt", R_DT), dr[:, sl(b)]),
                     lambda p, b=b: nc.vector.tensor_scalar_add(delta[:, sl(b)], p, k.c("bdt"))),
                    ("act", one(k.m("Wimp"), x),
                     lambda p, b=b: nc.scalar.activation(tmp[:, sl(b)], p, ACT.Sigmoid, bias=k.c("bimp"))),
                    ("act", one(k.m("Wg"), x),
                     lambda p, b=b: nc.scalar.activation(gate[:, sl(b)], p, ACT.Sigmoid, bias=k.c("bg")))]
            products(k, "ssm_p2", steps)
            with nc.Block() as block:
                @block.vector
                def _(dve):
                    nc.vector.tensor_tensor(bt[:, :], bt[:, :], tmp[:, :], ALU.mult)
                    nc.vector.tensor_tensor(xn[:, :], xn[:, :], gate[:, :], ALU.mult)

                @block.gpsimd
                def _(pool):
                    nc.gpsimd.tensor_tensor(ct[:, :], ct[:, :], tmp[:, :], ALU.mult)
            softplus(k, "delta", delta[:, :], delta[:, :], tmp[:, :])
            with nc.Block() as block:
                @block.vector
                def _(dve):
                    nc.vector.tensor_tensor(xn[:, :], xn[:, :], delta[:, :], ALU.mult)

            more_parts = [k.sb(f"xparts_lin{i}", [128, T], BF16, pre) for i in range(3)]

            def spread_to(dst, parts):
                def send(eng, p, sem):
                    for g in range(4):
                        eng.dma_start(dst[32 * p:32 * p + 32, g, :], parts[p][32 * g:32 * g + 32, :]).then_inc(sem, 16)
                    return 4
                return send
            split3(k, "split_dt", [(delta, parts, tmp, spread_to(dparts, parts)),
                                   (xn, more_parts, gate, spread_to(xparts, more_parts))], T)
        for b in range(2):
            scan_states(k, b, bt, ct, a_neg, dparts, xparts, sel, onehot, ssm_in)


def scan_states(k, b, bt, ct, a_neg, dparts, xparts, sel, onehot, ssm_in):
    nc = k.nc
    with ExitStack() as ctx:
        da = [k.sb(f"da{b}_{i}", [128, SEQ], ctx=ctx) for i in range(4)]
        inp = [k.sb(f"inp{b}_{i}", [128, SEQ], ctx=ctx) for i in range(2)]
        st = [k.sb(f"st{b}_{i}", [128, SEQ], ctx=ctx) for i in range(4)]
        hc = [k.sb(f"hc{b}_{i}", [128, SEQ], ctx=ctx) for i in range(8)]
        col = [k.sb(f"onecol{b}_{i}", [128, 32], ctx=ctx) for i in range(2)]
        zero = k.sb(f"zero_b{b}", [128, BLK], BF16, ctx)
        a_now = k.sb(f"a_now{b}", [128, 4, 4], ctx=ctx)
        a_copied = k.sem(f"scan{b}_a_copied")
        zeroed = k.sem(f"scan{b}_zeroed")
        dt_spread = k.sem(f"scan{b}_dt_spread")
        dtx_spread = k.sem(f"scan{b}_dtx_spread")
        decay_ready = k.sem(f"scan{b}_decay_ready")
        input_ready = k.sem(f"scan{b}_input_ready")
        state_ready = k.sem(f"scan{b}_state_ready")
        hc_ready = k.sem(f"scan{b}_hc_ready")
        summed = k.sem(f"scan{b}_summed")
        col_ready = k.sem(f"scan{b}_col_ready")
        AHEAD = 4
        UNITS = 16
        STEPS = D // UNITS
        y_bank = k.bank[0:2]
        dt_bank = k.bank[2:4]
        dtx_pair = k.pair[2:4]

        def after(eng, sem, value, u, n):
            if not isinstance(u, int) or u >= n:
                eng.wait_ge(sem, value)

        with nc.Block() as block:
            @block.tensor
            def _(pe):
                def spread(jj, n):
                    jp, g = n // 4, n % 4
                    u = UNITS * jj + n
                    w = sel[:, bass.ds(4 * jj + jp, 1), :].rearrange("p a m -> p (a m)")
                    for h in range(2):
                        cols = slice(b * SEQ + h * BLK, b * SEQ + (h + 1) * BLK)
                        after(pe, decay_ready, 2 * u + h - 1, u, 1)
                        nc.tensor.matmul(dt_bank[h][:, :], w, dparts[:, g, cols], start=True, stop=True)\
                            .then_inc(dt_spread, 1)
                        if h == 0:
                            after(pe, input_ready, u - 1, u, 2)
                        nc.tensor.matmul(dtx_pair[n % 2][:, h, :], w, xparts[:, g, cols], start=True, stop=True)\
                            .then_inc(dtx_spread, 1)

                def reduce(jj, jp, h):
                    if h == 0:
                        pe.wait_ge(col_ready, 4 * jj + jp + 1)
                        pe.wait_ge(hc_ready, UNITS * jj + 4 * jp + 4)
                    for g in range(4):
                        last = nc.tensor.matmul(y_bank[h][32 * g:32 * g + 32, :], col[jp % 2][:, :],
                                                hc[(4 * jp + g) % 8][:, sl(h)], start=False, stop=False,
                                                skip_group_check=True)
                    if h == 1:
                        last.then_inc(summed, 1)

                pe.wait_ge(zeroed, 1)
                for h in range(2):
                    nc.tensor.matmul(y_bank[h][:, :], zero[:, 0:128], zero[:, :], start=True, stop=False,
                                     skip_group_check=True)
                for n in range(AHEAD):
                    spread(0, n)

                def step(jj, last):
                    for n in range(UNITS):
                        if n % 2 == 1:
                            jp, h = n // 4 - 1, (n % 4) // 2
                            if jp >= 0:
                                reduce(jj, jp, h)
                            elif not (isinstance(jj, int) and jj == 0):
                                reduce(jj - 1, 3, h)
                        if n + AHEAD < UNITS:
                            spread(jj, n + AHEAD)
                        elif not last:
                            spread(jj + 1, n + AHEAD - UNITS)

                step(0, False)
                with pe.Fori(1, STEPS - 1) as jj:
                    step(jj, False)
                step(STEPS - 1, True)
                for h in range(2):
                    reduce(STEPS - 1, 3, h)
                for h in range(2):
                    nc.tensor.matmul(y_bank[h][:, :], zero[:, 0:128], zero[:, :], start=False, stop=True,
                                     skip_group_check=True)

            @block.scalar
            def _(act):
                nc.scalar.activation(k.warm[:, :], k.m("ident")[0:1, 0:1], ACT.Exp)

                def columns(jj):
                    after(act, decay_ready, 2 * UNITS * jj, UNITS * jj, 1)
                    src = a_neg[:, :].rearrange("p (g j) -> p g j", g=4)[:, :, bass.ds(4 * jj, 4)]
                    nc.scalar.copy(a_now[:, :, :], src).then_inc(a_copied, 1)
                    act.wait_ge(a_copied, jj + 1)

                def decay(jj, n):
                    jp, g = n // 4, n % 4
                    u = UNITS * jj + n
                    after(act, state_ready, u - 3, u, 4)
                    for h in range(2):
                        act.wait_ge(dt_spread, 2 * u + h + 1)
                        nc.scalar.activation(da[n % 4][:, sl(h)], dt_bank[h][:, :], ACT.Exp,
                                             scale=a_now[:, g, jp:jp + 1]).then_inc(decay_ready, 1)

                columns(0)
                for n in range(UNITS):
                    decay(0, n)
                with act.Fori(1, STEPS) as jj:
                    columns(jj)
                    for n in range(UNITS):
                        decay(jj, n)

            @block.vector
            def _(dve):
                nc.vector.memset(zero[:, :], 0.0).then_inc(zeroed, 1)
                b_rows = bt[:, b * SEQ:(b + 1) * SEQ].rearrange("p (h t) -> p h t", h=2)

                def make_input(u, n):
                    dve.wait_ge(dtx_spread, 2 * u + 2)
                    nc.vector.tensor_tensor(inp[n % 2][:, :].rearrange("p (h t) -> p h t", h=2), b_rows,
                                            dtx_pair[n % 2][:, :, :], ALU.mult).then_inc(input_ready, 1)

                def scan(u, n):
                    dve.wait_ge(decay_ready, 2 * u + 2)
                    dve.wait_ge(input_ready, u + 1)
                    after(dve, hc_ready, u - 3, u, 4)
                    nc.vector.tensor_tensor_scan(st[n % 4][:, :], da[n % 4][:, :], inp[n % 2][:, :], 0.0, ALU.mult,
                                                 ALU.add).then_inc(state_ready, 1)

                def unit(jj, n, last):
                    u = UNITS * jj + n
                    if not last:
                        after(dve, state_ready, u, u, 1)
                        make_input(u + 1, n + 1)
                    scan(u, n)

                make_input(0, 0)
                for n in range(UNITS):
                    unit(0, n, False)
                with dve.Fori(1, STEPS - 1) as jj:
                    for n in range(UNITS):
                        unit(jj, n, False)
                for n in range(UNITS):
                    unit(STEPS - 1, n, n == UNITS - 1)

            @block.gpsimd
            def _(pool):
                def unit(jj, n):
                    u = UNITS * jj + n
                    jp = n // 4
                    if n % 4 == 0:
                        after(pool, summed, 4 * jj + jp - 1, u, 8)
                        one_at_j = onehot[:, bass.ds(4 * jj + jp, 1), :].rearrange("p a c -> p (a c)")
                        nc.gpsimd.tensor_copy(col[jp % 2][:, :], one_at_j).then_inc(col_ready, 1)
                    pool.wait_ge(state_ready, u + 1)
                    nc.gpsimd.tensor_tensor(hc[n % 8][:, :], st[n % 4][:, :], ct[:, b * SEQ:(b + 1) * SEQ], ALU.mult)\
                        .then_inc(hc_ready, 1)

                for n in range(UNITS):
                    unit(0, n)
                with pool.Fori(1, STEPS) as jj:
                    for n in range(UNITS):
                        unit(jj, n)
        with nc.Block() as block:
            @block.vector
            def _(dve):
                for h in range(2):
                    cols = slice(b * SEQ + h * BLK, b * SEQ + (h + 1) * BLK)
                    nc.vector.scalar_tensor_tensor(ssm_in[:, cols], k.hn[:, cols], k.c("Dp"), y_bank[h][:, :],
                                                   ALU.mult, ALU.add)


def merge_and_glu(k, attn_t, ssm_in):
    nc = k.nc
    with ExitStack() as ctx:
        x1 = k.sb("x1", [128, T], ctx=ctx)
        xf = k.sb("xf", [128, T], ctx=ctx)
        products(k, "merge", [
            ("dve", [(slice(0, 128), slice(0, BLK), k.m("Wo"), attn_t[:, sl(b)], True, False),
                     (slice(0, 128), slice(0, BLK), k.m("Wout"), ssm_in[:, sl(b)], False, True)],
             lambda p, b=b: nc.vector.scalar_tensor_tensor(x1[:, sl(b)], p, 0.5, k.hn[:, sl(b)], ALU.mult, ALU.add))
            for b in blocks(T)])
        normalise(k, "rms_f", x1, T, [(xf, k.c("norm_ffn_w"))], eps=1e-6)
        silu = [k.sb(f"silu{i}", [128, BLK], ctx=ctx) for i in range(2)]
        hid = [k.sb(f"glu_hid{i}", [128, BLK], ctx=ctx) for i in range(2)]
        up = k.sem("glu_up")
        gated = k.sem("glu_silu")
        hid_ready = k.sem("glu_hid_ready")
        down = k.sem("glu_down")
        added = k.sem("glu_added")
        res = k.sem("glu_res")
        NC = FF0 // 128
        N = NBLK * NC
        with nc.Block() as block:
            @block.tensor
            def _(pe):
                def lower(n):
                    b, c = n // NC, n % NC
                    pe.wait_ge(hid_ready, n + 1)
                    if c == 0 and b >= 2:
                        pe.wait_ge(added, b - 1)
                    nc.tensor.matmul(k.bank[4 + b % 2][:, :], k.m("W2", lo=c * 128, n=128), hid[n % 2][:, :],
                                     start=c == 0, stop=c == NC - 1).then_inc(down, 1)
                for n in range(N):
                    b, c = n // NC, n % NC
                    if n >= 2:
                        pe.wait_ge(hid_ready, n - 1)
                    nc.tensor.matmul(k.bank[n % 2][:, :], k.m("W1", lo=c * 128, n=128), xf[:, sl(b)], start=True,
                                     stop=True)
                    nc.tensor.matmul(k.bank[2 + n % 2][:, :], k.m("W1", lo=FF0 + c * 128, n=128), xf[:, sl(b)],
                                     start=True, stop=True).then_inc(up, 1)
                    if n >= 1:
                        lower(n - 1)
                lower(N - 1)

            @block.scalar
            def _(act):
                for n in range(N):
                    act.wait_ge(up, n + 1)
                    if n >= 2:
                        act.wait_ge(hid_ready, n - 1)
                    nc.scalar.activation(silu[n % 2][:, :], k.bank[n % 2][:, :], ACT.Silu).then_inc(gated, 1)

            @block.vector
            def _(dve):
                nc.vector.tensor_tensor(x1[:, :], x1[:, :], k.x[:, :], ALU.add).then_inc(res, 1)
                dve.wait_ge(res, 1)
                for n in range(N + 1):
                    if n < N:
                        dve.wait_ge(gated, n + 1)
                        if n >= 2:
                            dve.wait_ge(down, n - 1)
                        nc.vector.tensor_tensor(hid[n % 2][:, :], silu[n % 2][:, :], k.bank[2 + n % 2][:, :], ALU.mult)\
                            .then_inc(hid_ready, 1)
                    if n >= NC and n % NC == 0:
                        b = n // NC - 1
                        dve.wait_ge(down, n)
                        nc.vector.tensor_tensor(k.x[:, sl(b)], x1[:, sl(b)], k.bank[4 + b % 2][:, :], ALU.add)\
                            .then_inc(added, 1)


def one_hot_weights(k, tag, idx, wgt, ntile, wt, tmp):
    nc = k.nc
    own = k.sem(f"{tag}_own")
    with nc.Block() as block:
        @block.vector
        def _(dve):
            link = linker(dve, own)
            shape = [128, ntile, EXPERTS]
            iota = k.m("iota8").unsqueeze(1).to_broadcast(shape)
            for c in range(2):
                link(nc.vector.tensor_tensor(tmp[:, :, c, :], idx[:, :, c:c + 1].to_broadcast(shape), iota,
                                             ALU.is_equal))
                link(nc.vector.tensor_tensor(tmp[:, :, c, :], tmp[:, :, c, :],
                                             wgt[:, :, c:c + 1].to_broadcast(shape), ALU.mult))
            link(nc.vector.tensor_tensor(wt[:, :, :], tmp[:, :, 0, :], tmp[:, :, 1, :], ALU.add))


def spread_weights(k, tag, wt, ntile, dst):
    nc = k.nc
    PE_ROWS = 3 * EXPERTS
    with ExitStack() as ctx:
        wp = k.sb(f"{tag}_parts", [128, ntile, 3, EXPERTS], BF16, ctx)
        rest = k.sb(f"{tag}_rest", [128, ntile, EXPERTS], F32, ctx)
        rows = k.sb(f"{tag}_rows", [PE_ROWS, ntile * TILE], BF16, ctx)
        ident_b = k.sb(f"{tag}_ident", [128, 128], BF16, ctx)
        picked = k.sb(f"{tag}_picked", [PE_ROWS, EXPERTS], F32, ctx)
        sel = k.sb(f"{tag}_sel", [PE_ROWS, EXPERTS, 128], BF16, ctx)
        own = k.sem(f"{tag}_own")
        with nc.Block() as block:
            @block.scalar
            def _(act):
                nc.scalar.copy(ident_b[:, :], k.m("ident"))

            @block.vector
            def _(dve):
                link = linker(dve, own)
                link(nc.vector.tensor_copy(wp[:, :, 0, :], wt[:, :, :]))
                link(nc.vector.tensor_tensor(rest[:, :, :], wt[:, :, :], wp[:, :, 0, :], ALU.subtract))
                link(nc.vector.tensor_copy(wp[:, :, 1, :], rest[:, :, :]))
                link(nc.vector.tensor_tensor(wp[:, :, 2, :], rest[:, :, :], wp[:, :, 1, :], ALU.subtract))
                eye = k.m("ident", PE_ROWS, n=PE_ROWS).rearrange("r (p e) -> r e p", p=3)
                link(nc.vector.tensor_reduce(picked[:, :], eye, AX.X, ALU.add))
                nc.vector.tensor_copy(sel[:, :, :], picked[:, :].unsqueeze(2).to_broadcast([PE_ROWS, EXPERTS, 128]))
        per = BLK // TILE
        products(k, f"{tag}_turn", [
            ("act" if b % 2 else "dve",
             [(slice(0, PE_ROWS), sl(j, TILE), wp[:, b * per + j, :, :].rearrange("p a e -> p (a e)"), ident_b[:, :],
               True, True) for j in range(per)],
             (lambda p, b=b: nc.scalar.copy(rows[:, sl(b)], p[0:PE_ROWS, :])) if b % 2 else
             (lambda p, b=b: nc.vector.tensor_copy(rows[:, sl(b)], p[0:PE_ROWS, :])))
            for b in range(ntile // per)])
        steps = []
        for e in range(EXPERTS):
            for b in range(ntile // per):
                mms = one(sel[:, e, :], rows[:, sl(b)])
                if len(steps) % 2:
                    steps.append(("act", mms, lambda p, e=e, b=b: nc.scalar.copy(dst[:, e, sl(b)], p)))
                else:
                    steps.append(("dve", mms, lambda p, e=e, b=b: nc.vector.tensor_copy(dst[:, e, sl(b)], p)))
        products(k, tag, steps)


def experts_of_layer0(k, d):
    nc = k.nc
    NC = FF0 // 128
    with ExitStack() as ctx:
        w1 = k.sb("moe_w1", [128, EXPERTS, FF0], ctx=ctx)
        w2 = k.sb("moe_w2", [128, EXPERTS, NC, 128], ctx=ctx)
        h = k.sb("moe_h", [128, MOE_T], ctx=ctx)
        hs = k.sb("moe_hs", [128, MOE_T], ctx=ctx)
        nt = MOE_T // TILE
        idx_i = k.sb("moe_idx_i", [128, nt, 2], I32, ctx)
        idx = k.sb("moe_idx", [128, nt, 2], ctx=ctx)
        wgt = k.sb("moe_wgt", [128, nt, 2], ctx=ctx)
        tmp = k.sb("moe_tmp", [128, nt, 2, EXPERTS], ctx=ctx)
        wt = k.sb("moe_wt", [128, nt, EXPERTS], ctx=ctx)
        wbc = k.sb("moe_wbc", [128, EXPERTS, MOE_T], ctx=ctx)
        hid = [k.sb(f"moe_hid{i}", [128, MOE_T], ctx=ctx) for i in range(4)]
        part = k.sb("moe_part", [128, 2, MOE_T], ctx=ctx)
        arrived = k.sem("moe_arrived")
        small = k.sem("moe_small")
        with nc.Block() as block:
            @block.sync
            def _(sp):
                sp.dma_start(idx_i[:, :, :], d["moe_idx"]).then_inc(small, 16)
                sp.dma_start(wgt[:, :, :], d["moe_wgt"]).then_inc(small, 16)
                sp.dma_start(w1[:, :, :], d["moe_w1"]).then_inc(arrived, 16)
                sp.dma_start(w2[:, :, :, :], d["moe_w2"]).then_inc(arrived, 16)

            @block.vector
            def _(dve):
                dve.wait_ge(small, 32)
                nc.vector.tensor_copy(idx[:, :, :], idx_i[:, :, :])
        one_hot_weights(k, "moe_oh", idx, wgt, nt, wt, tmp)
        spread_weights(k, "moe_sw", wt, nt, wbc)
        normalise(k, "ln_moe", h, MOE_T, [(hs, None)], centre=k.x)
        up = k.sem("moe_up")
        act_done = k.sem("moe_act_done")
        down = k.sem("moe_down")
        expert_out = k.sem("moe_expert_out")
        taken = k.sem("moe_taken")
        summed = k.sem("moe_summed")
        N = EXPERTS * NC
        LAG = 2
        with nc.Block() as block:
            @block.tensor
            def _(pe):
                pe.wait_ge(arrived, 32)

                def lower(n):
                    e, c = n // NC, n % NC
                    pe.wait_ge(act_done, n + 1)
                    if c == 0 and e >= 2:
                        pe.wait_ge(taken, e - 1)
                    ins = nc.tensor.matmul(k.bank[4 + e % 2][:, :], w2[:, e, c, :], hid[n % 4][:, :], start=c == 0,
                                           stop=c == NC - 1).then_inc(down, 1)
                for n in range(N):
                    e, c = n // NC, n % NC
                    if n >= 4:
                        pe.wait_ge(act_done, n - 3)
                    nc.tensor.matmul(k.bank[n % 4][:, :], w1[:, e, sl(c, 128)], hs[:, :], start=True, stop=True)\
                        .then_inc(up, 1)
                    if n >= LAG:
                        lower(n - LAG)
                for n in range(N - LAG, N):
                    lower(n)

            @block.scalar
            def _(act):
                for n in range(N):
                    act.wait_ge(up, n + 1)
                    if n >= 4:
                        act.wait_ge(down, n - 3)
                    nc.scalar.activation(hid[n % 4][:, :], k.bank[n % 4][:, :], ACT.Gelu).then_inc(act_done, 1)

            @block.vector
            def _(dve):
                nc.vector.tensor_scalar_add(k.x[:, :], k.x[:, :], k.c("moe_bias")).then_inc(summed, 1)
                for e in range(EXPERTS):
                    dve.wait_ge(down, NC * (e + 1))
                    dve.wait_ge(summed, max(e - 1, 0) + 1)
                    nc.vector.tensor_tensor(part[:, e % 2, :], wbc[:, e, :], k.bank[4 + e % 2][:, :], ALU.mult)\
                        .then_inc(taken, 1)
                    dve.wait_ge(taken, e + 1)
                    dve.wait_ge(summed, e + 1)
                    nc.vector.tensor_tensor(k.x[:, 0:MOE_T], k.x[:, 0:MOE_T], part[:, e % 2, :], ALU.add)\
                        .then_inc(summed, 1)


def latent_attention(k, d):
    nc = k.nc
    with ExitStack() as ctx:
        v_aug = k.sb("v_aug1", [128, NT, HEADS, 32], ctx=ctx)
        attn_t = k.sb("attn_t1", [128, T], ctx=ctx)
        cleared = k.sem("v1_cleared")
        with nc.Block() as block:
            @block.gpsimd
            def _(pool):
                nc.gpsimd.memset(v_aug[:, :, :, :], 0.0).then_inc(cleared, 1)
                pool.wait_ge(cleared, 1)
                nc.gpsimd.memset(v_aug[:, :, :, HD:HD + 1], 1.0)
        with ExitStack() as pre:
            hc = k.sb("lat_hc", [128, T], ctx=pre)
            normalise(k, "ln_lat", hc, T, [(k.hn, None)], centre=k.x)
        with ExitStack() as pre:
            ckv = k.sb("ckv", [32, T], ctx=pre)
            zq = k.sb("zq", [32, T], ctx=pre)
            qf = k.sb("qf1", [128, T], ctx=pre)
            kf = k.sb("kf1", [128, T], ctx=pre)
            tmp = k.sb("ltmp", [128, T], ctx=pre)
            m1 = k.sb("m1", [128, 128], ctx=pre)
            keff = k.sb("keff", [32, 128], ctx=pre)
            veff = k.sb("veff", [32, 128], ctx=pre)
            parts = [k.sb(f"lparts{i}", [128, T], BF16, pre) for i in range(3)]
            rows32, cols128 = slice(0, 32), slice(0, 128)
            steps = [("dve", one(k.m("W_uqT", 32), k.m("W_dq", 32), cols=cols128),
                      lambda p: nc.vector.tensor_copy(m1[:, :], p[:, 0:128])),
                     ("dve", one(k.m("W_uv"), k.m("W_oT"), rows=rows32, cols=cols128),
                      lambda p: nc.vector.tensor_copy(veff[:, :], p[0:32, 0:128]))]
            for b in blocks(T):
                steps += [("act", one(k.m("W_dkvT"), k.hn[:, sl(b)], rows=rows32),
                           lambda p, b=b: nc.scalar.copy(ckv[:, sl(b)], p[0:32, :])),
                          ("dve", one(k.m("W_dqT"), k.hn[:, sl(b)], rows=rows32),
                           lambda p, b=b: nc.vector.tensor_copy(zq[:, sl(b)], p[0:32, :]))]
            products(k, "lat_p1", steps)
            products(k, "lat_p2", [("dve", one(k.m("W_uk"), m1[:, :], rows=rows32, cols=cols128),
                                    lambda p: nc.vector.tensor_copy(keff[:, :], p[0:32, 0:128]))])
            steps = []
            for b in blocks(T):
                steps += [("act", one(k.m("W_uqT", 32), zq[:, sl(b)]), lambda p, b=b: nc.scalar.copy(qf[:, sl(b)], p)),
                          ("dve", one(keff[:, :], ckv[:, sl(b)]),
                           lambda p, b=b: nc.vector.tensor_copy(kf[:, sl(b)], p)),
                          ("act", [(slice(0, 128), sl(j, TILE), ckv[:, sl(4 * b + j, TILE)], veff[:, :], True, True)
                                   for j in range(4)],
                           lambda p, b=b: nc.scalar.copy(v_aug[:, 4 * b:4 * b + 4, :, 0:HD].rearrange("p t h d -> p (t h) d"),
                                                         p.rearrange("p (a d) -> p a d", d=HD)))]
            products(k, "lat_p3", steps)
            split3(k, "split_q1", [(qf, parts, tmp, send_linear(k, d["q_lin"], parts))], T)
            split3(k, "split_k1", [(kf, parts, tmp, send_linear(k, d["k_lin"], parts))], T,
                   also=replicate_terms(d["q_lin"], d["q_full"], Q_ORDER))
        attention(k, "attn1", d["q_full"], d["k_full"], HEADS, v_aug, True, attn_t,
                  also=replicate_terms(d["k_lin"], d["k_full"], K_ORDER))
        with nc.Block() as block:
            @block.vector
            def _(dve):
                nc.vector.tensor_tensor(k.x[:, :], k.x[:, :], attn_t[:, :], ALU.add)


def experts_of_layer1(k, d, y):
    nc = k.nc
    FB = 256
    NB = T // FB
    S = EXPERTS + 1
    xi = k.hn
    with ExitStack() as ctx:
        w9 = k.sb("w9", [128, EXPERTS, T], ctx=ctx)
        shared_w = k.sb("shared_w", [128, 1], ctx=ctx)
        w2p = k.sb("ew2_pad", [128, EXPERTS, 3 * D], ctx=ctx)
        eb2h = k.sb("eb2_half", [128, 3 * S], ctx=ctx)
        hb2 = k.sb("hb2_half", [128, 1], ctx=ctx)
        arrived = k.sem("ew2_arrived")
        with nc.Block() as block:
            @block.sync
            def _(sp):
                sp.dma_start(w2p[:, :, :], d["ew2_pad"]).then_inc(arrived, 16)

            @block.vector
            def _(dve):
                o = CI["eb2_0_0"]
                nc.vector.tensor_scalar_mul(eb2h[:, 0:24], k.cols[:, o:o + 24], 0.5)
                o = CI["b_s2_0"]
                nc.vector.tensor_scalar_mul(eb2h[:, 24:27], k.cols[:, o:o + 3], 0.5)
                nc.vector.tensor_scalar_mul(hb2[:, :], k.c("b_h2"), 0.5)
        with ExitStack() as pre:
            hc = k.sb("ffn_hc", [128, T], ctx=pre)
            normalise(k, "ln_ffn", hc, T, [(xi, None)], centre=k.x)
        with ExitStack() as pre:
            route(k, pre, w9, shared_w)
        with ExitStack() as pre:
            refine(k, pre, xi, w9, shared_w, w2p, eb2h, hb2, arrived, FB, NB, S)
        with nc.Block() as block:
            done = k.sem("y_done")
            sent = k.sem("y_sent")

            @block.vector
            def _(dve):
                for b in blocks(T):
                    nc.vector.tensor_tensor(k.x[:, sl(b)], k.x[:, sl(b)], xi[:, sl(b)], ALU.add).then_inc(done, 1)

            @block.sync
            def _(sp):
                for b in blocks(T):
                    sp.wait_ge(done, b + 1)
                    sp.dma_start(y[:, sl(b)], k.x[:, sl(b)]).then_inc(sent, 16)
                sp.wait_ge(sent, 16 * NBLK)


def route(k, ctx, w9, shared_w):
    nc = k.nc
    g1 = k.sb("route_g1", [32, T], ctx=ctx)
    lg = k.sb("route_logits", [128, NT, EXPERTS], ctx=ctx)
    t8 = k.sb("route_t8", [128, NT, EXPERTS], ctx=ctx)
    best = k.sb("route_best", [128, NT, 2], ctx=ctx)
    idx = k.sb("route_idx", [128, NT, 2], ctx=ctx)
    prob = k.sb("route_prob", [128, NT, 2], ctx=ctx)
    tmp = k.sb("route_tmp", [128, NT, 2, EXPERTS], ctx=ctx)
    wt = k.sb("route_wt", [128, NT, EXPERTS], ctx=ctx)
    sw = k.sb("route_sw", [128, 2], ctx=ctx)
    own = k.sem("route_own")
    steps = [("act", one(k.m("w_r1"), k.hn[:, sl(b)], rows=slice(0, 32)),
              lambda p, b=b: nc.scalar.activation(g1[:, sl(b)], p[0:32, :], ACT.Gelu, bias=k.c("b_r1", 32)))
             for b in blocks(T)]
    products(k, "route_p1", steps)
    b_r2 = k.m("b_r2").unsqueeze(1).to_broadcast([128, NT, EXPERTS])
    products(k, "route_p2", [
        ("dve", [(slice(0, 128), sl(t, EXPERTS), g1[:, sl(t, TILE)], k.m("w_r2", 32), True, True) for t in range(NT)],
         lambda p: nc.vector.tensor_tensor(lg[:, :, :], b_r2,
                                           p[:, 0:NT * EXPERTS].rearrange("p (t e) -> p t e", e=EXPERTS), ALU.add))])
    exps = k.sem("route_exps")
    diff = k.sem("route_diff")
    with nc.Block() as block:
        @block.vector
        def _(dve):
            link = linker(dve, own)
            shape = [128, NT, EXPERTS]
            iota = k.m("iota8").unsqueeze(1).to_broadcast(shape)
            for c in range(2):
                link(nc.vector.tensor_reduce(best[:, :, c], lg[:, :, :], AX.X, ALU.max))
                link(nc.vector.tensor_tensor(t8[:, :, :], lg[:, :, :], best[:, :, c:c + 1].to_broadcast(shape),
                                             ALU.is_lt))
                link(nc.vector.scalar_tensor_tensor(t8[:, :, :], t8[:, :, :], 8.0, iota, ALU.mult, ALU.add))
                link(nc.vector.tensor_reduce(idx[:, :, c], t8[:, :, :], AX.X, ALU.min))
                if c == 0:
                    link(nc.vector.tensor_tensor(t8[:, :, :], idx[:, :, 0:1].to_broadcast(shape), iota, ALU.is_equal))
                    link(nc.vector.scalar_tensor_tensor(lg[:, :, :], t8[:, :, :], -BIG, lg[:, :, :], ALU.mult,
                                                        ALU.add))
            nc.vector.tensor_tensor(best[:, :, 1], best[:, :, 1], best[:, :, 0], ALU.subtract).then_inc(diff, 1)
            dve.wait_ge(exps, 2)
            link(nc.vector.tensor_scalar_add(prob[:, :, 1], best[:, :, 1], 1.0))
            link(nc.vector.reciprocal(prob[:, :, 0], prob[:, :, 1]))
            link(nc.vector.tensor_tensor(prob[:, :, 1], best[:, :, 1], prob[:, :, 0], ALU.mult))
            link(nc.vector.tensor_scalar(sw[:, 1:2], sw[:, 0:1], -1.0, 1.0, ALU.mult, ALU.add))
            link(nc.vector.tensor_scalar_mul(prob[:, :, :], prob[:, :, :], sw[:, 1:2]))

        @block.scalar
        def _(act):
            nc.scalar.activation(sw[:, 0:1], k.c("shared_weight"), ACT.Sigmoid).then_inc(exps, 1)
            act.wait_ge(diff, 1)
            nc.scalar.activation(best[:, :, 1], best[:, :, 1], ACT.Exp).then_inc(exps, 1)
    one_hot_weights(k, "route_oh", idx, prob, NT, wt, tmp)
    spread_weights(k, "route_sw", wt, NT, w9)
    with nc.Block() as block:
        @block.vector
        def _(dve):
            nc.vector.tensor_copy(shared_w[:, :], sw[:, 0:1])


def refine(k, ctx, xi, w9, shared_w, w2p, eb2h, hb2, arrived, FB, NB, S):
    nc = k.nc
    v = k.sb("vel", [128, T], ctx=ctx)
    hid = [k.sb(f"hid{i}", [128, 5, FB], ctx=ctx) for i in range(2)]
    beta = [k.sb(f"beta{i}", [128, S, FB], ctx=ctx) for i in range(2)]
    gate = [k.sb(f"gate{i}", [128, S, FB], ctx=ctx) for i in range(2)]
    alpha = [k.sb(f"alpha{i}", [128, S, FB], ctx=ctx) for i in range(2)]
    spare = k.retired(0, (S + 4) * FB).rearrange("p (s f) -> p s f", f=FB)
    raw = [k.sb("beta_raw0", [128, S, FB], ctx=ctx)[:, :, :], spare[:, 0:S, :]]
    sum_g, sum_b, halt, ref = [spare[:, S + n, :] for n in range(4)]
    err = [k.sb(f"err{i}", [128, FB], ctx=ctx) for i in range(2)]
    xn = [k.sb(f"x_next{i}", [128, FB], ctx=ctx) for i in range(2)]
    hh = k.sb("halt_hid", [32, FB], ctx=ctx)
    fh = k.sb("ref_hid", [128, 2, FB], ctx=ctx)

    hid_scored = k.sem("hid_scored")
    hid_ready = k.sem("hid_ready")
    gate_made = k.sem("gate_made")
    beta_made = k.sem("beta_made")
    alpha_made = k.sem("alpha_made")
    gate_ready = k.sem("gate_ready")
    alpha_ready = k.sem("alpha_ready")
    beta_raw = k.sem("beta_raw")
    clipped = k.sem("beta_clipped")
    exped = k.sem("beta_exped")
    logged = k.sem("beta_logged")
    beta_ready = k.sem("beta_ready")
    err_ready = k.sem("err_ready")
    weighted = k.sem("weighted")
    gate_plus = k.sem("gate_plus")
    gate_weighted = k.sem("gate_weighted")
    mixed = k.sem("mixed")
    xn_ready = k.sem("xn_ready")
    halt_scored = k.sem("halt_scored")
    halt_hid = k.sem("halt_hid_ready")
    halt_ready = k.sem("halt_ready")
    refined = k.sem("refined_ready")
    xi_ready = k.sem("xi_ready")
    own_dve = k.sem("refine_own_dve")

    half = "p (c f) -> p c f"
    pairs_bank = [k.bank[p].rearrange(half, f=FB) for p in range(2)]
    shared_bank = k.bank[2][:, 0:FB]
    halt_hid_bank = k.bank[7][0:32, FB:2 * FB]
    ring = [k.bank[3 + n].rearrange(half, f=FB) for n in range(3)]
    f1_bank = k.bank[6].rearrange(half, f=FB)
    halt_bank = k.bank[6][:, 0:FB]
    ref_bank = k.bank[7][:, 0:FB]
    PAIRS = (S + 1) // 2

    def slots(q):
        return [e for e in (2 * q, 2 * q + 1) if e < S]

    def weights(e, comp):
        if e == EXPERTS:
            return k.m("w_s2", EH, lo=comp * D, n=D)
        return w2p[:, e, comp * D:(comp + 1) * D]

    def bias(e, comp):
        return k.c(f"b_s2_{comp}") if e == EXPERTS else k.c(f"eb2_{e}_{comp}")

    def half_bias(e, comp):
        return eb2h[:, 3 * e + comp:3 * e + comp + 1]

    def entries(second):
        rest = [(comp, q) for q in range(PAIRS) for comp in ((2, 0) if second else (2,))]
        return [(1, q) for q in range(PAIRS)] + rest

    def before(unit):
        if unit is None:
            return None
        second, i, par, u = unit
        if par:
            return second, i, 0, u - 1
        if isinstance(i, int) and i <= 0:
            return (False, NB // 2 - 1, 1, u - 1) if second else None
        return second, i - 1, 1, u - 1

    def each(eng, step):
        for second in (False, True):
            peeled = 1 if second else 2
            for i in range(peeled):
                for par in range(2):
                    unit = (second, i, par, NB * second + 2 * i + par)
                    step(unit, before(unit), before(before(unit)))
            with eng.Fori(peeled, NB // 2) as i:
                for par in range(2):
                    unit = (second, i, par, 2 * i + par + NB * second)
                    step(unit, before(unit), before(before(unit)))
        last = (True, NB // 2 - 1, 1, 2 * NB - 1)
        step(None, last, before(last))
        step(None, None, last)

    def since(eng, sem, value, unit, n):
        u = unit[3]
        if not isinstance(u, int) or u >= n:
            eng.wait_ge(sem, value)

    def cols(i, par):
        if isinstance(i, int):
            return slice((2 * i + par) * FB, (2 * i + par + 1) * FB)
        return bass.ds((2 * i + par) * FB, FB)

    with nc.Block() as block:
        @block.tensor
        def _(pe):
            def hidden(unit):
                second, i, par, u = unit
                cc = cols(i, par)
                since(pe, hid_ready, 5 * u, unit, 1)
                if second:
                    pe.wait_ge(xi_ready, u - NB + 1)
                for p in range(5):
                    if p < 4:
                        out, lx, lv = pairs_bank[p // 2][:, p % 2, :], k.m("ew1", lo=p * 128, n=128), \
                            k.m("ew1", lo=512 + p * 128, n=128)
                    else:
                        out, lx, lv = shared_bank[0:EH, :], k.m("w_s1", lo=0, n=EH), k.m("w_s1", lo=EH, n=EH)
                    ins = nc.tensor.matmul(out, lx, xi[:, cc], start=True, stop=not second)
                    if second:
                        ins = nc.tensor.matmul(out, lv, v[:, cc], start=False, stop=True)
                    if p in (1, 3, 4):
                        ins.then_inc(hid_scored, 1)

            def outputs(unit, n):
                second, i, par, u = unit
                listed = entries(second)

                def read_up_to(comp, q, u):
                    done = min(2 * q + 2, S)
                    if comp == 1:
                        pe.wait_ge(beta_raw, S * u + done)
                    elif comp == 2:
                        pe.wait_ge(gate_ready, S * u + done)
                    else:
                        pe.wait_ge(alpha_ready, S * (u - NB) + done)

                comp, q = listed[n]
                if n < PAIRS:
                    pe.wait_ge(hid_ready, 5 * u + q + 1)
                if n >= 3:
                    read_up_to(*listed[n - 3], u)
                elif n == 0 and not (isinstance(u, int) and u == 0):
                    read_up_to(2, PAIRS - 1, u - 1)
                    if second and not (isinstance(u, int) and u == NB):
                        read_up_to(0, PAIRS - 1, u - 1)
                for e in slots(q):
                    h = hid[par][:, e // 2, :] if e < EXPERTS else hid[par][0:EH, 4, :]
                    last = nc.tensor.matmul(ring[n % 3][:, e % 2, :], weights(e, comp), h, start=True, stop=True)
                last.then_inc((alpha_made, beta_made, gate_made)[comp], 1)

            def halting_hidden(unit):
                _, _, par, u = unit
                pe.wait_ge(xn_ready, u + 1)
                since(pe, halt_ready, u, unit, 1)
                since(pe, xi_ready, u, unit, 1)
                nc.tensor.matmul(halt_hid_bank, k.m("w_h1"), xn[par][:, :], start=True, stop=True)
                for c in range(2):
                    last = nc.tensor.matmul(f1_bank[:, c, :], k.m("w_f1", lo=c * 128, n=128), xn[par][:, :],
                                            start=True, stop=True)
                last.then_inc(halt_scored, 1)

            def halting_outputs(unit):
                u = unit[3]
                pe.wait_ge(halt_hid, 3 * u + 3)
                nc.tensor.matmul(halt_bank, k.m("w_h2", 32).to_broadcast([32, 128]), hh[:, :], start=True, stop=True)
                for c in range(2):
                    last = nc.tensor.matmul(ref_bank, k.m("w_f2", lo=c * 128, n=128), fh[:, c, :], start=c == 0,
                                            stop=c == 1)
                last.then_inc(halt_scored, 1)

            def step(now, one_back, two_back):
                three_back = before(two_back)
                if now:
                    hidden(now)
                if one_back:
                    for n in range(PAIRS, PAIRS + 3):
                        outputs(one_back, n)
                if three_back:
                    halting_outputs(three_back)
                if one_back:
                    for n in range(PAIRS + 3, len(entries(one_back[0]))):
                        outputs(one_back, n)
                if now:
                    for n in range(PAIRS):
                        outputs(now, n)
                if two_back:
                    halting_hidden(two_back)

            pe.wait_ge(arrived, 16)
            each(pe, step)
            halting_outputs((True, NB // 2 - 1, 1, 2 * NB - 1))

        @block.scalar
        def _(act):
            def hidden(unit):
                second, _, par, u = unit
                since(act, gate_made, PAIRS * (u - 1), unit, 2)
                if second and not (isinstance(u, int) and u < NB + 2):
                    act.wait_ge(alpha_made, PAIRS * (u - NB - 1))
                for p in range(5):
                    act.wait_ge(hid_scored, 3 * u + p // 2 + 1)
                    if p < 4:
                        nc.scalar.activation(hid[par][:, p, :], pairs_bank[p // 2][:, p % 2, :], ACT.Gelu,
                                             bias=k.c(f"eb1_{p}")).then_inc(hid_ready, 1)
                    else:
                        nc.scalar.activation(hid[par][0:EH, 4, :], shared_bank[0:EH, :], ACT.Gelu,
                                             bias=k.c("b_s1", EH)).then_inc(hid_ready, 1)

            def halting_hidden(unit):
                u = unit[3]
                act.wait_ge(halt_scored, 2 * u + 1)
                nc.scalar.activation(hh[:, :], halt_hid_bank, ACT.Gelu, bias=k.c("b_h1", 32)).then_inc(halt_hid, 1)
                for c in range(2):
                    nc.scalar.activation(fh[:, c, :], f1_bank[:, c, :], ACT.Gelu, bias=k.c(f"b_f1_{c}"))\
                        .then_inc(halt_hid, 1)

            def log_exp(unit):
                _, _, par, u = unit
                act.wait_ge(clipped, u + 1)
                nc.scalar.activation(beta[par][:, :, :], beta[par][:, :, :], ACT.Exp).then_inc(exped, 1)
                act.wait_ge(exped, u + 1)
                nc.scalar.activation(beta[par][:, :, :], beta[par][:, :, :], ACT.Ln, bias=1.0).then_inc(logged, 1)

            def halting_gate(unit):
                u = unit[3]
                act.wait_ge(halt_scored, 2 * u + 2)
                since(act, xi_ready, u, unit, 1)
                nc.scalar.activation(halt[:, :], halt_bank, ACT.Tanh, bias=hb2[:, :], scale=0.5).then_inc(halt_ready, 1)

            def gates(unit, q):
                second, _, par, u = unit
                if q == 0:
                    since(act, xn_ready, u - 1, unit, 2)
                act.wait_ge(gate_made, PAIRS * u + q + 1)
                for e in slots(q):
                    nc.scalar.activation(gate[par][:, e, :], ring[entries(second).index((2, q)) % 3][:, e % 2, :],
                                         ACT.Tanh, bias=half_bias(e, 2), scale=0.5).then_inc(gate_ready, 1)
                if second:
                    act.wait_ge(alpha_made, PAIRS * (u - NB) + q + 1)
                    for e in slots(q):
                        nc.scalar.activation(alpha[par][:, e, :], ring[entries(second).index((0, q)) % 3][:, e % 2, :],
                                             ACT.Tanh, bias=half_bias(e, 0), scale=0.5).then_inc(alpha_ready, 1)

            def step(now, one_back, two_back):
                if now:
                    hidden(now)
                if one_back:
                    log_exp(one_back)
                if two_back:
                    halting_hidden(two_back)
                for q in range(PAIRS):
                    if now:
                        gates(now, q)
                    if q == 1 and two_back:
                        halting_gate(two_back)

            each(act, step)

        @block.gpsimd
        def _(pool):
            def weigh(z, cc, sem):
                nc.gpsimd.tensor_tensor(z[:, EXPERTS, :], z[:, EXPERTS, :], shared_w[:, :].to_broadcast([128, FB]),
                                        ALU.mult).then_inc(sem, 1)
                nc.gpsimd.tensor_tensor(z[:, 0:EXPERTS, :], z[:, 0:EXPERTS, :], w9[:, :, cc], ALU.mult).then_inc(sem, 1)

            def weigh_gates(unit):
                second, i, par, u = unit
                pool.wait_ge(gate_ready, S * (u + 1))
                if second:
                    nc.gpsimd.tensor_tensor(gate[par][:, :, :], gate[par][:, :, :],
                                            k.c("one").unsqueeze(2).to_broadcast([128, S, FB]), ALU.add)\
                        .then_inc(gate_plus, 1)
                    pool.wait_ge(gate_plus, u - NB + 1)
                weigh(gate[par], cols(i, par), gate_weighted)

            def weigh_betas(unit):
                second, i, par, u = unit
                if not second:
                    pool.wait_ge(mixed, u + 1)
                    weigh(beta[par], cols(i, par), weighted)

            def step(now, one_back, two_back):
                if one_back:
                    weigh_betas(one_back)
                if now:
                    weigh_gates(now)

            each(pool, step)

        @block.vector
        def _(dve):
            def read_betas(unit, q):
                second, i, par, u = unit
                if q == 0:
                    since(dve, xn_ready, u - 1, unit, 2)
                    since(dve, beta_ready, u - 1, unit, 2)
                    nc.vector.tensor_scalar_sub(err[par][:, :], xi[:, cols(i, par)], k.c("mu")).then_inc(err_ready, 1)
                dve.wait_ge(beta_made, PAIRS * u + q + 1)
                e = 2 * q
                if e < EXPERTS:
                    o = CI["eb2_0_0"]
                    biases = k.cols[:, o:o + 3 * EXPERTS].rearrange("p (e c) -> p e c", c=3)[:, e:e + 2, 1]
                    nc.vector.tensor_tensor(raw[par][:, e:e + 2, :], biases.unsqueeze(2).to_broadcast([128, 2, FB]),
                                            ring[q % 3][:, :, :], ALU.add).then_inc(beta_raw, 2)
                else:
                    nc.vector.tensor_scalar_add(raw[par][:, e, :], ring[q % 3][:, 0, :], k.c("b_s2_1"))\
                        .then_inc(beta_raw, 1)
                if q == PAIRS - 1:
                    dve.wait_ge(beta_raw, S * (u + 1))
                    nc.vector.tensor_scalar_min(beta[par][:, :, :], raw[par][:, :, :], 40.0).then_inc(clipped, 1)

            def larger(unit):
                _, _, par, u = unit
                dve.wait_ge(logged, u + 1)
                nc.vector.tensor_tensor(beta[par][:, :, :], beta[par][:, :, :], raw[par][:, :, :], ALU.max)\
                    .then_inc(beta_ready, 1)

            def halting(unit):
                _, i, par, u = unit
                cc = cols(i, par)
                dve.wait_ge(halt_scored, 2 * u + 2)
                nc.vector.tensor_scalar(ref[:, :], ref_bank, k.c("b_f2"), k.c("iw"), ALU.add, ALU.mult)\
                    .then_inc(refined, 1)
                dve.wait_ge(refined, 2 * u + 1)
                dve.wait_ge(halt_ready, u + 1)
                nc.vector.scalar_tensor_tensor(ref[:, :], halt[:, :], 1.0, ref[:, :], ALU.add, ALU.mult)\
                    .then_inc(refined, 1)
                dve.wait_ge(refined, 2 * u + 2)
                nc.vector.scalar_tensor_tensor(xi[:, cc], ref[:, :], 0.5, xi[:, cc], ALU.mult, ALU.add)\
                    .then_inc(xi_ready, 1)
                dve.wait_ge(xi_ready, u + 1)

            def alpha_sum(unit):
                second, i, par, u = unit
                if second:
                    base = own_base(second, u)
                    dve.wait_ge(gate_weighted, 2 * u + 2)
                    dve.wait_ge(alpha_ready, S * (u - NB + 1))
                    link(nc.vector.scalar_tensor_tensor(alpha[par][:, :, :], alpha[par][:, :, :], 1.0,
                                                        gate[par][:, :, :], ALU.add, ALU.mult), base + 1)
                    link(nc.vector.tensor_reduce(sum_b, alpha[par][:, :, :].rearrange("p e f -> p f e"), AX.X,
                                                 ALU.add), base + 2)

            def mix(unit):
                second, i, par, u = unit
                dve.wait_ge(gate_weighted, 2 * u + 2)
                dve.wait_ge(beta_ready, u + 1)
                nc.vector.tensor_tensor(gate[par][:, :, :], gate[par][:, :, :], beta[par][:, :, :], ALU.mult)\
                    .then_inc(mixed, 1)

            def add_up(unit):
                second, i, par, u = unit
                base = own_base(second, u)
                cc = cols(i, par)
                dve.wait_ge(mixed, u + 1)
                if second:
                    link(nc.vector.tensor_reduce(sum_g, gate[par][:, :, :].rearrange("p e f -> p f e"), AX.X, ALU.add),
                         base + 3)
                    link(nc.vector.tensor_tensor(sum_b, sum_b, v[:, cc], ALU.mult), base + 4)
                    link(nc.vector.tensor_tensor(sum_g, sum_g, err[par][:, :], ALU.mult), base + 5)
                    link(nc.vector.scalar_tensor_tensor(sum_g, sum_b, 0.5, sum_g, ALU.mult, ALU.subtract), base + 6)
                    nc.vector.scalar_tensor_tensor(xn[par][:, :], sum_g, 0.05, xi[:, cc], ALU.mult, ALU.add)\
                        .then_inc(xn_ready, 1)
                else:
                    link(nc.vector.tensor_reduce(sum_g, gate[par][:, :, :].rearrange("p e f -> p f e"), AX.X, ALU.add),
                         base + 1)

            def velocity(unit):
                second, i, par, u = unit
                if not second:
                    base = own_base(second, u)
                    cc = cols(i, par)
                    dve.wait_ge(weighted, 2 * u + 2)
                    link(nc.vector.tensor_reduce(sum_b, beta[par][:, :, :].rearrange("p e f -> p f e"), AX.X,
                                                 ALU.add), base + 2)
                    link(nc.vector.tensor_tensor(sum_g, sum_g, sum_b, ALU.add), base + 3)
                    link(nc.vector.tensor_tensor(sum_g, sum_g, err[par][:, :], ALU.mult), base + 4)
                    link(nc.vector.scalar_tensor_tensor(v[:, cc], sum_b, -1.0, err[par][:, :], ALU.mult, ALU.mult),
                         base + 5)
                    nc.vector.scalar_tensor_tensor(xn[par][:, :], sum_g, -0.05, xi[:, cc], ALU.mult, ALU.add)\
                        .then_inc(xn_ready, 1)
                dve.wait_ge(xn_ready, u + 1)

            def own_base(second, u):
                return 5 * u if not second else 5 * NB + 6 * (u - NB)

            def link(ins, value):
                ins.then_inc(own_dve, 1)
                dve.wait_ge(own_dve, value)

            def step(now, one_back, two_back):
                if now:
                    for q in range(PAIRS):
                        read_betas(now, q)
                if one_back:
                    larger(one_back)
                    alpha_sum(one_back)
                    mix(one_back)
                    add_up(one_back)
                if two_back:
                    halting(two_back)
                if one_back:
                    velocity(one_back)

            each(dve, step)


def build_program(nc, d, y, upto=4):
    with ExitStack() as ctx:
        k = Core(nc, ctx)
        scratch = {}
        for name, rows in (("q", HEADS), ("k", HEADS)):
            scratch[f"{name}_lin"] = nc.dram_tensor(f"{name}_lin", [3, rows * HD, T], BF16, kind="Internal").ap()
            scratch[f"{name}_full"] = nc.dram_tensor(f"{name}_full", [9 * HD, rows, T], BF16, kind="Internal").ap()
        d = {**d, **scratch}
        arrived = k.sem("inputs_arrived")
        weights_arrived = k.sem("weights_arrived")
        first = MOFF["mask_kq"]
        with nc.Block() as block:
            @block.sync
            def _(sp):
                sp.dma_start(k.x[:, :], d["x"]).then_inc(arrived, 16)
                sp.dma_start(k.mats[:, 0:first], d["mats"][:, 0:first]).then_inc(arrived, 16)
                sp.dma_start(k.mats[:, first:], d["mats"][:, first:]).then_inc(weights_arrived, 16)
                sp.dma_start(k.cols[:, :], d["cols"]).then_inc(weights_arrived, 16)
                sp.wait_ge(arrived, 32)
        with ExitStack() as layer:
            hc = k.sb("ln0_c", [128, T], ctx=layer)
            normalise(k, "ln0", hc, T, [(k.hn, None)], centre=k.x)
        with ExitStack() as layer:
            attn_t = k.sb("attn_t", [128, T], ctx=layer)
            ssm_in = k.sb("ssm_in", [128, T], ctx=layer)
            with k.scope():
                hybrid_attention(k, d, d["rope_q"], d["rope_k"], weights_arrived, attn_t)
            with k.scope():
                state_space(k, ssm_in)
            with k.scope():
                merge_and_glu(k, attn_t, ssm_in)
        if upto >= 2:
            with k.scope():
                experts_of_layer0(k, d)
        if upto >= 3:
            with k.scope():
                latent_attention(k, d)
        if upto >= 4:
            with k.scope():
                experts_of_layer1(k, d, y)
        else:
            with nc.Block() as block:
                @block.sync
                def _(sp):
                    sp.dma_start(y, k.x[:, :]).then_inc(arrived, 16)
                    sp.wait_ge(arrived, 48)


def constants():
    i = np.arange(128)
    m = {"ident": np.eye(128), "center": np.eye(128) - 1.0 / D,
         "mean8": (i[:, None] // HD == np.arange(16)[None]) / float(HD), "mean128": np.full((128, 1), 1.0 / D),
         "eye96": i[:, None] % 32 == np.arange(32)[None], "iota8": np.tile(np.arange(8.0), (128, 1)),
         "mask_kq": np.where(i[:, None] > i[None], -BIG, 0.0), "mask_qk": np.where(i[None] > i[:, None], -BIG, 0.0)}
    rot = np.zeros((128, 128))
    for r in range(128):
        if r % HD < HD // 2:
            rot[r + HD // 2, r] = -1.0
        else:
            rot[r - HD // 2, r] = 1.0
    m["rot"] = rot
    inv_freq = (np.float32(1.0) / np.float32(10000.0) ** (np.arange(0, HD, 2, dtype=np.float32) / np.float32(HD)))
    ang = np.arange(SEQ, dtype=np.float32)[None] * inv_freq.astype(np.float32)[i % 4][:, None]
    rope_q = np.stack([np.cos(ang), np.sin(ang)], 1).astype(np.float32)
    rope_k = np.stack([rope_q[32 * c:32 * c + 32, :, (c % 2) * BLK:(c % 2 + 1) * BLK] for c in range(4)], 0)
    return {n: v.astype(np.float32) for n, v in m.items()}, rope_q, rope_k.reshape(128, 2, BLK)


def lay_out(inp):
    a = {n: np.asarray(v) for n, v in inp.items()}
    h = {n[8:]: v for n, v in a.items() if n.startswith("L0_attn_")}
    e = {n[7:]: v for n, v in a.items() if n.startswith("L0_ffn_")}
    l = {n[8:]: v for n, v in a.items() if n.startswith("L1_attn_")}
    f = {n[7:]: v for n, v in a.items() if n.startswith("L1_ffn_")}
    m, rope_q, rope_k = constants()
    for n in ("Wq", "Wk", "Wv", "Wo", "Wx", "Wdt", "Wsel", "Wimp", "Wg", "Wout", "W1"):
        m[n] = h[n]
    m["W2"] = h["W2"].reshape(4, 128, 128).transpose(1, 0, 2).reshape(128, 512)
    m["A_log"] = h["A_log"].T
    m.update({"W_dqT": l["W_dq"].T, "W_dkvT": l["W_dkv"].T, "W_dq": l["W_dq"], "W_uqT": l["W_uq"].T,
              "W_uk": l["W_uk"], "W_uv": l["W_uv"], "W_oT": l["W_o"].T})
    m.update({"w_r1": f["w_r1"], "w_r2": f["w_r2"], "b_r2": np.tile(f["b_r2"], (128, 1)), "w_h1": f["w_h1"],
              "w_h2": f["w_h2"], "w_s1": np.concatenate([f["w_s1"][:D], f["w_s1"][D:]], 1), "w_s2": f["w_s2"],
              "w_f1": f["w_f1"], "w_f2": np.concatenate([f["w_f2"][:128], f["w_f2"][128:]], 1),
              "ew1": f["expert_w1"].reshape(EXPERTS, 2, D, EH).transpose(2, 1, 0, 3).reshape(D, 2 * EXPERTS * EH)})
    mats = np.zeros((128, MTOT), np.float32)
    for n, w in MATS.items():
        mats[:m[n].shape[0], MOFF[n]:MOFF[n] + w] = m[n]
    cols = np.zeros((128, len(COLS)), np.float32)

    def put(name, v):
        cols[:len(v), CI[name]] = v
    for n in ("norm_attn_w", "ssm_norm_w", "bdt", "Dp", "bsel", "sel_gate", "bimp", "bg", "norm_ffn_w"):
        put(n, h[n])
    put("qn", np.tile(h["qn_w"], 16))
    put("kn", np.tile(h["kn_w"], 16))
    put("moe_bias", e["bias"])
    put("b_r1", f["b_r1"])
    put("b_h1", f["b_h1"])
    put("b_f1_0", f["b_f1"][:128])
    put("b_f1_1", f["b_f1"][128:])
    put("b_f2", f["b_f2"])
    put("iw", f["integration_weight"])
    put("one", np.ones(128, np.float32))
    put("mu", f["mu"])
    put("b_h2", np.tile(f["b_h2"], 128))
    put("shared_weight", np.tile(f["shared_weight"].reshape(1), 128))
    put("b_s1", f["b_s1"])
    for c in range(3):
        put(f"b_s2_{c}", f["b_s2"][c * D:(c + 1) * D])
    for p in range(4):
        put(f"eb1_{p}", f["expert_b1"][2 * p:2 * p + 2].reshape(128))
    for x in range(EXPERTS):
        for c in range(3):
            put(f"eb2_{x}_{c}", f["expert_b2"][x, c * D:(c + 1) * D])
    ew2 = np.zeros((128, EXPERTS, 3 * D), np.float32)
    for x in range(EXPERTS):
        ew2[EH * (x % 2):EH * (x % 2) + EH, x] = f["expert_w2"][x]
    nt = MOE_T // TILE
    return {
        "x": h["x"].reshape(T, D).T, "mats": mats, "cols": cols, "rope_q": rope_q, "rope_k": rope_k,
        "moe_w1": e["w1"].transpose(1, 0, 2), "moe_w2": e["w2"].reshape(EXPERTS, FF0 // 128, 128, D).transpose(2, 0, 1, 3),
        "moe_idx": e["expert_indices"].astype(np.int32).reshape(nt, TILE, 2).transpose(1, 0, 2),
        "moe_wgt": e["expert_weights"].reshape(nt, TILE, 2).transpose(1, 0, 2), "ew2_pad": ew2}


def kernel(**inputs):
    import concourse.bacc as bacc
    from concourse.bass_utils import run_bass_kernel_spmd

    nc = bacc.Bacc("TRN2", target_bir_lowering=False, num_devices=1)
    arrays, d = {}, {}
    for name, value in lay_out(inputs).items():
        value = np.ascontiguousarray(value)
        arrays[f"in_{name}"] = value
        d[name] = nc.dram_tensor(f"in_{name}", value.shape, mybir.dt.from_np(value.dtype), kind="ExternalInput").ap()
    y = nc.dram_tensor("out_y", [D, T], F32, kind="ExternalOutput").ap()
    build_program(nc, d, y)
    r = run_bass_kernel_spmd(nc, [arrays], core_ids=[0])
    return r.results[0]["out_y"].T.reshape(BATCH, SEQ, D).copy()
```
